# Optimizing a Trainium2 kernel written in Bass

```python
import numpy as np
import jax
import jax.numpy as jnp

def _softmax(x, axis=-1):
    return jax.nn.softmax(x, axis=axis)

def _gelu(x):
    return jax.nn.gelu(x, approximate=True)

def _silu(x):
    return jax.nn.silu(x)

def _sigmoid(x):
    return jax.nn.sigmoid(x)

def _layernorm(x, axis=-1, eps=1e-05):
    m = jnp.mean(x, axis=axis, keepdims=True)
    v = jnp.var(x, axis=axis, keepdims=True)
    return (x - m) / jnp.sqrt(v + eps)

def _scatter_add(tgt, idx, src, axis=0):
    return tgt.at[idx].add(src)

def _segment_sum(src, seg, n):
    return jax.ops.segment_sum(src, seg, n)
kernel_name = 'mk_perceiver_d2_seqx_r4_a7901f'

def setup_inputs(seed: int=0):
    np.random.seed(seed)
    _w = jnp.asarray

    def _rec_inputs():
        import jax
        import jax.numpy as jnp
        _rk = jax.random.key(seed)
        x = -0.0003929 + 0.9999 * jax.random.normal(jax.random.fold_in(_rk, 1), (64, 32, 256), jnp.float32)
        _lenS = 32 - jax.random.randint(jax.random.fold_in(_rk, 7), (64,), 0, max(1, 32 // 4) + 1, jnp.int32)
        _lenS2 = 257 - jax.random.randint(jax.random.fold_in(_rk, 8), (64,), 0, max(1, 257 // 4) + 1, jnp.int32)
        _ctx_1024P = jax.random.normal(jax.random.fold_in(_rk, 11), (64, 16, 256), jnp.float32)
        _ctx_1024c = jax.random.dirichlet(jax.random.fold_in(_rk, 511), 0.3 * jnp.ones((16,), jnp.float32), (64, 257))
        _ctx_1024t = jnp.einsum('bsk,bkd->bsd', _ctx_1024c, _ctx_1024P)
        _ctx_1024t = _ctx_1024t * jax.lax.rsqrt(jnp.mean(jnp.square(_ctx_1024t)) + 1e-12) * 0.953939
        ctx_1024 = 2.81802e-05 + 1.00001 * (_ctx_1024t + 0.3 * jax.random.normal(jax.random.fold_in(_rk, 611), (64, 257, 256), jnp.float32))
        _validS = jnp.arange(32)[None, :] < _lenS[:, None]
        _validS2 = jnp.arange(257)[None, :] < _lenS2[:, None]
        _causal = jnp.tril(jnp.ones((32, 32), dtype=bool))
        mask_Bx1xS2_ik1 = jnp.where(jnp.broadcast_to(_validS2[:, None, :], (64, 1, 257)), 1, 0).astype(jnp.int32)
        return (x, ctx_1024, mask_Bx1xS2_ik1)
    x, ctx_1024, mask_Bx1xS2_ik1 = _rec_inputs()

    def _L0_xattn_setup():
        import jax, jax.numpy as jnp
        import numpy as np
        B, NQ, NK = (8, 512, 512)
        DQ = DK = DV = 256
        EPS = 1e-05

        def _xavier(key, shape):
            fan_in, fan_out = (shape[0], shape[1])
            lim = float(np.sqrt(6.0 / (fan_in + fan_out)))
            return jax.random.uniform(key, shape, jnp.float32, -lim, lim)

        def _layernorm(x, g, b):
            mu = jnp.mean(x, axis=-1, keepdims=True)
            var = jnp.mean(jnp.square(x - mu), axis=-1, keepdims=True)
            return (x - mu) * jax.lax.rsqrt(var + EPS) * g + b
        key = jax.random.key(seed)
        ks = jax.random.split(key, 12)
        return {'Q': jax.random.normal(ks[0], (B, NQ, DQ), jnp.float32), 'K': jax.random.normal(ks[1], (B, NK, DK), jnp.float32), 'V': jax.random.normal(ks[2], (B, NK, DK), jnp.float32), 'pad_mask': jax.random.randint(ks[3], (B, 1, NK), 0, 2, jnp.int32), 'Wq': _xavier(ks[4], (DQ, DV)), 'bq': jnp.zeros((DV,), jnp.float32), 'Wk': _xavier(ks[5], (DK, DV)), 'bk': jnp.zeros((DV,), jnp.float32), 'Wv': _xavier(ks[6], (DK, DV)), 'bv': jnp.zeros((DV,), jnp.float32), 'Wo': _xavier(ks[7], (DV, DV)), 'bo': jnp.zeros((DV,), jnp.float32), 'g0': jnp.ones((DV,), jnp.float32), 'beta0': jnp.zeros((DV,), jnp.float32)}
    _L0_xattn_all = _L0_xattn_setup()
    _L0_xattn_in = {k: v for k, v in _L0_xattn_all.items() if k in ('Wq', 'bq', 'Wk', 'bk', 'Wv', 'bv', 'Wo', 'bo', 'g0', 'beta0')}
    del _L0_xattn_all

    def _L0_attn_setup():
        import jax, jax.numpy as jnp
        import numpy as np
        B, L, D = (4, 512, 256)
        H, DK, DV = (4, 64, 64)
        CHUNK = 32
        MIN_FLOOR, MAX_FLOOR = (0.01, 0.1)
        EPS = 1e-05

        def _l2norm(x):
            return x * jax.lax.rsqrt(jnp.sum(x * x, -1, keepdims=True) + 1e-06)

        def _causal_dwconv(x, w):
            b, l, c = x.shape
            k = w.shape[-1]
            xt = jnp.transpose(x, (0, 2, 1))
            y = jax.lax.conv_general_dilated(xt, w[:, None, :], (1,), [(k - 1, 0)], dimension_numbers=('NCH', 'OIH', 'NCH'), feature_group_count=c)
            return jnp.transpose(y, (0, 2, 1))

        def _delta_rule_chunkwise(q, k, v, beta, chunk=CHUNK):
            b, h, l, dk = q.shape
            dv = v.shape[-1]
            q = _l2norm(q)
            k = _l2norm(k)
            v = v * beta[..., None]
            kb = k * beta[..., None]
            n = l // chunk
            resh = lambda t: t.reshape(b, h, n, chunk, t.shape[-1])
            q, k, v, kb = (resh(q), resh(k), resh(v), resh(kb))
            tri = jnp.triu(jnp.ones((chunk, chunk), bool))
            strict = jnp.triu(jnp.ones((chunk, chunk), bool), 1)
            att = jnp.where(tri, 0.0, -(kb @ jnp.swapaxes(k, -1, -2)))
            for i in range(1, chunk):
                upd = jnp.einsum('bhnj,bhnjk->bhnk', att[..., i, :], att)
                att = att.at[..., i, :i].add(upd[..., :i])
            att = att + jnp.eye(chunk, dtype=att.dtype)
            u = att @ v
            w = att @ kb

            def step(S, xs):
                q_i, k_i, u_i, w_i = xs
                local = jnp.where(strict, 0.0, q_i @ jnp.swapaxes(k_i, -1, -2))
                u_adj = u_i - w_i @ S
                o_i = q_i @ S + local @ u_adj
                return (S + jnp.swapaxes(k_i, -1, -2) @ u_adj, o_i)
            xs = tuple((jnp.moveaxis(t, 2, 0) for t in (q, k, u, w)))
            S0 = jnp.zeros((b, h, dk, dv), q.dtype)
            S, o = jax.lax.scan(step, S0, xs)
            return (jnp.moveaxis(o, 0, 2).reshape(b, h, l, dv), S)

        def _rmsnorm(x, w):
            return x * jax.lax.rsqrt(jnp.mean(x * x, -1, keepdims=True) + EPS) * w
        key = jax.random.key(seed)
        ks = jax.random.split(key, 16)
        s = 0.02
        return {'hidden_states': jax.random.normal(ks[0], (B, L, D), jnp.float32), 'W_q': jax.random.normal(ks[1], (D, H * DK), jnp.float32) * s, 'W_k': jax.random.normal(ks[2], (D, H * DK), jnp.float32) * s, 'W_v': jax.random.normal(ks[3], (D, H * DV), jnp.float32) * s, 'W_b': jax.random.normal(ks[4], (D, H), jnp.float32) * s, 'conv_w_q': jax.random.normal(ks[5], (H * DK, 4), jnp.float32) * 0.3, 'conv_w_k': jax.random.normal(ks[6], (H * DK, 4), jnp.float32) * 0.3, 'conv_w_v': jax.random.normal(ks[7], (H * DV, 4), jnp.float32) * 0.3, 'fir_short_w': jax.random.normal(ks[8], (H, DV, 3), jnp.float32) * 0.1, 'fir_long_w': jax.random.normal(ks[9], (H, DV, 31), jnp.float32) * 0.1, 'W_fuse1': jax.random.normal(ks[10], (D + 3 * H * DV, 2 * D), jnp.float32) * s, 'b_fuse1': jnp.zeros((2 * D,), jnp.float32), 'W_fuse2': jax.random.normal(ks[11], (2 * D, H * 4), jnp.float32) * s, 'b_fuse2': jnp.zeros((H * 4,), jnp.float32).at[3::4].set(4.0), 'others_log_tau': jnp.zeros((H,), jnp.float32), 'norm_w': jnp.ones((DV,), jnp.float32), 'W_o': jax.random.normal(ks[12], (H * DV, D), jnp.float32) * s}
    _L0_attn_all = _L0_attn_setup()
    _L0_attn_in = {k: v for k, v in _L0_attn_all.items() if k in ('W_q', 'W_k', 'W_v', 'W_b', 'conv_w_q', 'conv_w_k', 'conv_w_v', 'fir_short_w', 'fir_long_w', 'W_fuse1', 'b_fuse1', 'W_fuse2', 'b_fuse2', 'others_log_tau', 'norm_w', 'W_o')}
    del _L0_attn_all

    def _L0_ffn_setup():
        import jax, jax.numpy as jnp
        import numpy as np
        B, T, D = (2, 512, 256)
        E, DFF, TOPK = (8, 1024, 2)
        TEMPERATURE = 1.0
        key = jax.random.key(seed)
        k_x, k_w1, k_w2, k_r = jax.random.split(key, 4)
        x = jax.random.normal(k_x, (B, T, D), dtype=jnp.float32)
        W1 = jax.random.normal(k_w1, (E, DFF, D), dtype=jnp.float32) * 0.02
        W2 = jax.random.normal(k_w2, (E, D, DFF), dtype=jnp.float32) * 0.02
        Wr = jax.random.normal(k_r, (E, D), dtype=jnp.float32) * 0.02
        return {'x': x, 'W1': W1, 'W2': W2, 'Wr': Wr}
    _L0_ffn_all = _L0_ffn_setup()
    _L0_ffn_in = {k: v for k, v in _L0_ffn_all.items() if k in ('W1', 'W2', 'Wr')}
    del _L0_ffn_all

    def _L1_xattn_setup():
        import jax, jax.numpy as jnp
        import numpy as np
        D_MODEL = 256
        NUM_HEADS = 16
        D_K = D_MODEL // NUM_HEADS

        def _split_heads(x):
            B, S, _ = x.shape
            return x.reshape(B, S, NUM_HEADS, D_K).transpose(0, 2, 1, 3)
        key = jax.random.key(seed)
        ks = jax.random.split(key, 11)
        B, S = (2, 512)
        s = 1.0 / np.sqrt(D_MODEL)
        return {'Q': jax.random.normal(ks[0], (B, S, D_MODEL), jnp.float32), 'K': jax.random.normal(ks[1], (B, S, D_MODEL), jnp.float32), 'V': jax.random.normal(ks[2], (B, S, D_MODEL), jnp.float32), 'Wq': jax.random.normal(ks[3], (D_MODEL, D_MODEL), jnp.float32) * s, 'bq': jax.random.normal(ks[4], (D_MODEL,), jnp.float32) * s, 'Wk': jax.random.normal(ks[5], (D_MODEL, D_MODEL), jnp.float32) * s, 'bk': jax.random.normal(ks[6], (D_MODEL,), jnp.float32) * s, 'Wv': jax.random.normal(ks[7], (D_MODEL, D_MODEL), jnp.float32) * s, 'bv': jax.random.normal(ks[8], (D_MODEL,), jnp.float32) * s, 'Wo': jax.random.normal(ks[9], (D_MODEL, D_MODEL), jnp.float32) * s, 'bo': jax.random.normal(ks[10], (D_MODEL,), jnp.float32) * s}
    _L1_xattn_all = _L1_xattn_setup()
    _L1_xattn_in = {k: v for k, v in _L1_xattn_all.items() if k in ('Wq', 'bq', 'Wk', 'bk', 'Wv', 'bv', 'Wo', 'bo')}
    del _L1_xattn_all

    def _L1_attn_setup():
        import jax, jax.numpy as jnp
        import numpy as np
        B, L, HID = (8, 1025, 256)
        H, KV, DH = (16, 4, 64)
        EPS = 1e-06
        ROPE_BASE = 10000.0

        def _rms_norm(x, w):
            var = jnp.mean(jnp.square(x), axis=-1, keepdims=True)
            return x * jax.lax.rsqrt(var + EPS) * w

        def _rotate_half(x):
            x1, x2 = jnp.split(x, 2, axis=-1)
            return jnp.concatenate([-x2, x1], axis=-1)

        def _rope_cache(seq_len, dim):
            inv_freq = 1.0 / ROPE_BASE ** (jnp.arange(0, dim, 2, dtype=jnp.float32) / dim)
            pos = jnp.arange(seq_len, dtype=jnp.float32)
            freqs = pos[:, None] * inv_freq[None, :]
            emb = jnp.concatenate([freqs, freqs], axis=-1)
            return (jnp.cos(emb), jnp.sin(emb))
        key = jax.random.key(seed)
        ks = jax.random.split(key, 5)
        s_in = 1.0
        s_q = float(np.sqrt(2.0 / (HID + H * DH)))
        s_kv = float(np.sqrt(2.0 / (HID + KV * DH)))
        s_o = float(np.sqrt(2.0 / (H * DH + HID)) / np.sqrt(2.0))
        return {'inputs': jax.random.normal(ks[0], (B, L, HID), jnp.float32) * s_in, 'Wq': jax.random.normal(ks[1], (H * DH, HID), jnp.float32) * s_q, 'Wk': jax.random.normal(ks[2], (KV * DH, HID), jnp.float32) * s_kv, 'Wv': jax.random.normal(ks[3], (KV * DH, HID), jnp.float32) * s_kv, 'Wo': jax.random.normal(ks[4], (HID, H * DH), jnp.float32) * s_o, 'q_norm_w': jnp.ones((DH,), jnp.float32), 'k_norm_w': jnp.ones((DH,), jnp.float32)}
    _L1_attn_all = _L1_attn_setup()
    _L1_attn_in = {k: v for k, v in _L1_attn_all.items() if k in ('Wq', 'Wk', 'Wv', 'Wo', 'q_norm_w', 'k_norm_w')}
    del _L1_attn_all

    def _L1_ffn_setup():
        import jax, jax.numpy as jnp
        import numpy as np
        DIM = 256
        N_EXPERTS = 16
        TOP_K = 4
        N_GROUP = 4
        TOPK_GROUP = 2
        MOE_INTER = 128
        SHARED_INTER = 512
        ROUTED_SCALE = 2.5

        def relu2(x):
            return jnp.square(jax.nn.relu(x))

        def _router(x2, gate_w, bias_e):
            T = x2.shape[0]
            logits = x2 @ gate_w.T
            scores = jax.nn.sigmoid(logits)
            sc = jax.lax.stop_gradient(scores + bias_e[None, :])
            grp = sc.reshape(T, N_GROUP, N_EXPERTS // N_GROUP)
            top2, _ = jax.lax.top_k(grp, 2)
            group_scores = top2.sum(-1)
            _, gidx = jax.lax.top_k(group_scores, TOPK_GROUP)
            rows = jnp.arange(T)[:, None]
            gmask = jnp.zeros((T, N_GROUP), dtype=sc.dtype).at[rows, gidx].set(1.0)
            smask = jnp.repeat(gmask, N_EXPERTS // N_GROUP, axis=1)
            masked = jnp.where(smask > 0, sc, 0.0)
            _, topk_idx = jax.lax.top_k(masked, TOP_K)
            topk_w = jnp.take_along_axis(scores, topk_idx, axis=1)
            topk_w = topk_w / (topk_w.sum(-1, keepdims=True) + 1e-20)
            topk_w = topk_w * ROUTED_SCALE
            return (topk_idx, topk_w)
        key = jax.random.key(seed)
        ks = jax.random.split(key, 6)
        hidden_states = jax.random.normal(ks[0], (2, 512, DIM), dtype=jnp.float32)
        gate_w = jax.random.normal(ks[1], (N_EXPERTS, DIM), dtype=jnp.float32) * 0.02
        bias_e = jnp.zeros((N_EXPERTS,), dtype=jnp.float32)
        up_w = jax.random.normal(ks[2], (N_EXPERTS, MOE_INTER, DIM), dtype=jnp.float32) * 0.02
        down_w = jax.random.normal(ks[3], (N_EXPERTS, DIM, MOE_INTER), dtype=jnp.float32) * 0.02
        shared_up = jax.random.normal(ks[4], (SHARED_INTER, DIM), dtype=jnp.float32) * 0.02
        shared_down = jax.random.normal(ks[5], (DIM, SHARED_INTER), dtype=jnp.float32) * 0.02
        return {'hidden_states': hidden_states, 'gate_w': gate_w, 'bias_e': bias_e, 'up_w': up_w, 'down_w': down_w, 'shared_up': shared_up, 'shared_down': shared_down}
    _L1_ffn_all = _L1_ffn_setup()
    _L1_ffn_in = {k: v for k, v in _L1_ffn_all.items() if k in ('gate_w', 'bias_e', 'up_w', 'down_w', 'shared_up', 'shared_down')}
    del _L1_ffn_all
    return {'x': x, 'ctx_1024': ctx_1024, 'mask_Bx1xS2_ik1': mask_Bx1xS2_ik1, 'L0_xattn_Wq': _L0_xattn_in['Wq'], 'L0_xattn_bq': _L0_xattn_in['bq'], 'L0_xattn_Wk': _L0_xattn_in['Wk'], 'L0_xattn_bk': _L0_xattn_in['bk'], 'L0_xattn_Wv': _L0_xattn_in['Wv'], 'L0_xattn_bv': _L0_xattn_in['bv'], 'L0_xattn_Wo': _L0_xattn_in['Wo'], 'L0_xattn_bo': _L0_xattn_in['bo'], 'L0_xattn_g0': _L0_xattn_in['g0'], 'L0_xattn_beta0': _L0_xattn_in['beta0'], 'L0_attn_W_q': _L0_attn_in['W_q'], 'L0_attn_W_k': _L0_attn_in['W_k'], 'L0_attn_W_v': _L0_attn_in['W_v'], 'L0_attn_W_b': _L0_attn_in['W_b'], 'L0_attn_conv_w_q': _L0_attn_in['conv_w_q'], 'L0_attn_conv_w_k': _L0_attn_in['conv_w_k'], 'L0_attn_conv_w_v': _L0_attn_in['conv_w_v'], 'L0_attn_fir_short_w': _L0_attn_in['fir_short_w'], 'L0_attn_fir_long_w': _L0_attn_in['fir_long_w'], 'L0_attn_W_fuse1': _L0_attn_in['W_fuse1'], 'L0_attn_b_fuse1': _L0_attn_in['b_fuse1'], 'L0_attn_W_fuse2': _L0_attn_in['W_fuse2'], 'L0_attn_b_fuse2': _L0_attn_in['b_fuse2'], 'L0_attn_others_log_tau': _L0_attn_in['others_log_tau'], 'L0_attn_norm_w': _L0_attn_in['norm_w'], 'L0_attn_W_o': _L0_attn_in['W_o'], 'L0_ffn_W1': _L0_ffn_in['W1'], 'L0_ffn_W2': _L0_ffn_in['W2'], 'L0_ffn_Wr': _L0_ffn_in['Wr'], 'L1_xattn_Wq': _L1_xattn_in['Wq'], 'L1_xattn_bq': _L1_xattn_in['bq'], 'L1_xattn_Wk': _L1_xattn_in['Wk'], 'L1_xattn_bk': _L1_xattn_in['bk'], 'L1_xattn_Wv': _L1_xattn_in['Wv'], 'L1_xattn_bv': _L1_xattn_in['bv'], 'L1_xattn_Wo': _L1_xattn_in['Wo'], 'L1_xattn_bo': _L1_xattn_in['bo'], 'L1_attn_Wq': _L1_attn_in['Wq'], 'L1_attn_Wk': _L1_attn_in['Wk'], 'L1_attn_Wv': _L1_attn_in['Wv'], 'L1_attn_Wo': _L1_attn_in['Wo'], 'L1_attn_q_norm_w': _L1_attn_in['q_norm_w'], 'L1_attn_k_norm_w': _L1_attn_in['k_norm_w'], 'L1_ffn_gate_w': _L1_ffn_in['gate_w'], 'L1_ffn_bias_e': _L1_ffn_in['bias_e'], 'L1_ffn_up_w': _L1_ffn_in['up_w'], 'L1_ffn_down_w': _L1_ffn_in['down_w'], 'L1_ffn_shared_up': _L1_ffn_in['shared_up'], 'L1_ffn_shared_down': _L1_ffn_in['shared_down']}

def reference(x, ctx_1024, mask_Bx1xS2_ik1, L0_xattn_Wq, L0_xattn_bq, L0_xattn_Wk, L0_xattn_bk, L0_xattn_Wv, L0_xattn_bv, L0_xattn_Wo, L0_xattn_bo, L0_xattn_g0, L0_xattn_beta0, L0_attn_W_q, L0_attn_W_k, L0_attn_W_v, L0_attn_W_b, L0_attn_conv_w_q, L0_attn_conv_w_k, L0_attn_conv_w_v, L0_attn_fir_short_w, L0_attn_fir_long_w, L0_attn_W_fuse1, L0_attn_b_fuse1, L0_attn_W_fuse2, L0_attn_b_fuse2, L0_attn_others_log_tau, L0_attn_norm_w, L0_attn_W_o, L0_ffn_W1, L0_ffn_W2, L0_ffn_Wr, L1_xattn_Wq, L1_xattn_bq, L1_xattn_Wk, L1_xattn_bk, L1_xattn_Wv, L1_xattn_bv, L1_xattn_Wo, L1_xattn_bo, L1_attn_Wq, L1_attn_Wk, L1_attn_Wv, L1_attn_Wo, L1_attn_q_norm_w, L1_attn_k_norm_w, L1_ffn_gate_w, L1_ffn_bias_e, L1_ffn_up_w, L1_ffn_down_w, L1_ffn_shared_up, L1_ffn_shared_down):
    import jax
    import jax.numpy as jnp

    def _L0_xattn_ref(Q, K, V, pad_mask, Wq, bq, Wk, bk, Wv, bv, Wo, bo, g0, beta0):
        import jax, jax.numpy as jnp
        import numpy as np
        B, NQ, NK = (8, 512, 512)
        DQ = DK = DV = 256
        EPS = 1e-05

        def _xavier(key, shape):
            fan_in, fan_out = (shape[0], shape[1])
            lim = float(np.sqrt(6.0 / (fan_in + fan_out)))
            return jax.random.uniform(key, shape, jnp.float32, -lim, lim)

        def _layernorm(x, g, b):
            mu = jnp.mean(x, axis=-1, keepdims=True)
            var = jnp.mean(jnp.square(x - mu), axis=-1, keepdims=True)
            return (x - mu) * jax.lax.rsqrt(var + EPS) * g + b
        q = Q @ Wq + bq
        k = K @ Wk + bk
        v = V @ Wv + bv
        scale = 1.0 / jnp.sqrt(jnp.float32(DV))
        scores = jnp.einsum('bqd,bkd->bqk', q, k) * scale
        scores = jnp.where(pad_mask == 0, jnp.float32(-1000000000.0), scores)
        w = jax.nn.softmax(scores, axis=-1)
        out = jnp.einsum('bqk,bkd->bqd', w, v)
        out = out @ Wo + bo
        out = _layernorm(out, g0, beta0)
        return out

    def _L0_attn_ref(hidden_states, W_q, W_k, W_v, W_b, conv_w_q, conv_w_k, conv_w_v, fir_short_w, fir_long_w, W_fuse1, b_fuse1, W_fuse2, b_fuse2, others_log_tau, norm_w, W_o):
        import jax, jax.numpy as jnp
        import numpy as np
        B, L, D = (4, 512, 256)
        H, DK, DV = (4, 64, 64)
        CHUNK = 32
        MIN_FLOOR, MAX_FLOOR = (0.01, 0.1)
        EPS = 1e-05

        def _l2norm(x):
            return x * jax.lax.rsqrt(jnp.sum(x * x, -1, keepdims=True) + 1e-06)

        def _causal_dwconv(x, w):
            b, l, c = x.shape
            k = w.shape[-1]
            xt = jnp.transpose(x, (0, 2, 1))
            y = jax.lax.conv_general_dilated(xt, w[:, None, :], (1,), [(k - 1, 0)], dimension_numbers=('NCH', 'OIH', 'NCH'), feature_group_count=c)
            return jnp.transpose(y, (0, 2, 1))

        def _delta_rule_chunkwise(q, k, v, beta, chunk=CHUNK):
            b, h, l, dk = q.shape
            dv = v.shape[-1]
            q = _l2norm(q)
            k = _l2norm(k)
            v = v * beta[..., None]
            kb = k * beta[..., None]
            n = l // chunk
            resh = lambda t: t.reshape(b, h, n, chunk, t.shape[-1])
            q, k, v, kb = (resh(q), resh(k), resh(v), resh(kb))
            tri = jnp.triu(jnp.ones((chunk, chunk), bool))
            strict = jnp.triu(jnp.ones((chunk, chunk), bool), 1)
            att = jnp.where(tri, 0.0, -(kb @ jnp.swapaxes(k, -1, -2)))
            for i in range(1, chunk):
                upd = jnp.einsum('bhnj,bhnjk->bhnk', att[..., i, :], att)
                att = att.at[..., i, :i].add(upd[..., :i])
            att = att + jnp.eye(chunk, dtype=att.dtype)
            u = att @ v
            w = att @ kb

            def step(S, xs):
                q_i, k_i, u_i, w_i = xs
                local = jnp.where(strict, 0.0, q_i @ jnp.swapaxes(k_i, -1, -2))
                u_adj = u_i - w_i @ S
                o_i = q_i @ S + local @ u_adj
                return (S + jnp.swapaxes(k_i, -1, -2) @ u_adj, o_i)
            xs = tuple((jnp.moveaxis(t, 2, 0) for t in (q, k, u, w)))
            S0 = jnp.zeros((b, h, dk, dv), q.dtype)
            S, o = jax.lax.scan(step, S0, xs)
            return (jnp.moveaxis(o, 0, 2).reshape(b, h, l, dv), S)

        def _rmsnorm(x, w):
            return x * jax.lax.rsqrt(jnp.mean(x * x, -1, keepdims=True) + EPS) * w
        b, l, d = hidden_states.shape
        q = jax.nn.silu(_causal_dwconv(hidden_states @ W_q, conv_w_q))
        k = jax.nn.silu(_causal_dwconv(hidden_states @ W_k, conv_w_k))
        v = jax.nn.silu(_causal_dwconv(hidden_states @ W_v, conv_w_v))
        q = q.reshape(b, l, H, DK)
        k = k.reshape(b, l, H, DK)
        v = v.reshape(b, l, H, DV)
        beta = jax.nn.sigmoid(hidden_states @ W_b)
        delta_out, _ = _delta_rule_chunkwise(jnp.transpose(q, (0, 2, 1, 3)), jnp.transpose(k, (0, 2, 1, 3)), jnp.transpose(v, (0, 2, 1, 3)), jnp.transpose(beta, (0, 2, 1)))
        delta_out = jnp.transpose(delta_out, (0, 2, 1, 3))
        vc = v.reshape(b, l, H * DV)
        fir_s = _causal_dwconv(vc, fir_short_w.reshape(H * DV, -1)).reshape(b, l, H, DV)
        fir_l = _causal_dwconv(vc, fir_long_w.reshape(H * DV, -1)).reshape(b, l, H, DV)
        gate_in = jnp.concatenate([hidden_states, fir_s.reshape(b, l, -1), fir_l.reshape(b, l, -1), delta_out.reshape(b, l, -1)], -1)
        hid = jax.nn.gelu(gate_in @ W_fuse1 + b_fuse1, approximate=False)
        logits = (hid @ W_fuse2 + b_fuse2).reshape(b, l, H, 4)
        p_raw = jax.nn.sigmoid(logits[..., 3])
        floor = MIN_FLOOR + (MAX_FLOOR - MIN_FLOOR) * (1.0 - p_raw)
        p_val = (1.0 - floor) * p_raw
        tau = jnp.exp(others_log_tau)
        others = jax.nn.softmax(logits[..., :3] / tau[None, None, :, None], -1)
        p_ctx = (1.0 - p_val)[..., None] * others
        o = p_ctx[..., 0:1] * fir_s + p_ctx[..., 1:2] * fir_l + p_ctx[..., 2:3] * delta_out + p_val[..., None] * v
        o = _rmsnorm(o, norm_w)
        return o.reshape(b, l, H * DV) @ W_o

    def _L0_ffn_ref(x, W1, W2, Wr):
        import jax, jax.numpy as jnp
        import numpy as np
        B, T, D = (2, 512, 256)
        E, DFF, TOPK = (8, 1024, 2)
        TEMPERATURE = 1.0
        logits = jnp.einsum('btd,ed->bte', x, Wr)
        probs = jax.nn.softmax(logits / TEMPERATURE, axis=-1)
        topk_vals, topk_idx = jax.lax.top_k(probs, TOPK)
        router_weights = topk_vals / topk_vals.sum(-1, keepdims=True)
        one_hot = jax.nn.one_hot(topk_idx, E, dtype=x.dtype)
        gate = jnp.einsum('btk,btke->bte', router_weights, one_hot)
        h = jax.nn.silu(jnp.einsum('btd,efd->btef', x, W1))
        y = jnp.einsum('btef,edf->bted', h, W2)
        out = jnp.einsum('bte,bted->btd', gate, y)
        return out

    def _L1_xattn_ref(Q, K, V, Wq, bq, Wk, bk, Wv, bv, Wo, bo):
        import jax, jax.numpy as jnp
        import numpy as np
        D_MODEL = 256
        NUM_HEADS = 16
        D_K = D_MODEL // NUM_HEADS

        def _split_heads(x):
            B, S, _ = x.shape
            return x.reshape(B, S, NUM_HEADS, D_K).transpose(0, 2, 1, 3)
        q = _split_heads(Q @ Wq.T + bq)
        k = _split_heads(K @ Wk.T + bk)
        v = _split_heads(V @ Wv.T + bv)
        scale = 1.0 / jnp.sqrt(jnp.asarray(D_K, q.dtype))
        scores = jnp.einsum('bhqd,bhkd->bhqk', q, k) * scale
        attn = jax.nn.softmax(scores, axis=-1)
        out = jnp.einsum('bhqk,bhkd->bhqd', attn, v)
        B, H, S, dk = out.shape
        out = out.transpose(0, 2, 1, 3).reshape(B, S, H * dk)
        return out @ Wo.T + bo

    def _L1_attn_ref(inputs, Wq, Wk, Wv, Wo, q_norm_w, k_norm_w):
        import jax, jax.numpy as jnp
        import numpy as np
        B, L, HID = (8, 1025, 256)
        H, KV, DH = (16, 4, 64)
        EPS = 1e-06
        ROPE_BASE = 10000.0

        def _rms_norm(x, w):
            var = jnp.mean(jnp.square(x), axis=-1, keepdims=True)
            return x * jax.lax.rsqrt(var + EPS) * w

        def _rotate_half(x):
            x1, x2 = jnp.split(x, 2, axis=-1)
            return jnp.concatenate([-x2, x1], axis=-1)

        def _rope_cache(seq_len, dim):
            inv_freq = 1.0 / ROPE_BASE ** (jnp.arange(0, dim, 2, dtype=jnp.float32) / dim)
            pos = jnp.arange(seq_len, dtype=jnp.float32)
            freqs = pos[:, None] * inv_freq[None, :]
            emb = jnp.concatenate([freqs, freqs], axis=-1)
            return (jnp.cos(emb), jnp.sin(emb))
        b, l, _ = inputs.shape
        q = (inputs @ Wq.T).reshape(b, l, H, DH)
        k = (inputs @ Wk.T).reshape(b, l, KV, DH)
        v = (inputs @ Wv.T).reshape(b, l, KV, DH)
        q = _rms_norm(q, q_norm_w).transpose(0, 2, 1, 3)
        k = _rms_norm(k, k_norm_w).transpose(0, 2, 1, 3)
        v = v.transpose(0, 2, 1, 3)
        l_img = l - 1
        cos, sin = _rope_cache(l_img, DH)
        cos = cos[None, None].astype(q.dtype)
        sin = sin[None, None].astype(q.dtype)
        q_img = q[:, :, 1:]
        k_img = k[:, :, 1:]
        q = jnp.concatenate([q[:, :, :1], q_img * cos + _rotate_half(q_img) * sin], axis=2)
        k = jnp.concatenate([k[:, :, :1], k_img * cos + _rotate_half(k_img) * sin], axis=2)
        rep = H // KV
        k = jnp.repeat(k, rep, axis=1)
        v = jnp.repeat(v, rep, axis=1)
        scores = jnp.einsum('bhqd,bhkd->bhqk', q, k)
        attn = jax.nn.softmax(scores.astype(jnp.float32), axis=-1).astype(q.dtype)
        out = jnp.einsum('bhqk,bhkd->bhqd', attn, v)
        out = out.transpose(0, 2, 1, 3).reshape(b, l, H * DH)
        return out @ Wo.T

    def _L1_ffn_ref(hidden_states, gate_w, bias_e, up_w, down_w, shared_up, shared_down):
        import jax, jax.numpy as jnp
        import numpy as np
        DIM = 256
        N_EXPERTS = 16
        TOP_K = 4
        N_GROUP = 4
        TOPK_GROUP = 2
        MOE_INTER = 128
        SHARED_INTER = 512
        ROUTED_SCALE = 2.5

        def relu2(x):
            return jnp.square(jax.nn.relu(x))

        def _router(x2, gate_w, bias_e):
            T = x2.shape[0]
            logits = x2 @ gate_w.T
            scores = jax.nn.sigmoid(logits)
            sc = jax.lax.stop_gradient(scores + bias_e[None, :])
            grp = sc.reshape(T, N_GROUP, N_EXPERTS // N_GROUP)
            top2, _ = jax.lax.top_k(grp, 2)
            group_scores = top2.sum(-1)
            _, gidx = jax.lax.top_k(group_scores, TOPK_GROUP)
            rows = jnp.arange(T)[:, None]
            gmask = jnp.zeros((T, N_GROUP), dtype=sc.dtype).at[rows, gidx].set(1.0)
            smask = jnp.repeat(gmask, N_EXPERTS // N_GROUP, axis=1)
            masked = jnp.where(smask > 0, sc, 0.0)
            _, topk_idx = jax.lax.top_k(masked, TOP_K)
            topk_w = jnp.take_along_axis(scores, topk_idx, axis=1)
            topk_w = topk_w / (topk_w.sum(-1, keepdims=True) + 1e-20)
            topk_w = topk_w * ROUTED_SCALE
            return (topk_idx, topk_w)
        B, S, D = hidden_states.shape
        x2 = hidden_states.reshape(-1, D)
        T = x2.shape[0]
        topk_idx, topk_w = _router(x2, gate_w, bias_e)
        rows = jnp.arange(T)[:, None]
        combine = jnp.zeros((T, N_EXPERTS), dtype=topk_w.dtype).at[rows, topk_idx].add(topk_w)

        def body(acc, inp):
            wu, wd, cw = inp
            y = relu2(x2 @ wu.T) @ wd.T
            return (acc + cw[:, None] * y, None)
        routed, _ = jax.lax.scan(body, jnp.zeros_like(x2), (up_w, down_w, combine.T))
        shared = relu2(x2 @ shared_up.T) @ shared_down.T
        out = routed + shared
        return out.reshape(B, S, D)
    x = x + _L0_xattn_ref(_layernorm(x, axis=-1), ctx_1024, ctx_1024, mask_Bx1xS2_ik1, L0_xattn_Wq, L0_xattn_bq, L0_xattn_Wk, L0_xattn_bk, L0_xattn_Wv, L0_xattn_bv, L0_xattn_Wo, L0_xattn_bo, L0_xattn_g0, L0_xattn_beta0)
    x = x + _L0_attn_ref(_layernorm(x, axis=-1), L0_attn_W_q, L0_attn_W_k, L0_attn_W_v, L0_attn_W_b, L0_attn_conv_w_q, L0_attn_conv_w_k, L0_attn_conv_w_v, L0_attn_fir_short_w, L0_attn_fir_long_w, L0_attn_W_fuse1, L0_attn_b_fuse1, L0_attn_W_fuse2, L0_attn_b_fuse2, L0_attn_others_log_tau, L0_attn_norm_w, L0_attn_W_o)
    x = x + _L0_ffn_ref(_layernorm(x, axis=-1), L0_ffn_W1, L0_ffn_W2, L0_ffn_Wr)
    x = x + _L1_xattn_ref(_layernorm(x, axis=-1), ctx_1024, ctx_1024, L1_xattn_Wq, L1_xattn_bq, L1_xattn_Wk, L1_xattn_bk, L1_xattn_Wv, L1_xattn_bv, L1_xattn_Wo, L1_xattn_bo)
    x = x + _L1_attn_ref(_layernorm(x, axis=-1), L1_attn_Wq, L1_attn_Wk, L1_attn_Wv, L1_attn_Wo, L1_attn_q_norm_w, L1_attn_k_norm_w)
    x = x + _L1_ffn_ref(_layernorm(x, axis=-1), L1_ffn_gate_w, L1_ffn_bias_e, L1_ffn_up_w, L1_ffn_down_w, L1_ffn_shared_up, L1_ffn_shared_down)
    return x

_drawn_inputs = setup_inputs


def setup_inputs(seed=0):
    import zlib

    import numpy as np

    out = dict(_drawn_inputs(seed))
    spreads = {'L0_xattn_bq': (0.0, 0.1),
     'L0_xattn_bk': (0.0, 0.8),
     'L0_xattn_bv': (0.0, 0.1),
     'L0_xattn_bo': (0.0, 0.1),
     'L0_xattn_g0': (1.0, 0.2),
     'L0_xattn_beta0': (0.0, 0.1),
     'L0_attn_b_fuse1': (0.0, 0.8),
     'L0_attn_others_log_tau': (0.0, 0.8),
     'L0_attn_norm_w': (1.0, 0.2),
     'L1_attn_q_norm_w': (1.0, 0.2),
     'L1_attn_k_norm_w': (1.0, 0.2),
     'L1_ffn_bias_e': (0.0, 0.402)}
    factors = {'L0_attn_W_q': 8.0,
     'L0_attn_W_k': 8.0,
     'L0_attn_W_b': 8.0,
     'L0_attn_conv_w_q': 8.0,
     'L0_attn_conv_w_k': 8.0,
     'L0_attn_fir_short_w': 8.0,
     'L0_attn_fir_long_w': 8.0,
     'L0_attn_W_fuse1': 8.0,
     'L0_attn_W_fuse2': 8.0,
     'L1_xattn_bq': 4.823,
     'L1_xattn_bk': 8.0,
     'L1_ffn_gate_w': 4.53,
     'L1_ffn_up_w': 3.136,
     'L1_ffn_down_w': 2.871}
    for name, (base, spread) in spreads.items():
        noise = np.random.default_rng([zlib.crc32(name.encode()), seed]).standard_normal(out[name].shape)
        drawn = base * np.exp(spread * noise) if base else spread * noise
        out[name] = jnp.asarray(drawn.astype(out[name].dtype))
    for name, factor in factors.items():
        out[name] = (out[name] * factor).astype(out[name].dtype)
    return out
```

```python
from contextlib import ExitStack

import numpy as np

import concourse.bass as bass
from concourse import mybir

F32 = mybir.dt.float32
I32 = mybir.dt.int32
ALU = mybir.AluOpType
ACT = mybir.ActivationFunctionType
AX = mybir.AxisListType

P = 128
B, L, D = 64, 32, 256
DC = D // P
NK = 257
ROWS = B * L
NT = ROWS // P
BT = P // L
NG = ROWS // 512

ENGINES = ("pe", "act", "dve", "pool", "sp")


class Stage:

    def __init__(self, K, name, turns):
        self.K, self.name, self.turns = K, name, turns
        self.steps = {e: [] for e in ENGINES}
        self.first = {e: [] for e in ENGINES}
        self.dma, self.late = {}, False

    def step(self, engine, name, emit, needs=(), dmas=0, late=False):
        self.steps[engine].append((name, emit, tuple(needs), late))
        self.late = self.late or late
        if dmas:
            self.dma[name] = (self.K.sem(f"{self.name}_{name}"), 16 * dmas)

    def before(self, engine, emit, needs=()):
        self.first[engine].append((emit, needs))

    def wanted(self, need, turn):
        what, _, back = need.partition("<")
        engine, _, name = what.partition(".")
        back = int(back or 0)
        if name in self.dma:
            sem, per = self.dma[name]
            return sem, (turn + 1 - back) * per
        at = [s[0] for s in self.steps[engine]].index(name)
        per = len(self.steps[engine])
        return self.K.count[engine], (turn + 2 - back) * per + at + 1 + self.base[engine]

    def turn(self, eng, key, i, which=None):
        for name, emit, needs, late in self.steps[key]:
            if which is not None and late != which:
                if name not in self.dma:
                    eng.drain().then_inc(self.K.count[key], 1)
                continue
            latest = {}
            for need in needs:
                engine = need if need.partition("<")[0].partition(".")[2] in self.dma else need[:need.index(".")]
                if engine not in latest or self.wanted(need, 0)[1] > self.wanted(latest[engine], 0)[1]:
                    latest[engine] = need
            for need in latest.values():
                eng.wait_ge(*self.wanted(need, i))
                if key == "sp" and not isinstance(i, int):
                    eng.sem_inc(self.K.gate[key], 1)
            if needs and key != "sp" and not isinstance(i, int):
                eng.sem_inc(self.K.gate[key], 1)
            done = emit(eng, i - 1 if late else i)
            if name not in self.dma:
                done.then_inc(self.K.count[key], 1)

    def run(self):
        used = [e for e in ENGINES if self.steps[e] or self.first[e]]
        self.base = dict(self.K.base)
        for e in used:
            self.K.base[e] += (self.turns + 2 + self.late) * len(self.steps[e])
        with self.K.nc.Block() as block:
            def program(key):
                def body(eng):
                    for emit, needs in self.first[key]:
                        for sem, value in needs:
                            eng.wait_ge(sem, value)
                        emit(eng)
                    if not self.steps[key]:
                        return
                    eng.sem_inc(self.K.count[key], 2 * len(self.steps[key]))
                    if self.late:
                        self.turn(eng, key, 0, False)
                        with eng.Fori(1, self.turns) as i:
                            self.turn(eng, key, i)
                        self.turn(eng, key, self.turns, True)
                    elif self.turns == 1:
                        self.turn(eng, key, 0)
                    else:
                        with eng.Fori(0, self.turns) as i:
                            self.turn(eng, key, i)
                return body
            for key, where in (("sp", block.sync), ("pool", block.gpsimd), ("act", block.scalar),
                               ("pe", block.tensor), ("dve", block.vector)):
                if key in used:
                    where(program(key))


class Kern:

    def __init__(self, nc, ctx, ins, out):
        self.nc, self.ctx, self.ins, self.out = nc, ctx, ins, out

    def sem(self, name):
        return self.ctx.enter_context(self.nc.semaphore(name))

    def sb(self, name, shape, dt=F32, ctx=None):
        return (ctx or self.ctx).enter_context(self.nc.sbuf_tensor(name, shape, dt))


def features(w):
    return w.rearrange("(c p) m -> p c m", p=P)


def tile_at(i, s):
    return bass.ds(2 * i + s, 1)


def cols_at(i, s, width=P):
    return bass.ds((2 * i + s) * width, width)


def load(K, name, dst, srcs):
    sem = K.sem("ld_" + name)
    for d, s in zip(dst, srcs):
        K.pending.append((d, s, sem))
    return sem, 16 * len(dst)


def start_loads(K, stage):
    pending, K.pending = K.pending, []

    def emit(eng):
        for d, s, sem in pending:
            eng.dma_start(d, s).then_inc(sem, 16)
    stage.before("sp", emit)


def row_stats(K, tag, src, eps, wait=()):
    S = Stage(K, tag, 1)
    S.before("dve", lambda e: None, wait)
    start_loads(K, S)

    def stats(e, i):
        for t in range(NT):
            done = e.bn_stats(K.bn[:, t, :], src[:, t, :])
        return done

    def aggregate(e, i):
        for t in range(NT):
            done = e.bn_aggr(K.mv[:, t, :], K.bn[:, t, :])
        return done
    S.step("dve", "stats", stats)
    S.step("dve", "aggr", aggregate, ["dve.stats"])
    S.step("dve", "eps", lambda e, i: e.tensor_scalar(K.std[:, :], K.mv[:, :, 1], eps, None, ALU.add), ["dve.aggr"])
    S.step("act", "root", lambda e, i: e.activation(K.std[:, :], K.std[:, :], ACT.Sqrt), ["dve.eps"])
    S.step("dve", "inv", lambda e, i: e.reciprocal(K.rstd[:, :], K.std[:, :]), ["act.root"])
    S.run()


def norm_transpose(K, tag, extra=None):
    S = Stage(K, tag, NT // 2)
    for s in range(2):
        S.step("dve", f"xn{s}", lambda e, i, s=s: e.tensor_scalar(
            K.xnb[:, s, :], K.x[:, tile_at(i, s), :], K.mv[:, tile_at(i, s), 0], K.rstd[:, tile_at(i, s)],
            ALU.subtract, ALU.mult), [f"pe.tr{s}<1"])

        def transposes(e, i, s=s):
            for c in range(DC):
                done = e.transpose(K.ps[:, s, c * P:(c + 1) * P], K.xnb[:, s, c * P:(c + 1) * P], K.ident[:, :])
            return done
        S.step("pe", f"tr{s}", transposes, [f"dve.xn{s}", f"act.ev{s}<1"])
    last = []
    if extra:
        last = extra(S)
    for s in range(2):
        S.step("act", f"ev{s}", lambda e, i, s=s: e.activation(
            K.xs[:, s, :, :], K.ps[:, s, 0:D].rearrange("p (c n) -> p c n", c=DC), ACT.Copy),
            [f"pe.tr{s}", f"pool.cp{s}<1"] + [n.format(s=s) + "<1" for n in last])
        S.step("pool", f"cp{s}", lambda e, i, s=s: e.tensor_copy(
            K.xnT[:, :, cols_at(i, s)], K.xs[:, s, :, :]), [f"act.ev{s}"])
    S.run()


def feature_gemm(K, tag, outT, w, inT, kc, mc, finish, needs=(), pre=None):
    S = Stage(K, tag, NG)
    S.before("pe", lambda e: None, needs)
    nb = min(4, mc)
    assert mc % nb == 0
    for m in range(mc):
        bank = K.ps[:, m % nb, :]
        key, emit = finish(m)
        free = f"{key if m >= nb else finish(m + mc - nb)[0]}.ev{m - nb if m >= nb else m + mc - nb}" + ("" if m >= nb else "<1")
        if m >= nb:
            free = f"{finish(m - nb)[0]}.ev{m - nb}"

        def product(e, i, m=m, bank=bank):
            for k in range(kc):
                done = e.matmul(bank, w[:, k, m * P:(m + 1) * P], inT(k, i), start=(k == 0), stop=(k == kc - 1))
            return done
        S.step("pe", f"mm{m}", product, [free])
        S.step(key, f"ev{m}", lambda e, i, emit=emit, bank=bank: emit(e, i, bank), [f"pe.mm{m}"])
    if pre:
        pre(S)
    S.run()


def rows_of(t):
    return lambda k, i: t[:, k, bass.ds(i * 512, 512)]


def cross_attention_0(K):
    I = K.ins
    with ExitStack() as ctx:
        def sb(name, shape, dt=F32):
            return K.sb("a0_" + name, shape, dt, ctx)
        wq, wkT, wv, wo = (sb(n, [P, DC, D]) for n in ("wq", "wkT", "wv", "wo"))
        bq, bk, bv = (sb(n, [P, DC]) for n in ("bq", "bk", "bv"))
        bo, g0, beta0 = (sb(n, [P, D]) for n in ("bo", "g0", "beta0"))
        qT, kqT = (sb(n, [P, DC, ROWS]) for n in ("qT", "kqT"))
        ctxT = sb("ctxT", [P, 2, DC, BT, NK])
        ctxR = sb("ctxR", [P, 2, 2, BT, D])
        ctxL = sb("ctxL", [1, 2, BT, D])
        mask = sb("mask", [P, 2, NK], I32)
        off = sb("off", [P, 2, NK])
        keep = sb("keep", [P, 2, NK])
        qs = sb("qs", [P, 2, DC, P])
        kqs = sb("kqs", [P, 2, DC, P])
        qbk = sb("qbk", [P, 2])
        sc = sb("sc", [P, 2, NK])
        sm = sb("sm", [P, 2, NK])
        pr = sb("pr", [P, 2, NK])
        prT = sb("prT", [P, 2, 2, P])
        prL = sb("prL", [1, 2, P])
        mx, neg, tot, inv = (sb(n, [P, 2]) for n in ("mx", "neg", "tot", "inv"))
        mix = sb("mix", [P, 2, D])
        y = sb("y", [P, NT, D])

        w_qk = load(K, "a0_qk", [wq[:, :, :], wkT[:, :, :]], [features(I["L0_xattn_Wq"]), features(I["L0_xattn_WkT"])])
        w_b = load(K, "a0_b", [bq[:, :], bk[:, :], bv[:, :], bo[:, :], g0[:, :], beta0[:, :]],
                   [I["L0_xattn_" + n] for n in ("bq", "bk", "bv")]
                   + [I["L0_xattn_" + n].partition_broadcast(P) for n in ("bo", "g0", "beta0")])
        w_vo = load(K, "a0_vo", [wv[:, :, :], wo[:, :, :]], [features(I["L0_xattn_Wv"]), features(I["L0_xattn_Wo"])])
        row_stats(K, "a0_ln", K.x, 1e-5, [K.x_loaded])
        norm_transpose(K, "a0_nt")

        def q_finish(m):
            return "dve", lambda e, i, ps, m=m: e.tensor_scalar(
                qT[:, m, bass.ds(i * 512, 512)], ps, bq[:, m:m + 1], 1.0 / 16.0, ALU.add, ALU.mult)
        feature_gemm(K, "a0_q", qT, wq, rows_of(K.xnT), DC, DC, q_finish, [w_qk, w_b])

        def kq_finish(m):
            return ("dve", "act")[m], lambda e, i, ps, m=m: copy(e, kqT[:, m, bass.ds(i * 512, 512)], ps)
        feature_gemm(K, "a0_kq", kqT, wkT, rows_of(qT), DC, DC, kq_finish)

        S = Stage(K, "a0_at", NT // 2)
        mask_rows = I["mask"].rearrange("b q k -> b (q k)")
        for s in range(2):
            def loads(e, i, s=s):
                at = bass.ds((2 * i + s) * BT, BT)
                sem = S.dma[f"ctx{s}"][0]
                for c in range(DC):
                    e.dma_start(ctxT[:, s, c, :, :], I["ctxT"][at, c * P:(c + 1) * P, :].rearrange(
                        "b p k -> p b k")).then_inc(sem, 16)
                for c in range(2):
                    e.dma_start(ctxR[:, s, c, :, :], I["ctx"][at, c * P:(c + 1) * P, :].rearrange(
                        "b p d -> p b d")).then_inc(sem, 16)
                e.dma_start(ctxL[:, s, :, :], I["ctx"][at, NK - 1:NK, :].rearrange(
                    "b k d -> k b d")).then_inc(sem, 16)
                for b in range(BT):
                    e.dma_start(mask[L * b:L * b + L, s, :], mask_rows[bass.ds((2 * i + s) * BT + b, 1), :].rearrange(
                        "a k -> (a k)").partition_broadcast(L)).then_inc(sem, 16)
            S.step("sp", f"ctx{s}", loads, [f"pe.pv{s}<1", f"pool.keep{s}<1"], dmas=5 + BT)

            S.step("pool", f"qs{s}", lambda e, i, s=s: e.tensor_copy(qs[:, s, :, :], qT[:, :, cols_at(i, s)]),
                   [f"pe.sc{s}<1"])
            S.step("pool", f"kqs{s}", lambda e, i, s=s: e.tensor_copy(kqs[:, s, :, :], kqT[:, :, cols_at(i, s)]),
                   [f"pe.sc{s}<1"])
            S.step("pool", f"off{s}", lambda e, i, s=s: e.tensor_scalar(
                off[:, s, :], mask[:, s, :], 0.0, -1e9, ALU.is_equal, ALU.mult), [f"sp.ctx{s}", f"dve.sm{s}<1"])
            S.step("pool", f"keep{s}", lambda e, i, s=s: e.tensor_scalar(
                keep[:, s, :], off[:, s, :], 0.0, None, ALU.is_equal), [f"pool.off{s}", f"dve.sc{s}<1"])

            def scores(e, i, s=s):
                for c in range(DC):
                    e.matmul(K.ps[:, s, 300:301], qs[:, s, c, :], bk[:, c:c + 1], start=(c == 0), stop=(c == DC - 1))
                for c in range(DC):
                    for b in range(BT):
                        done = e.matmul(K.ps[L * b:L * b + L, s, 0:NK], kqs[:, s, c, L * b:L * b + L],
                                        ctxT[:, s, c, b, :], start=(c == 0), stop=(c == DC - 1))
                return done
            S.step("pe", f"sc{s}", scores, [f"sp.ctx{s}", f"pool.kqs{s}", f"dve.sc{s}<1"])
            S.step("dve", f"qbk{s}", lambda e, i, s=s: e.tensor_copy(qbk[:, s:s + 1], K.ps[:, s, 300:301]),
                   [f"pe.sc{s}", f"dve.sc{s}<1"])
        for s in range(2):
            S.step("dve", f"sc{s}", lambda e, i, s=s: e.scalar_tensor_tensor(
                sc[:, s, :], K.ps[:, s, 0:NK], qbk[:, s:s + 1], keep[:, s, :], ALU.add, ALU.mult),
                [f"dve.qbk{s}", f"pool.keep{s}"])
            S.step("dve", f"sm{s}", lambda e, i, s=s: e.tensor_tensor(
                sm[:, s, :], sc[:, s, :], off[:, s, :], ALU.add), [f"dve.sc{s}", f"act.exp{s}<1"])
            S.step("dve", f"mx{s}", lambda e, i, s=s: e.tensor_reduce(
                neg[:, s:s + 1], sm[:, s, :], AX.X, ALU.max, negate=True), [f"dve.sm{s}"])
            S.step("act", f"exp{s}", lambda e, i, s=s: e.activation(
                pr[:, s, :], sm[:, s, :], ACT.Exp, bias=neg[:, s:s + 1], accum_out=tot[:, s:s + 1]),
                [f"dve.mx{s}", f"pe.prT{s}<1", f"dve.inv{s}<1"])
            S.step("dve", f"inv{s}", lambda e, i, s=s: e.reciprocal(inv[:, s:s + 1], tot[:, s:s + 1]),
                   [f"act.exp{s}", f"act.mix{s}<1"])

        for s in range(2):
            def turn_probs(e, i, s=s):
                e.transpose(K.ps[:, 2 + s, 0:P], pr[:, s, 0:P], K.ident[:, :])
                e.transpose(K.ps[:, 2 + s, P:2 * P], pr[:, s, P:2 * P], K.ident[:, :])
                return e.transpose(K.ps[0:1, 2 + s, 2 * P:3 * P], pr[:, s, 2 * P:NK], K.ident[:, :])
            S.step("pe", f"prT{s}", turn_probs, [f"act.exp{s}", f"act.prL{s}<1", f"dve.prT{s}<1"])
            S.step("dve", f"prT{s}", lambda e, i, s=s: e.tensor_copy(
                prT[:, s, :, :], K.ps[:, 2 + s, 0:2 * P].rearrange("p (c n) -> p c n", c=2)),
                [f"pe.prT{s}", f"pe.pv{s}<1"])
            S.step("act", f"prL{s}", lambda e, i, s=s: e.activation(
                prL[:, s, :], K.ps[0:1, 2 + s, 2 * P:3 * P], ACT.Copy), [f"dve.prT{s}", f"pe.pv{s}<1"])

            def mixing(e, i, s=s):
                for b in range(BT):
                    rows = slice(L * b, L * b + L)
                    e.matmul(K.ps[rows, 4 + s, 0:D], prT[:, s, 0, rows], ctxR[:, s, 0, b, :], start=True, stop=False)
                    e.matmul(K.ps[rows, 4 + s, 0:D], prT[:, s, 1, rows], ctxR[:, s, 1, b, :], start=False, stop=False)
                    done = e.matmul(K.ps[rows, 4 + s, 0:D], prL[:, s, rows], ctxL[:, s, b, :], start=False, stop=True)
                return done
            S.step("pe", f"pv{s}", mixing, [f"act.prL{s}", f"act.mix{s}<1"])
            S.step("act", f"mix{s}", lambda e, i, s=s: e.activation(
                mix[:, s, :], K.ps[:, 4 + s, 0:D], ACT.Copy, scale=inv[:, s:s + 1]),
                [f"pe.pv{s}", f"dve.inv{s}", f"pe.mixT{s}<1"])
        for s in range(2):
            def turn_mix(e, i, s=s):
                for c in range(DC):
                    done = e.transpose(K.ps[:, 6 + s, c * P:(c + 1) * P], mix[:, s, c * P:(c + 1) * P], K.ident[:, :])
                return done
            S.step("pe", f"mixT{s}", turn_mix, [f"act.mix{s}", f"dve.mixT{s}<1"])
            S.step("dve", f"mixT{s}", lambda e, i, s=s: e.tensor_copy(
                kqT[:, :, cols_at(i, s)], K.ps[:, 6 + s, 0:D].rearrange("p (c n) -> p c n", c=DC)), [f"pe.mixT{s}", f"pool.kqs{s}"])
        S.run()

        def v_finish(m):
            return ("dve", "act")[m], lambda e, i, ps, m=m: add_bias(e, qT[:, m, bass.ds(i * 512, 512)], ps, bv[:, m:m + 1])
        feature_gemm(K, "a0_v", qT, wv, rows_of(kqT), DC, DC, v_finish, [w_vo])
        output_rows(K, "a0_o", qT, wo, DC, lambda e, t, ps: e.tensor_tensor(y[:, t, :], ps, bo[:, :], ALU.add))

        row_stats(K, "a0_ln2", y, 1e-5)
        S = Stage(K, "a0_res", NT // 2)
        for s in range(2):
            S.step("dve", f"g{s}", lambda e, i, s=s: e.scalar_tensor_tensor(
                y[:, tile_at(i, s), :], y[:, tile_at(i, s), :], K.mv[:, tile_at(i, s), 0], g0[:, :], ALU.subtract, ALU.mult))
            S.step("pool", f"b{s}", lambda e, i, s=s: e.tensor_tensor(
                K.x[:, tile_at(i, s), :], K.x[:, tile_at(i, s), :], beta0[:, :], ALU.add))
        for s in range(2):
            S.step("dve", f"r{s}", lambda e, i, s=s: e.scalar_tensor_tensor(
                K.x[:, tile_at(i, s), :], y[:, tile_at(i, s), :], K.rstd[:, tile_at(i, s)], K.x[:, tile_at(i, s), :],
                ALU.mult, ALU.add), [f"dve.g{s}", f"pool.b{s}"])
        S.run()


def copy(e, out, ps):
    if e.engine == mybir.EngineType.Activation:
        return e.activation(out, ps, ACT.Copy)
    return e.tensor_copy(out, ps)


def add_bias(e, out, ps, bias):
    if e.engine == mybir.EngineType.Activation:
        return e.activation(out, ps, ACT.Identity, bias=bias)
    return e.tensor_scalar(out, ps, bias, None, ALU.add)


def output_rows(K, tag, inT, w, kc, finish, needs=(), pre=None, after=None):
    S = Stage(K, tag, NT // 2)
    S.before("pe", lambda e: None, needs)
    if pre:
        pre(S)
    for s in range(2):
        S.step("pool", f"st{s}", lambda e, i, s=s: e.tensor_copy(
            K.stage[:, s, 0:kc, :], inT[:, 0:kc, cols_at(i, s)]), [f"pe.mm{s}<1"])

        def product(e, i, s=s):
            for k in range(kc):
                done = e.matmul(K.ps[:, s, 0:D], K.stage[:, s, k, :], w[:, k, :], start=(k == 0), stop=(k == kc - 1))
            return done
        S.step("pe", f"mm{s}", product, [f"pool.st{s}", f"dve.ev{s}<1"])
        S.step("dve", f"ev{s}", lambda e, i, s=s: finish(e, tile_at(i, s), K.ps[:, s, 0:D]),
               [f"pe.mm{s}"] + ([after.format(s=s)] if after else []))
    S.run()


def constants(K):
    S = Stage(K, "cst", 1)
    S.step("pool", "zero", lambda e, i: e.memset(K.ident[:, :], 0.0))
    S.step("pool", "one", lambda e, i: e.affine_select(
        out=K.ident[:, :], in_=K.ident[:, :], compare_op=ALU.not_equal, fill=1.0, base=0,
        pattern=[[-1, P]], channel_multiplier=1), ["pool.zero"])
    sem = K.sem("ld_x")
    x_rows = K.ins["x"].rearrange("(t p) d -> p t d", p=P)
    S.before("sp", lambda e: e.dma_start(K.x[:, :, :], x_rows).then_inc(sem, 16))
    S.before("sp", lambda e: e.dma_start(K.masks[:, :], K.ins["masks"]).then_inc(sem, 16))
    S.before("sp", lambda e: e.dma_start(K.before[:, :, :], K.ins["before"].partition_broadcast(P)).then_inc(sem, 16))
    K.x_loaded = (sem, 48)
    S.run()


def store(K):
    S = Stage(K, "out", 1)
    sem = K.sem("st_out")
    S.before("sp", lambda e: (e.dma_start(K.out.rearrange("(t p) d -> p t d", p=P), K.x[:, :, :]).then_inc(sem, 16),
                              e.wait_ge(sem, 16)))
    S.run()


H0, DV0 = 4, 64
TAPS, SHORT, LONG = 4, 3, 31


def row_logits(K, w, n, dst):
    def extra(S):
        for s in range(2):
            def product(e, i, s=s):
                for c in range(DC):
                    done = e.matmul(K.ps[:, 2 + s, 0:n], K.xs[:, s, c, :], w[:, c, :], start=(c == 0), stop=(c == DC - 1))
                return done
            S.step("pe", f"lg{s}", product, [f"act.ev{s}", f"dve.lg{s}<1"])
            S.step("dve", f"lg{s}", lambda e, i, s=s: e.tensor_copy(dst[:, tile_at(i, s), :], K.ps[:, 2 + s, 0:n]),
                   [f"pe.lg{s}"])
        return ["pe.lg{s}"]
    return extra


def delta_attention(K):
    I = K.ins
    with ExitStack() as ctx:
        def sb(name, shape, dt=F32, c=ctx):
            return K.sb("b0_" + name, shape, dt, c)
        wqkv = sb("wqkv", [P, 3, DC, D])
        wo = sb("wo", [P, DC, D])
        wb = sb("wb", [P, DC, H0])
        conv = sb("conv", [P, 3, DC, TAPS])
        fir = sb("fir", [P, DC, SHORT + LONG])
        bf1 = sb("bf1", [P, 4])
        f2 = sb("f2", [P, 4, 16])
        bf2 = sb("bf2", [P, 16])
        ltau = sb("ltau", [P, H0])
        nw = sb("nw", [P, 1])
        beta = sb("beta", [P, NT, H0])
        qk = sb("qk", [P, 4, ROWS])
        F = sb("F", [P, 6, ROWS])
        dr = sb("dr", [P, NT, D])
        lg = sb("lg", [P, NT, H0, 4])
        gates = sb("gates", [P, NT, H0, 4])
        rn = sb("rn", [P, NT, 8])
        cb = sb("cb", [P, NT, H0])
        ab = sb("ab", [P, NT, H0])

        w_1 = load(K, "b0_1", [wqkv[:, j, :, :] for j in range(3)] + [wb[:, :, :], conv[:, :, :, :], fir[:, :, :]],
                   [features(I["L0_attn_W_" + n]) for n in ("q", "k", "v")] + [features(I["L0_attn_W_b"]),
                    I["L0_attn_conv"], I["L0_attn_fir"]])
        w_2 = load(K, "b0_2", [bf1[:, :], f2[:, :, :], bf2[:, :], ltau[:, :], nw[:, :], wo[:, :, :]],
                   [I["L0_attn_b_fuse1"], features(I["L0_attn_W_fuse2"]),
                    I["L0_attn_b_fuse2"].partition_broadcast(P), I["L0_attn_others_log_tau"].partition_broadcast(P),
                    I["L0_attn_norm_w"], features(I["L0_attn_W_o"])])
        row_stats(K, "b0_ln", K.x, 1e-5, [w_1])
        S = Stage(K, "b0_w", 1)
        S.before("pe", lambda e: None, [w_1])
        S.run()
        norm_transpose(K, "b0_nt", row_logits(K, wb, H0, beta))

        with ExitStack() as c1:
            cv = sb("cv", [P, 6, 512], c=c1)
            S = Stage(K, "b0_qkv", NG)
            S.before("act", lambda e: e.activation(beta[:, :, :], beta[:, :, :], ACT.Sigmoid))
            jobs = [(j, m) for j in range(3) for m in range(DC)]
            for n, (j, m) in enumerate(jobs):
                def product(e, i, j=j, m=m, n=n):
                    for k in range(DC):
                        done = e.matmul(K.ps[:, n, :], wqkv[:, j, k, m * P:(m + 1) * P], K.xnT[:, k, bass.ds(i * 512, 512)],
                                        start=(k == 0), stop=(k == DC - 1))
                    return done
                S.step("pe", f"mm{n}", product, [f"dve.tap{n}_2<1"])
                S.step("act", f"tap{n}", lambda e, i, j=j, m=m, n=n: e.activation(
                    cv[:, n, :], K.ps[:, n, :], ACT.Copy, scale=conv[:, j, m, TAPS - 1:TAPS]),
                    [f"pe.mm{n}", f"act.silu{n}<1"])
                if n >= 2:
                    silu(S, jobs[n - 2], n - 2, cv, qk, F)
            silu(S, jobs[4], 4, cv, qk, F)
            silu(S, jobs[5], 5, cv, qk, F)
            for pair in (0, 2, 4):
                for sh in range(1, TAPS):
                    for n in (pair, pair + 1):
                        j, m = jobs[n]

                        def tap(e, i, j=j, m=m, n=n, sh=sh):
                            src = K.ps[:, n, :].rearrange("p (b l) -> p b l", l=L)[:, :, 0:L - sh]
                            acc = cv[:, n, :].rearrange("p (b l) -> p b l", l=L)[:, :, sh:L]
                            return e.scalar_tensor_tensor(acc, src, conv[:, j, m, TAPS - 1 - sh:TAPS - sh], acc,
                                                          ALU.mult, ALU.add)
                        S.step("dve", f"tap{n}_{sh - 1}", tap,
                               [f"act.tap{n}"] if sh == 1 else [f"dve.tap{n}_{sh - 2}"])
            S.run()

        with ExitStack() as c1:
            sq = sb("sq", [P, 2, 4, P], c=c1)
            S = Stage(K, "b0_n2", NT // 2)
            for s in range(2):
                S.step("act", f"sq{s}", lambda e, i, s=s: e.activation(sq[:, s, :, :], qk[:, :, cols_at(i, s)], ACT.Square),
                       [f"pe.n{s}<1"])

                def sums(e, i, s=s):
                    for c in range(4):
                        done = e.matmul(K.ps[:, s, 2 * c:2 * c + 2], sq[:, s, c, :], K.headsel, start=True, stop=True)
                    return done
                S.step("pe", f"n{s}", sums, [f"act.sq{s}", f"dve.n{s}<1"])
                S.step("dve", f"n{s}", lambda e, i, s=s: e.tensor_scalar(
                    rn[:, tile_at(i, s), :], K.ps[:, s, 0:8], 1e-6, None, ALU.add), [f"pe.n{s}"])
            S.run()
        S = Stage(K, "b0_rn", 1)
        S.step("act", "root", lambda e, i: e.activation(rn[:, :, :], rn[:, :, :], ACT.Sqrt))
        S.step("dve", "inv", lambda e, i: e.reciprocal(rn[:, :, :], rn[:, :, :]), ["act.root"])
        S.step("dve", "ab", lambda e, i: e.tensor_tensor(ab[:, :, :], beta[:, :, :], rn[:, :, 4:8], ALU.mult), ["dve.inv"])
        S.step("dve", "cb", lambda e, i: e.tensor_tensor(cb[:, :, :], ab[:, :, :], rn[:, :, 4:8], ALU.mult), ["dve.ab"])
        S.run()
        fir_stage(K, F, fir)
        delta_solve(K, sb, qk, F, dr, rn, cb, ab)

        with ExitStack() as c1:
            hid = sb("hid", [P, 4, 512], c=c1)
            f1 = sb("f1", [P, 8, 512], c=c1)
            w_f1 = load(K, "b0_f1", [f1[:, :, :]], [features(I["L0_attn_W_fuse1"])])
            S = Stage(K, "b0_fuse", NG)
            start_loads(K, S)
            S.before("pe", lambda e: None, [w_f1])
            S.before("pe", lambda e: None, [w_2])
            S.before("act", lambda e: None, [w_2])
            S.before("dve", lambda e: None, [w_2])

            def source(k, i):
                at = bass.ds(i * 512, 512)
                return (K.xnT[:, k, at] if k < 2 else F[:, k, at] if k < 6 else qk[:, k - 6, at])
            for m in range(4):
                def product(e, i, m=m):
                    for k in range(8):
                        done = e.matmul(K.ps[:, m, :], f1[:, k, m * P:(m + 1) * P], source(k, i), start=(k == 0), stop=(k == 7))
                    return done
                S.step("pe", f"h{m}", product, [f"act.h{m}<1"])
                S.step("act", f"h{m}", lambda e, i, m=m: e.activation(
                    hid[:, m, :], K.ps[:, m, :], ACT.Gelu, bias=bf1[:, m:m + 1]), [f"pe.h{m}", "pe.lg<1"])

            def logits(e, i):
                for t in range(4):
                    for k in range(4):
                        done = e.matmul(K.ps[:, 4, 16 * t:16 * t + 16], hid[:, k, t * P:(t + 1) * P], f2[:, k, :],
                                        start=(k == 0), stop=(k == 3))
                return done
            S.step("pe", "lg", logits, ["act.h3", "dve.lg<1"])
            S.step("dve", "lg", lambda e, i: e.tensor_tensor(
                lg[:, bass.ds(4 * i, 4), :, :].rearrange("p t h g -> p t (h g)"), K.ps[:, 4, 0:64].rearrange("p (t g) -> p t g", t=4),
                bf2[:, :].unsqueeze(1).to_broadcast([P, 4, 16]), ALU.add), ["pe.lg"])
            S.run()
        mixture_gates(K, sb, lg, gates, ltau)
        delta_mix(K, sb, F, dr, gates, wo, nw)


def silu(S, job, n, cv, qk, F):
    j, m = job
    dst = (qk[:, m, :], qk[:, 2 + m, :], F[:, m, :])[j]
    S.step("act", f"silu{n}", lambda e, i, n=n: e.activation(dst[:, bass.ds(i * 512, 512)], cv[:, n, :], ACT.Silu),
           [f"dve.tap{n}_2"])


def fir_stage(K, F, fir):
    S = Stage(K, "b0_fir", 1)
    lanes = [(m, 2 + m, 0, SHORT) for m in range(DC)] + [(m, 4 + m, SHORT, LONG) for m in range(DC)]
    for n, (src, dst, at, taps) in enumerate(lanes):
        S.step("act", f"t{n}_0", lambda e, i, src=src, dst=dst, at=at, taps=taps: e.activation(
            F[:, dst, :], F[:, src, :], ACT.Copy, scale=fir[:, src, at + taps - 1:at + taps]))
    for sh in range(1, LONG):
        for n, (src, dst, at, taps) in enumerate(lanes):
            if sh < taps:
                def tap(e, i, src=src, dst=dst, at=at, taps=taps, sh=sh):
                    x = F[:, src, :].rearrange("p (b l) -> p b l", l=L)[:, :, 0:L - sh]
                    acc = F[:, dst, :].rearrange("p (b l) -> p b l", l=L)[:, :, sh:L]
                    return e.scalar_tensor_tensor(acc, x, fir[:, src, at + taps - 1 - sh:at + taps - sh], acc, ALU.mult, ALU.add)
                S.step("dve", f"t{n}_{sh}", tap, [f"act.t{n}_0" if sh == 1 else f"dve.t{n}_{sh - 1}"])
    S.run()


def delta_solve(K, sb, qk, F, dr, rn, cb, ab):
    with ExitStack() as ctx:
        kqs = sb("kqs", [P, 2, 4, P], c=ctx)
        vs = sb("vs", [P, 2, DC, P], c=ctx)
        cm, Ac, ATc, X, Y, P1 = (sb(n, [P, 2, H0, L], c=ctx) for n in ("cm", "Ac", "ATc", "X", "Y", "P1"))
        Lbd, Ybd = (sb(n, [P, 2, H0, P], c=ctx) for n in ("Lbd", "Ybd"))
        AT = [sb(f"AT{m}", [P, 2, H0, P], c=ctx) for m in range(4)]
        v0, w1, w2, u, od = (sb(n, [P, 2, D], c=ctx) for n in ("v0", "w1", "w2", "u", "od"))
        S = Stage(K, "b0_ds", NT // 2)
        low = K.low.unsqueeze(1).to_broadcast([P, H0, L])
        one = K.eye.unsqueeze(1).to_broadcast([P, H0, L])
        half = K.half.unsqueeze(1).to_broadcast([P, H0, L])

        def heads(ap):
            return ap.rearrange("p (h l) -> p h l", h=H0)

        def by_bank(ap):
            return ap.rearrange("p (c b) l -> p c b l", b=2)

        def spread(e, out, compact, mask):
            shape = [P, compact.shape[1], BT, L]
            return e.tensor_tensor(out.rearrange("p h (b l) -> p h b l", b=BT), compact.unsqueeze(2).to_broadcast(shape),
                                   mask.rearrange("p (b l) -> p b l", b=BT).unsqueeze(1).to_broadcast(shape), ALU.mult)

        def two(f):
            for s in range(2):
                f(s)

        def stage_in(s):
            S.step("act", f"kq{s}", lambda e, i: e.activation(kqs[:, s, :, :], qk[:, :, cols_at(i, s)], ACT.Copy),
                   [f"pe.G{s}<1"])
            S.step("act", f"v{s}", lambda e, i: e.activation(vs[:, s, :, :], F[:, 0:2, cols_at(i, s)], ACT.Copy),
                   [f"pe.vT{s}<1"])
            S.step("pool", f"cm{s}", lambda e, i: e.tensor_tensor(
                cm[:, s, :, :], low, cb[:, tile_at(i, s), :].rearrange("p t h -> p (t h)").unsqueeze(2).to_broadcast([P, H0, L]), ALU.mult),
                [f"dve.A{s}<1"])
        two(stage_in)
        b0 = lambda s: 4 * s

        def grams(s):
            def emit(e, i):
                for h in range(H0):
                    rows = slice(64 * (h % 2), 64 * (h % 2) + 64)
                    for b in range(BT):
                        own = slice(L * b, L * b + L)
                        bank, col = b0(s) + h % 2, L * (h // 2)
                        e.matmul(K.ps[own, bank, col:col + L], kqs[rows, s, 2 + h // 2, own],
                                 kqs[rows, s, 2 + h // 2, own], start=True, stop=True)
                        done = e.matmul(K.ps[own, bank, P + col:P + col + L], kqs[rows, s, 2 + h // 2, own],
                                        kqs[rows, s, h // 2, own], start=True, stop=True)
                return done
            S.step("pe", f"G{s}", emit, [f"act.kq{s}", f"dve.L1{s}<1", f"act.w2{s}<1"])

            def turn_v(e, i):
                for c in range(DC):
                    done = e.transpose(K.ps[:, b0(s) + 3, c * P:(c + 1) * P], vs[:, s, c, :], K.ident[:, :])
                return done
            S.step("pe", f"vT{s}", turn_v, [f"act.v{s}", f"act.oT{s}<1"])
        two(grams)

        def first(s):
            S.step("dve", f"A{s}", lambda e, i: e.tensor_tensor(
                by_bank(Ac[:, s, :, :]), K.ps[:, b0(s):b0(s) + 2, 0:2 * L].rearrange("p b (c l) -> p c b l", c=2),
                by_bank(cm[:, s, :, :]), ALU.mult), [f"pe.G{s}", f"pool.cm{s}"])
            for r in range(2):
                S.step("dve", f"L{r}{s}", lambda e, i, r=r: spread(
                    e, Lbd[:, s, r::2, :], K.ps[:, b0(s) + r, P:P + 2 * L].rearrange("p (c l) -> p c l", c=2), K.upto),
                    [f"pe.o{s}<1"])
            S.step("dve", f"AT{s}", lambda e, i: e.transpose(
                ATc[:, s, :, :].rearrange("p h l -> p (h l)"), Ac[:, s, :, :].rearrange("p h l -> p (h l)")),
                [f"dve.A{s}", f"pool.AT3{s}<1"])
            S.step("dve", f"X0{s}", lambda e, i: e.tensor_tensor(X[:, s, :, :], Ac[:, s, :, :], half, ALU.mult), [f"dve.A{s}"])
            S.step("dve", f"X1{s}", lambda e, i: e.tensor_tensor(X[:, s, :, :], one, X[:, s, :, :], ALU.subtract), [f"dve.X0{s}"])
            for m in range(4):
                S.step("pool", f"AT{m}{s}", lambda e, i, m=m: spread(e, AT[m][:, s, :, :], ATc[:, s, :, :], K.between[m]),
                       [f"dve.AT{s}", f"pe.{'w2' if m == 3 else f'P{m}'}{s}<1"])
        two(first)

        def ys(s, m):
            S.step("dve", f"Y{m}{s}", lambda e, i: e.transpose(
                Y[:, s, :, :].rearrange("p h l -> p (h l)"), X[:, s, :, :].rearrange("p h l -> p (h l)")), [f"dve.X{m + 1}{s}"])
            S.step("dve", f"Yb{m}{s}", lambda e, i: spread(e, Ybd[:, s, :, :], Y[:, s, :, :], K.blocks),
                   [f"dve.Y{m}{s}"] + ([f"pe.w3{s}<1"] if m == 0 else [f"pe.XP{m - 1}{s}"]))
        two(lambda s: ys(s, 0))
        for s in range(2):
            S.step("dve", f"v0{s}", lambda e, i, s=s: e.tensor_tensor(
                v0[:, s, :].rearrange("p (h v) -> p h v", h=H0), K.ps[:, b0(s) + 3, 0:D].rearrange("p (h v) -> p h v", h=H0),
                ab[:, tile_at(i, s), :].rearrange("p t h -> p (t h)").unsqueeze(2).to_broadcast([P, H0, DV0]), ALU.mult),
                [f"pe.vT{s}", f"pe.w1{s}<1"])
        for m in range(3):
            def p1(s, m=m):
                def emit(e, i):
                    for h in range(H0):
                        done = e.matmul(K.ps[:, b0(s) + 1, L * h:L * h + L], AT[m][:, s, h, :], X[:, s, h, :], start=True, stop=True)
                    return done
                S.step("pe", f"P{m}{s}", emit, [f"pool.AT{m}{s}", f"dve.X{m + 1}{s}",
                                                f"act.P{m - 1}{s}" if m else f"dve.L1{s}"])
                S.step("act", f"P{m}{s}", lambda e, i: e.activation(P1[:, s, :, :], heads(K.ps[:, b0(s) + 1, 0:P]), ACT.Copy),
                       [f"pe.P{m}{s}"] + ([f"pe.XP{m - 1}{s}"] if m else [f"pe.XP2{s}<1"]))
            two(p1)

            def xp(s, m=m):
                def emit(e, i):
                    for h in range(H0):
                        done = e.matmul(K.ps[:, b0(s) + 2, L * h:L * h + L], Ybd[:, s, h, :], P1[:, s, h, :], start=True, stop=True)
                    return done
                S.step("pe", f"XP{m}{s}", emit, [f"act.P{m}{s}", f"dve.Yb{m}{s}"] + ([] if m else [f"dve.u{s}<1"]))
                S.step("dve", f"X{m + 2}{s}", lambda e, i: e.tensor_tensor(
                    X[:, s, :, :], X[:, s, :, :], heads(K.ps[:, b0(s) + 2, 0:P]), ALU.subtract), [f"pe.XP{m}{s}"])
                ys(s, m + 1)
            two(xp)

        def apply(name, bank, lhs, rhs, needs):
            def per(s):
                def emit(e, i):
                    for h in range(H0):
                        done = e.matmul(K.ps[:, b0(s) + bank, DV0 * h:DV0 * h + DV0], lhs[:, s, h, :],
                                        rhs[:, s, DV0 * h:DV0 * h + DV0], start=True, stop=True)
                    return done
                S.step("pe", f"{name}{s}", emit, [n.format(s=s) for n in needs])
            two(per)
        apply("w1", 1, Ybd, v0, ["dve.Yb3{s}", "dve.v0{s}", "act.P2{s}"])
        two(lambda s: S.step("act", f"w1{s}", lambda e, i: e.activation(w1[:, s, :], K.ps[:, b0(s) + 1, 0:D], ACT.Copy),
                             [f"pe.w1{s}", f"dve.u{s}<1"]))
        apply("w2", 1, AT[3], w1, ["act.w1{s}", "pool.AT3{s}"])
        two(lambda s: S.step("act", f"w2{s}", lambda e, i: e.activation(w2[:, s, :], K.ps[:, b0(s) + 1, 0:D], ACT.Copy),
                             [f"pe.w2{s}", f"pe.w3{s}<1"]))
        apply("w3", 2, Ybd, w2, ["act.w2{s}", "dve.X4{s}"])
        two(lambda s: S.step("dve", f"u{s}", lambda e, i: e.tensor_tensor(
            u[:, s, :], w1[:, s, :], K.ps[:, b0(s) + 2, 0:D], ALU.subtract), [f"pe.w3{s}", f"pe.o{s}<1"]))
        apply("o", 3, Lbd, u, ["dve.u{s}", "dve.v0{s}", "dve.L1{s}"])

        def rows_out(s):
            S.step("dve", f"o{s}", lambda e, i: e.tensor_tensor(
                od[:, s, :].rearrange("p (h v) -> p h v", h=H0), K.ps[:, b0(s) + 3, 0:D].rearrange("p (h v) -> p h v", h=H0),
                rn[:, tile_at(i, s), 0:4].rearrange("p t h -> p (t h)").unsqueeze(2).to_broadcast([P, H0, DV0]), ALU.mult),
                [f"pe.o{s}", f"pe.oT{s}<1", f"pool.dr{s}<1"])
            S.step("pool", f"dr{s}", lambda e, i: e.tensor_copy(dr[:, tile_at(i, s), :], od[:, s, :].unsqueeze(1)), [f"dve.o{s}"])

            def turn_o(e, i):
                for c in range(DC):
                    done = e.transpose(K.ps[:, b0(s) + 3, c * P:(c + 1) * P], od[:, s, c * P:(c + 1) * P], K.ident[:, :])
                return done
            S.step("pe", f"oT{s}", turn_o, [f"dve.o{s}"])
            S.step("act", f"oT{s}", lambda e, i: e.activation(
                qk[:, 0:2, cols_at(i, s)], K.ps[:, b0(s) + 3, 0:D].rearrange("p (c n) -> p c n", c=DC), ACT.Copy), [f"pe.oT{s}"])
        two(rows_out)
        S.run()


def mixture_gates(K, sb, lg, gates, ltau):
    with ExitStack() as ctx:
        raw, fl, mx, tot = (sb(n, [P, NT, H0], c=ctx) for n in ("raw", "fl", "mx", "tot"))
        tau = sb("tau", [P, H0], c=ctx)
        oth = sb("oth", [P, NT, H0, 3], c=ctx)
        S = Stage(K, "b0_g", 1)
        S.step("act", "sig", lambda e, i: e.activation(raw[:, :, :], lg[:, :, :, 3], ACT.Sigmoid))
        S.step("act", "tau", lambda e, i: e.activation(tau[:, :], ltau[:, :], ACT.Exp))
        S.step("dve", "itau", lambda e, i: e.reciprocal(tau[:, :], tau[:, :]), ["act.tau"])
        S.step("dve", "scl", lambda e, i: e.tensor_tensor(
            oth[:, :, :, :], lg[:, :, :, 0:3], tau[:, :].unsqueeze(1).unsqueeze(3).to_broadcast([P, NT, H0, 3]), ALU.mult), ["dve.itau"])
        S.step("dve", "max", lambda e, i: e.tensor_reduce(mx[:, :, :], oth[:, :, :, :], AX.X, ALU.max), ["dve.scl"])
        S.step("dve", "sub", lambda e, i: e.tensor_tensor(
            oth[:, :, :, :], oth[:, :, :, :], mx[:, :, :].unsqueeze(3).to_broadcast([P, NT, H0, 3]), ALU.subtract), ["dve.max"])
        S.step("act", "exp", lambda e, i: e.activation(oth[:, :, :, :], oth[:, :, :, :], ACT.Exp), ["dve.sub"])
        S.step("dve", "sum", lambda e, i: e.tensor_reduce(tot[:, :, :], oth[:, :, :, :], AX.X, ALU.add), ["act.exp"])
        S.step("dve", "inv", lambda e, i: e.reciprocal(tot[:, :, :], tot[:, :, :]), ["dve.sum"])
        S.step("dve", "floor", lambda e, i: e.tensor_scalar(fl[:, :, :], raw[:, :, :], 0.09, 0.9, ALU.mult, ALU.add), ["act.sig"])
        S.step("dve", "pval", lambda e, i: e.tensor_tensor(raw[:, :, :], raw[:, :, :], fl[:, :, :], ALU.mult), ["dve.floor"])
        S.step("dve", "put", lambda e, i: e.tensor_copy(gates[:, :, :, 3], raw[:, :, :]), ["dve.pval"])
        S.step("dve", "rest", lambda e, i: e.tensor_scalar(fl[:, :, :], raw[:, :, :], -1.0, 1.0, ALU.mult, ALU.add), ["dve.pval"])
        S.step("dve", "scale", lambda e, i: e.tensor_tensor(tot[:, :, :], tot[:, :, :], fl[:, :, :], ALU.mult), ["dve.rest", "dve.inv"])
        S.step("dve", "ctx", lambda e, i: e.tensor_tensor(
            gates[:, :, :, 0:3], oth[:, :, :, :], tot[:, :, :].unsqueeze(3).to_broadcast([P, NT, H0, 3]), ALU.mult), ["dve.scale"])
        S.run()


def delta_mix(K, sb, F, dr, gates, wo, nw):
    with ExitStack() as ctx:
        fs = sb("fs", [P, 2, 6, P], c=ctx)
        pm = sb("pm", [P, 2, 4, D], c=ctx)
        ss = sb("ss", [P, NT, H0], c=ctx)
        sq = sb("sq2", [P, 2, D], c=ctx)
        S = Stage(K, "b0_mx", NT // 2)

        def by_head(ap):
            return ap.rearrange("p (h v) -> p h v", h=H0)

        def gate(i, s, g):
            return gates[:, tile_at(i, s), :, g].rearrange("p t h -> p (t h)").unsqueeze(2).to_broadcast([P, H0, DV0])
        for s in range(2):
            S.step("act", f"fs{s}", lambda e, i, s=s: e.activation(fs[:, s, :, :], F[:, :, cols_at(i, s)], ACT.Copy), [f"pe.T{s}<1"])

            def turns(e, i, s=s):
                for c in range(6):
                    done = e.transpose(K.ps[:, 2 * s + c // 4, (c % 4) * P:(c % 4 + 1) * P], fs[:, s, c, :], K.ident[:, :])
                return done
            S.step("pe", f"T{s}", turns, [f"act.fs{s}", f"dve.p2{s}<1"])
        for s in range(2):
            S.step("pool", f"p3{s}", lambda e, i, s=s: e.tensor_tensor(
                by_head(pm[:, s, 3, :]), dr[:, tile_at(i, s), :].rearrange("p t (h v) -> p (t h) v", h=H0), gate(i, s, 2), ALU.mult),
                [f"dve.a1{s}<1"])
            for n, (col, g) in enumerate(((0, 3), (256, 0), (512, 1))):
                S.step("dve", f"p{n}{s}", lambda e, i, s=s, n=n, col=col, g=g: e.tensor_tensor(
                    by_head(pm[:, s, n, :]), by_head(K.ps[:, 2 * s + col // 512, col % 512:col % 512 + D]), gate(i, s, g), ALU.mult),
                    [f"pe.T{s}", f"dve.a1{s}<1"])
        for s in range(2):
            S.step("dve", f"a0{s}", lambda e, i, s=s: e.tensor_tensor(
                pm[:, s, 0:2, :], pm[:, s, 0:2, :], pm[:, s, 2:4, :], ALU.add), [f"dve.p2{s}", f"pool.p3{s}"])
            S.step("dve", f"a1{s}", lambda e, i, s=s: e.tensor_tensor(
                dr[:, tile_at(i, s), :], pm[:, s, 0:1, :], pm[:, s, 1:2, :], ALU.add), [f"dve.a0{s}"])
            S.step("act", f"sq{s}", lambda e, i, s=s: e.activation(sq[:, s, :].unsqueeze(1), dr[:, tile_at(i, s), :], ACT.Square),
                   [f"dve.a1{s}", f"dve.ss{s}<1"])
            S.step("dve", f"ss{s}", lambda e, i, s=s: e.tensor_reduce(
                ss[:, tile_at(i, s), :].rearrange("p t h -> p (t h)"), by_head(sq[:, s, :]), AX.X, ALU.add), [f"act.sq{s}"])
        S.run()
        S = Stage(K, "b0_rm", 1)
        S.step("dve", "eps", lambda e, i: e.tensor_scalar(ss[:, :, :], ss[:, :, :], 1.0 / DV0, 1e-5, ALU.mult, ALU.add))
        S.step("act", "root", lambda e, i: e.activation(ss[:, :, :], ss[:, :, :], ACT.Sqrt), ["dve.eps"])
        S.step("dve", "inv", lambda e, i: e.reciprocal(ss[:, :, :], ss[:, :, :]), ["act.root"])
        S.run()
        S = Stage(K, "b0_o", NT // 2)
        for s in range(2):
            S.step("dve", f"n{s}", lambda e, i, s=s: e.tensor_tensor(
                by_head(K.xnb[:, s, :]), dr[:, tile_at(i, s), :].rearrange("p t (h v) -> p (t h) v", h=H0),
                ss[:, tile_at(i, s), :].rearrange("p t h -> p (t h)").unsqueeze(2).to_broadcast([P, H0, DV0]), ALU.mult), [f"pe.T{s}<1"])

            def turn_o(e, i, s=s):
                for c in range(DC):
                    done = e.transpose(K.ps[:, s, c * P:(c + 1) * P], K.xnb[:, s, c * P:(c + 1) * P], K.ident[:, :])
                return done
            S.step("pe", f"T{s}", turn_o, [f"dve.n{s}", f"act.T{s}<1"])
            S.step("act", f"T{s}", lambda e, i, s=s: e.activation(
                K.xs[:, s, :, :], K.ps[:, s, 0:D].rearrange("p (c n) -> p c n", c=DC), ACT.Copy, scale=nw[:, 0:1]), [f"pe.T{s}", f"pe.mm{s}<1"])
        for s in range(2):
            def product(e, i, s=s):
                for c in range(DC):
                    done = e.matmul(K.ps[:, 2 + s, 0:D], K.xs[:, s, c, :], wo[:, c, :], start=(c == 0), stop=(c == DC - 1))
                return done
            S.step("pe", f"mm{s}", product, [f"act.T{s}", f"dve.x{s}<1"])
            S.step("dve", f"x{s}", lambda e, i, s=s: e.tensor_tensor(
                K.x[:, tile_at(i, s), :], K.x[:, tile_at(i, s), :], K.ps[:, 2 + s, 0:D].unsqueeze(1), ALU.add), [f"pe.mm{s}"])
        S.run()


def top_ranks(S, prefix, rank, gt, eq, before, p, n, needs):
    T = p.shape[1]
    shape = [P, T, n, n]
    own = p.unsqueeze(3).to_broadcast(shape)
    other = p.unsqueeze(2).to_broadcast(shape)
    S.step("dve", prefix + "gt", lambda e, i: e.tensor_tensor(gt, other, own, ALU.is_gt), needs)
    S.step("dve", prefix + "eq", lambda e, i: e.tensor_tensor(eq, other, own, ALU.is_equal), needs)
    S.step("dve", prefix + "tie", lambda e, i: e.tensor_tensor(
        eq, eq, before.unsqueeze(1).to_broadcast(shape), ALU.mult), ["dve." + prefix + "eq"])
    S.step("dve", prefix + "or", lambda e, i: e.tensor_tensor(gt, gt, eq, ALU.add), ["dve." + prefix + "tie", "dve." + prefix + "gt"])
    S.step("dve", prefix + "rank", lambda e, i: e.tensor_reduce(rank, gt, AX.X, ALU.add), ["dve." + prefix + "or"])


def experts_0(K):
    I = K.ins
    E, FC = 8, 8
    with ExitStack() as ctx:
        def sb(name, shape, dt=F32, c=ctx):
            return K.sb("f0_" + name, shape, dt, c)
        wr = sb("wr", [P, DC, E])
        w1 = sb("w1", [P, 2, DC, FC * P])
        w2 = sb("w2", [P, 2, FC, D])
        rl, rank, gate = (sb(n, [P, NT, E]) for n in ("rl", "rank", "gate"))
        gt, eq = (sb(n, [P, NT, E, E]) for n in ("gt", "eq"))
        mx, tot = (sb(n, [P, NT]) for n in ("mx", "tot"))
        h = sb("h", [P, 2, FC, 512])
        w_r = load(K, "f0_r", [wr[:, :, :]], [features(I["L0_ffn_WrT"])])
        row_stats(K, "f0_ln", K.x, 1e-5, [w_r])
        norm_transpose(K, "f0_nt", row_logits(K, wr, E, rl))

        def over(t):
            return t[:, :].unsqueeze(2).to_broadcast([P, NT, E])
        S = Stage(K, "f0_g", 1)
        S.step("dve", "max", lambda e, i: e.tensor_reduce(mx[:, :], rl[:, :, :], AX.X, ALU.max))
        S.step("dve", "sub", lambda e, i: e.tensor_tensor(rl[:, :, :], rl[:, :, :], over(mx), ALU.subtract), ["dve.max"])
        S.step("act", "exp", lambda e, i: e.activation(rl[:, :, :], rl[:, :, :], ACT.Exp), ["dve.sub"])
        S.step("dve", "sum", lambda e, i: e.tensor_reduce(tot[:, :], rl[:, :, :], AX.X, ALU.add), ["act.exp"])
        S.step("dve", "inv", lambda e, i: e.reciprocal(tot[:, :], tot[:, :]), ["dve.sum"])
        S.step("dve", "p", lambda e, i: e.tensor_tensor(rl[:, :, :], rl[:, :, :], over(tot), ALU.mult), ["dve.inv"])
        top_ranks(S, "e", rank[:, :, :], gt[:, :, :, :], eq[:, :, :, :], K.before[0:P, 0:E, 0:E], rl[:, :, :], E, ["dve.p"])
        S.step("dve", "pick", lambda e, i: e.scalar_tensor_tensor(
            gate[:, :, :], rank[:, :, :], 1.5, rl[:, :, :], ALU.is_lt, ALU.mult), ["dve.erank"])
        S.step("dve", "sum2", lambda e, i: e.tensor_reduce(tot[:, :], gate[:, :, :], AX.X, ALU.add), ["dve.pick"])
        S.step("dve", "inv2", lambda e, i: e.reciprocal(tot[:, :], tot[:, :]), ["dve.sum2"])
        S.step("dve", "gate", lambda e, i: e.tensor_tensor(gate[:, :, :], gate[:, :, :], over(tot), ALU.mult), ["dve.inv2"])
        S.run()

        S = Stage(K, "f0_e", E // 2)
        for s in range(2):
            def loads(e, i, s=s):
                sem = S.dma[f"w{s}"][0]
                e.dma_start(w1[:, s, :, :], I["L0_ffn_W1T"][bass.ds(2 * i + s, 1), :, :].rearrange(
                    "e (c p) f -> p (e c) f", p=P)).then_inc(sem, 16)
                e.dma_start(w2[:, s, :, :], I["L0_ffn_W2T"][bass.ds(2 * i + s, 1), :, :].rearrange(
                    "e (c p) d -> p (e c) d", p=P)).then_inc(sem, 16)
            S.step("sp", f"w{s}", loads, [f"pe.y{4 * s + 3}_1<1"], dmas=2)
        jobs = [(s, g) for s in range(2) for g in range(NG)]

        def hidden(n):
            s, g = jobs[n]
            for f in range(FC):
                def product(e, i, f=f):
                    for c in range(DC):
                        done = e.matmul(K.ps[:, f % 4, :], w1[:, s, c, f * P:(f + 1) * P], K.xnT[:, c, g * 512:(g + 1) * 512],
                                        start=(c == 0), stop=(c == DC - 1))
                    return done
                free = f"act.h{n}_{f - 4}" if f >= 4 else f"act.h{n - 1}_{f + 4}" if n else f"act.h{len(jobs) - 1}_{f + 4}<1"
                S.step("pe", f"h{n}_{f}", product, [free, f"sp.w{s}"])
                S.step("act", f"h{n}_{f}", lambda e, i, f=f: e.activation(h[:, n % 2, f, :], K.ps[:, f % 4, :], ACT.Silu),
                       [f"pe.h{n}_{f}", f"pe.y{n - 2}_1" if n >= 2 else f"pe.y{n + 6}_1<1"])

        def outputs(n):
            s, g = jobs[n]
            for half in range(2):
                bank = 4 + 2 * (n % 2) + half

                def product(e, i, half=half, bank=bank):
                    for t in range(2):
                        for f in range(FC):
                            at = (2 * half + t) * P
                            done = e.matmul(K.ps[:, bank, t * D:(t + 1) * D], h[:, n % 2, f, at:at + P], w2[:, s, f, :],
                                            start=(f == 0), stop=(f == FC - 1))
                    return done
                S.step("pe", f"y{n}_{half}", product, [f"act.h{n}_7", f"dve.y{n - 2}_{half}" if n >= 2 else f"dve.y{n + 6}_{half}<1"])

                def add(e, i, half=half, bank=bank):
                    for t in range(2):
                        row = 4 * g + 2 * half + t
                        done = e.scalar_tensor_tensor(K.x[:, row, :], K.ps[:, bank, t * D:(t + 1) * D],
                                                      gate[:, row, bass.ds(2 * i + s, 1)], K.x[:, row, :], ALU.mult, ALU.add)
                    return done
                S.step("dve", f"y{n}_{half}", add, [f"pe.y{n}_{half}"])
        hidden(0)
        for n in range(len(jobs)):
            if n + 1 < len(jobs):
                hidden(n + 1)
            outputs(n)
        S.run()


def cross_attention_1(K):
    I = K.ins
    HG = 4
    with ExitStack() as ctx:
        def sb(name, shape, dt=F32, c=ctx):
            return K.sb("a1_" + name, shape, dt, c)
        wq, wk, wv, wo = (sb(n, [P, DC, D]) for n in ("wq", "wk", "wv", "wo"))
        bq, bk, bv = (sb(n, [P, DC]) for n in ("bq", "bk", "bv"))
        bo = sb("bo", [P, D])
        qT = sb("qT", [P, DC, ROWS])
        ctxT = sb("ctxT", [P, 2, DC, NK])
        qb = sb("qb", [P, 2, DC, 8, L])
        kT = sb("kT", [P, 2, DC, NK])
        v = sb("v", [P, 2, 2, D])
        vL = sb("vL", [1, 2, D])
        pr = sb("pr", [P, 2, HG, NK])
        prT = sb("prT", [P, 2, 2, HG, P])
        prL = sb("prL", [1, 2, HG, P])
        neg, tot, inv = (sb(n, [P, 2, HG]) for n in ("neg", "tot", "inv"))
        mr = sb("mr", [P, 2, HG, 64])
        mo = sb("mo", [P, 2, HG, 64])
        w_a = load(K, "a1", [wq[:, :, :], wk[:, :, :], wv[:, :, :], wo[:, :, :], bq[:, :], bk[:, :], bv[:, :], bo[:, :]],
                   [features(I["L1_xattn_" + n + "T"]) for n in ("Wq", "Wk", "Wv", "Wo")]
                   + [I["L1_xattn_" + n] for n in ("bq", "bk", "bv")] + [I["L1_xattn_bo"].partition_broadcast(P)])
        row_stats(K, "a1_ln", K.x, 1e-5, [w_a])
        norm_transpose(K, "a1_nt")

        def q_finish(m):
            return "dve", lambda e, i, ps, m=m: e.tensor_scalar(
                qT[:, m, bass.ds(i * 512, 512)], ps, bq[:, m:m + 1], 0.25, ALU.add, ALU.mult)
        feature_gemm(K, "a1_q", qT, wq, rows_of(K.xnT), DC, DC, q_finish, [w_a])

        S = Stage(K, "a1_at", B // 2)

        def cols(i, s):
            return bass.ds((2 * i + s) * L, L)

        def front(s):
            S.step("sp", f"ctx{s}", lambda e, i: e.dma_start(
                ctxT[:, s, :, :], I["ctxT"][bass.ds(2 * i + s, 1), :, :].rearrange("b (c p) k -> p (b c) k", p=P)).then_inc(
                    S.dma[f"ctx{s}"][0], 16), [f"pe.V{s}<1"], dmas=1)
            for c in range(DC):
                S.step("pool", f"q{c}{s}", lambda e, i, c=c: e.tensor_tensor(
                    qb[:, s, c, :, :], qT[:, c, cols(i, s)].unsqueeze(1).to_broadcast([P, 8, L]),
                    K.head16.unsqueeze(2).to_broadcast([P, 8, L]), ALU.mult), [f"pe.S{s}<1"])

        def keys(s):
            def emit(e, i):
                for m in range(DC):
                    for c in range(DC):
                        done = e.matmul(K.ps[:, 4 + m, 0:NK], wk[:, c, m * P:(m + 1) * P], ctxT[:, s, c, :],
                                        start=(c == 0), stop=(c == DC - 1))
                return done
            S.step("pe", f"K{s}", emit, [f"sp.ctx{s}", "dve.T0<1" if s == 0 else "dve.T1", "act.T0<1" if s == 0 else "act.T1"])
            for c in range(DC):
                S.step("act", f"K{c}{s}", lambda e, i, c=c: e.activation(
                    kT[:, s, c, :], K.ps[:, 4 + c, 0:NK], ACT.Identity, bias=bk[:, c:c + 1]), [f"pe.K{s}", f"pe.S{s}<1"])

        def values(s):
            def emit(e, i):
                for t in range(2):
                    for c in range(DC):
                        e.matmul(K.ps[:, 6, t * D:(t + 1) * D], ctxT[:, s, c, t * P:(t + 1) * P], wv[:, c, :],
                                 start=(c == 0), stop=(c == DC - 1))
                for c in range(DC):
                    done = e.matmul(K.ps[0:1, 7, 0:D], ctxT[:, s, c, 2 * P:NK], wv[:, c, :], start=(c == 0), stop=(c == DC - 1))
                return done
            S.step("pe", f"V{s}", emit, ["dve.L0<1" if s == 0 else "dve.L1", "act.O0" if s == 0 else "act.O1"])
            S.step("dve", f"V{s}", lambda e, i: e.tensor_copy(
                v[:, s, :, :], K.ps[:, 6, :].rearrange("p (t d) -> p t d", t=2)),
                [f"pe.V{s}", "pe.P0<1" if s == 0 else "pe.P1"])
            S.step("dve", f"VL{s}", lambda e, i: e.tensor_copy(vL[:, s, :], K.ps[0:1, 7, 0:D]), [f"pe.V{s}"])

        def scores(s):
            def emit(e, i):
                for g in range(HG):
                    done = e.matmul(K.ps[:, g, 0:NK], qb[:, s, g // 2, 4 * (g % 2):4 * (g % 2) + 4, :].rearrange("p h q -> p (h q)"),
                                    kT[:, s, g // 2, :], start=True, stop=True)
                return done
            S.step("pe", f"S{s}", emit, [f"pool.q1{s}", f"act.K1{s}", "act.e3_1<1" if s == 0 else "act.e3_0"])
            S.step("dve", f"mx{s}", lambda e, i: e.tensor_reduce(neg[:, s, :], K.ps[:, 0:HG, 0:NK], AX.X, ALU.max, negate=True),
                   [f"pe.S{s}", f"act.e3_{s}<1"])
            for g in range(HG):
                S.step("act", f"e{g}_{s}", lambda e, i, g=g: e.activation(
                    pr[:, s, g, :], K.ps[:, g, 0:NK], ACT.Exp, bias=neg[:, s, g:g + 1], accum_out=tot[:, s, g:g + 1]),
                    [f"dve.mx{s}", f"dve.inv{s}<1"] + ([f"pe.T{s}<1"] if s == 0 else ["pe.T1"]))
            S.step("dve", f"inv{s}", lambda e, i: e.reciprocal(inv[:, s, :], tot[:, s, :]), [f"act.e3_{s}", f"pool.mr{s}<1"])
            S.step("pool", f"mr{s}", lambda e, i: e.tensor_tensor(
                mr[:, s, :, :], K.diag16.unsqueeze(1).to_broadcast([P, HG, 64]), inv[:, s, :].unsqueeze(2).to_broadcast([P, HG, 64]),
                ALU.mult), [f"dve.inv{s}", "dve.M0<1" if s == 0 else "dve.M1"])

        def turn_probs(s, late):
            now = "<1" if late else ""
            def emit(e, i):
                for t in range(2):
                    for g in range(HG):
                        e.transpose(K.ps[:, 4 + t, g * P:(g + 1) * P], pr[:, s, g, t * P:(t + 1) * P], K.ident[:, :])
                for g in range(HG):
                    done = e.transpose(K.ps[0:1, 6, g * P:(g + 1) * P], pr[:, s, g, 2 * P:NK], K.ident[:, :])
                return done
            S.step("pe", f"T{s}", emit, [f"act.e3_{s}{now}", f"act.K1{1 - s}", f"dve.V{1 - s}"], late=late)
            S.step("dve", f"T{s}", lambda e, i: e.tensor_copy(
                prT[:, s, 0, :, :], K.ps[:, 4, :].rearrange("p (g n) -> p g n", g=HG)), [f"pe.T{s}", f"pe.P{s}<1"], late=late)
            S.step("act", f"T{s}", lambda e, i: e.activation(
                prT[:, s, 1, :, :], K.ps[:, 5, :].rearrange("p (g n) -> p g n", g=HG), ACT.Copy), [f"pe.T{s}", f"pe.P{s}<1"], late=late)
            S.step("dve", f"L{s}", lambda e, i: e.tensor_copy(
                prL[:, s, :, :], K.ps[0:1, 6, :].rearrange("p (g n) -> p g n", g=HG)), [f"pe.T{s}"], late=late)

        def weigh(s, late):
            def emit(e, i):
                for g in range(HG):
                    out = K.ps[:, 7, D + 64 * g:D + 64 * g + 64]
                    own = slice(64 * g, 64 * g + 64)
                    e.matmul(out, prT[:, s, 0, g, :], v[:, s, 0, own], start=True, stop=False)
                    e.matmul(out, prT[:, s, 1, g, :], v[:, s, 1, own], start=False, stop=False)
                    done = e.matmul(out, prL[:, s, g, :], vL[:, s, own], start=False, stop=True)
                return done
            S.step("pe", f"P{s}", emit, [f"dve.L{s}", f"act.T{s}", f"dve.VL{1 - s}"], late=late)
            S.step("dve", f"M{s}", lambda e, i: e.tensor_tensor(
                mo[:, s, :, :], K.ps[:, 7, D:2 * D].rearrange("p (g n) -> p g n", g=HG), mr[:, s, :, :], ALU.mult),
                [f"pe.P{s}", f"pool.mr{s}{'<1' if late else ''}", "pe.O0" if s == 0 else "pe.O1<1"], late=late)

        def outputs(s):
            def emit(e, i):
                for g in range(HG):
                    half = slice(64 * (g % 2), 64 * (g % 2) + 64)
                    done = e.matmul(K.ps[half, 7, L * (g // 2):L * (g // 2) + L], mo[:, s, g, :], K.eye, start=True, stop=True)
                return done
            S.step("pe", f"O{s}", emit, ["dve.M0<1" if s == 0 else "dve.M1"], late=True)

            def bias(e, i):
                for c in range(DC):
                    done = e.activation(qT[:, c, cols(i, s)], K.ps[:, 7, L * c:L * c + L], ACT.Identity, bias=bv[:, c:c + 1])
                return done
            S.step("act", f"O{s}", bias, [f"pe.O{s}"], late=True)
        front(0)
        front(1)
        keys(0)
        outputs(0)
        values(0)
        turn_probs(1, True)
        scores(0)
        weigh(1, True)
        keys(1)
        outputs(1)
        values(1)
        turn_probs(0, False)
        scores(1)
        weigh(0, False)
        S.run()

        def add_bo(S):
            for s in range(2):
                S.step("pool", f"bo{s}", lambda e, i, s=s: e.tensor_tensor(
                    K.x[:, tile_at(i, s), :], K.x[:, tile_at(i, s), :], bo[:, :].unsqueeze(1), ALU.add))
        output_rows(K, "a1_o", qT, wo, DC, lambda e, t, ps: e.tensor_tensor(
            K.x[:, t, :], K.x[:, t, :], ps.unsqueeze(1), ALU.add), pre=add_bo, after="pool.bo{s}")


def self_attention(K):
    I = K.ins
    HQ, HT, W = 16, 20, 64
    with ExitStack() as ctx:
        def sb(name, shape, dt=F32, c=ctx):
            return K.sb("s_" + name, shape, dt, c)
        w = sb("w", [P, DC, 3 * 512])
        wo = sb("wo", [P, 8, D])
        rope = sb("rope", [P, 2, W])
        nw = sb("nw", [P, 2, W])
        cw, sw = (sb(n, [P, HT, W]) for n in ("cw", "sw"))
        qkT = sb("qkT", [P, 10, ROWS])
        vr = sb("vr", [P, NT, D])
        w_a = load(K, "s_w", [w[:, :, :], rope[:, :, :], nw[:, 0, :], nw[:, 1, :]],
                   [features(I["L1_attn_WqkvT"]), I["rope"], I["L1_attn_q_norm_w"].partition_broadcast(P),
                    I["L1_attn_k_norm_w"].partition_broadcast(P)])
        w_o = load(K, "s_wo", [wo[:, :, :]], [features(I["L1_attn_WoT"])])
        row_stats(K, "s_ln", K.x, 1e-5, [w_a])
        norm_transpose(K, "s_nt")

        S = Stage(K, "s_tab", 1)
        for n, (lo, hi) in enumerate(((0, HQ), (HQ, HT))):
            heads = [P, hi - lo, W]
            S.step("dve", f"c{n}", lambda e, i, n=n, lo=lo, hi=hi, heads=heads: e.tensor_tensor(
                cw[:, lo:hi, :], rope[:, 0:1, :].to_broadcast(heads), nw[:, n:n + 1, :].to_broadcast(heads), ALU.mult))
            for h in range(2):
                a, b = slice(32 * h, 32 * h + 32), slice(32 - 32 * h, 64 - 32 * h)
                part = [P, hi - lo, 32]
                S.step("dve", f"s{n}{h}", lambda e, i, n=n, lo=lo, hi=hi, a=a, b=b, part=part: e.tensor_tensor(
                    sw[:, lo:hi, a], rope[:, 1:2, a].to_broadcast(part), nw[:, n:n + 1, b].to_broadcast(part), ALU.mult))
        S.run()

        with ExitStack() as c1:
            sq = sb("sq", [P, HT * W], c=c1)
            ta, tb, tr = (sb(n, [P, HT, W], c=c1) for n in ("ta", "tb", "tr"))
            ss = sb("ss", [P, 2, HT], c=c1)
            S = Stage(K, "s_qk", NT // 2)
            S.before("pe", lambda e: None, [w_a])
            half = [slice(0, 32), slice(32, 64)]
            qk = K.ps[:, 0:3, :].rearrange("p b n -> p (b n)")[:, 0:HT * W].rearrange("p (h n) -> p h n", n=W)
            for s in range(2):
                o = 1 - s
                was = "<1" if s == 0 else ""
                S.step("act", f"st{s}", lambda e, i, s=s: e.activation(
                    K.stage[:, s, 0:DC, :], K.xnT[:, :, cols_at(i, s)], ACT.Copy), [f"pe.mm{s}<1"])

                def project(e, i, s=s):
                    for n in range(3):
                        for c in range(DC):
                            done = e.matmul(K.ps[:, n, :], K.stage[:, s, c, :], w[:, c, n * 512:(n + 1) * 512],
                                            start=(c == 0), stop=(c == DC - 1))
                    return done
                S.step("pe", f"mm{s}", project, [f"act.st{s}", f"dve.r1{o}{was}", f"act.v{o}{was}", f"act.sq{o}{was}"])
                S.step("act", f"sq{s}", lambda e, i, s=s: e.activation(
                    sq[:, :].rearrange("p (h n) -> p h n", n=W), qk, ACT.Square), [f"pe.mm{s}", f"dve.ss{o}{was}"])
                S.step("act", f"v{s}", lambda e, i, s=s: e.activation(
                    vr[:, tile_at(i, s), :], K.ps[:, 2, D:2 * D].unsqueeze(1), ACT.Copy), [f"pe.mm{s}"])
                S.step("dve", f"c{s}", lambda e, i, s=s: e.tensor_tensor(ta[:, :, :], qk, cw[:, :, :], ALU.mult),
                       [f"act.v{s}", f"pool.ad{o}{was}"])
                for h in range(2):
                    S.step("dve", f"r{h}{s}", lambda e, i, h=h: e.tensor_tensor(
                        tb[:, :, half[h]], qk[:, :, half[1 - h]], sw[:, :, half[h]], ALU.mult), [f"act.v{s}", f"pool.ad{o}{was}"])
                S.step("dve", f"ss{s}", lambda e, i, s=s: e.tensor_reduce(
                    ss[:, s, :], sq[:, :].rearrange("p (h n) -> p h n", n=W), AX.X, ALU.add), [f"act.sq{s}", f"dve.n{s}<1"])
                S.step("dve", f"ep{s}", lambda e, i, s=s: e.tensor_scalar(
                    ss[:, s, :], ss[:, s, :], 1.0 / W, 1e-6, ALU.mult, ALU.add), [f"dve.ss{s}"])
                S.step("act", f"rt{s}", lambda e, i, s=s: e.activation(ss[:, s, :], ss[:, s, :], ACT.Sqrt), [f"dve.ep{s}"])
                S.step("pool", f"ad{s}", lambda e, i, s=s: e.tensor_tensor(tr[:, :, :], ta[:, :, :], tb[:, :, :], ALU.add),
                       [f"dve.r1{s}", f"pe.T{o}{was}"])
                S.step("dve", f"iv{s}", lambda e, i, s=s: e.reciprocal(ss[:, s, :], ss[:, s, :]), [f"act.rt{s}"])
                S.step("dve", f"n{s}", lambda e, i, s=s: e.tensor_tensor(
                    tr[:, :, :], tr[:, :, :], ss[:, s, :].unsqueeze(2).to_broadcast([P, HT, W]), ALU.mult), [f"dve.iv{s}", f"pool.ad{s}"])

                def turns(e, i, s=s):
                    for c in range(10):
                        done = e.transpose(K.ps[:, 3 + c // 4, (c % 4) * P:(c % 4 + 1) * P],
                                           tr[:, 2 * c:2 * c + 2, :].rearrange("p h n -> p (h n)"), K.ident[:, :])
                    return done
                S.step("pe", f"T{s}", turns, [f"dve.n{s}", f"act.T{o}{was}"])
                S.step("act", f"T{s}", lambda e, i, s=s: e.activation(
                    qkT[:, :, cols_at(i, s)], K.ps[:, 3:6, :].rearrange("p b n -> p (b n)")[:, 0:10 * P].rearrange(
                        "p (c n) -> p c n", n=P), ACT.Copy), [f"pe.T{s}"])
            S.run()

        qs = sb("qs", [P, 2, 10, P])
        vs = sb("vs", [P, 2, D])
        sc, pt, pn = (sb(n, [P, 2, 2, 8, L]) for n in ("sc", "pt", "pn"))
        mx, tot = (sb(n, [P, 2, 2, 8]) for n in ("mx", "tot"))
        oT = K.stage
        S = Stage(K, "s_at", NT // 2)
        S.before("pe", lambda e: None, [w_o])

        def both(f):
            for s in range(2):
                f(s)

        def stage_in(s):
            S.step("act", f"q{s}", lambda e, i: e.activation(qs[:, s, :, :], qkT[:, :, cols_at(i, s)], ACT.Copy), [f"pe.S{s}<1"])
            S.step("pool", f"v{s}", lambda e, i: e.tensor_copy(vs[:, s, :].unsqueeze(1), vr[:, tile_at(i, s), :]), [f"pe.O{s}<1"])

            def scores(e, i):
                for c in range(8):
                    for r in range(2):
                        rows = slice(W * r, W * r + W)
                        for b in range(BT):
                            own = slice(L * b, L * b + L)
                            done = e.matmul(K.ps[own, 2 * s + r, L * c:L * c + L], qs[rows, s, c, own],
                                            qs[rows, s, 8 + c // 4, own], start=True, stop=True)
                return done
            S.step("pe", f"S{s}", scores, [f"act.q{s}", f"dve.x{s}<1"])
        both(stage_in)

        def softmax(s):
            view = K.ps[:, 2 * s:2 * s + 2, 0:256].rearrange("p r (c k) -> p r c k", k=L)
            shape = [P, 2, 8, L]

            def flat(t):
                return t[:, s, :, :, :].rearrange("p r c k -> p (r c) k")

            def each(t):
                return t[:, s, :, :].rearrange("p r c -> p (r c)").unsqueeze(2).to_broadcast([P, 16, L])
            S.step("dve", f"mx{s}", lambda e, i: e.tensor_reduce(mx[:, s, :, :], view, AX.X, ALU.max), [f"pe.S{s}"])
            S.step("dve", f"sb{s}", lambda e, i: e.tensor_tensor(
                sc[:, s, :, :, :], view, mx[:, s, :, :].unsqueeze(3).to_broadcast(shape), ALU.subtract), [f"dve.mx{s}", f"pool.pn{s}<1"])
            S.step("act", f"ex{s}", lambda e, i: e.activation(flat(sc), flat(sc), ACT.Exp), [f"dve.sb{s}"])
            S.step("dve", f"su{s}", lambda e, i: e.tensor_reduce(
                tot[:, s, :, :].rearrange("p r c -> p (r c)"), flat(sc), AX.X, ALU.add), [f"act.ex{s}"])
            S.step("dve", f"iv{s}", lambda e, i: e.reciprocal(tot[:, s, :, :], tot[:, s, :, :]), [f"dve.su{s}"])
            S.step("pool", f"pn{s}", lambda e, i: e.tensor_tensor(flat(pn), flat(sc), each(tot), ALU.mult),
                   [f"dve.iv{s}", f"dve.pt{s}<1"])
            S.step("dve", f"pt{s}", lambda e, i: e.transpose(
                pt[:, s, :, :, :].rearrange("p r c k -> p (r c k)"), pn[:, s, :, :, :].rearrange("p r c k -> p (r c k)")),
                [f"pool.pn{s}", f"pe.O{s}<1"])
        both(softmax)

        def mix(s):
            was, o = ("<1" if s == 0 else ""), 1 - s

            def weigh(e, i):
                for g in range(2):
                    for r in range(2):
                        for b in range(BT):
                            rows = slice(L * b, L * b + L)
                            done = e.matmul(K.ps[W * r:W * r + W, 4 + b, P * g:P * g + P], vs[rows, s, (2 * g + r) * W:(2 * g + r + 1) * W],
                                            pt[rows, s, r, 4 * g:4 * g + 4, :].rearrange("p c q -> p (c q)"), start=True, stop=True)
                return done
            S.step("pe", f"O{s}", weigh, [f"dve.pt{s}", f"pool.v{s}", f"act.o{o}{was}", f"dve.o{o}{was}"])
            for n, (key, lo) in enumerate((("act", 0), ("dve", 2))):
                S.step(key, f"o{s}", lambda e, i, lo=lo: copy(
                    e, oT[:, s, :, :].rearrange("p c (b q) -> p c b q", b=BT)[:, :, lo:lo + 2, :],
                    K.ps[:, 4 + lo:6 + lo, 0:256].rearrange("p b (c q) -> p c b q", q=L)), [f"pe.O{s}", f"pe.W{s}<1"])
        both(mix)

        def project(s):
            def emit(e, i):
                for c in range(8):
                    done = e.matmul(K.ps[:, 2 * s, D:2 * D], oT[:, s, c, :], wo[:, c, :], start=(c == 0), stop=(c == 7))
                return done
            S.step("pe", f"W{s}", emit, [f"act.o{s}", f"dve.o{s}", f"dve.sb{s}"])
            S.step("dve", f"x{s}", lambda e, i: e.tensor_tensor(
                K.x[:, tile_at(i, s), :], K.x[:, tile_at(i, s), :], K.ps[:, 2 * s, D:2 * D].unsqueeze(1), ALU.add), [f"pe.W{s}"])
        both(project)
        S.run()


def experts_1(K):
    I = K.ins
    E, G, EA = 16, 4, 20
    with ExitStack() as ctx:
        def sb(name, shape, dt=F32, c=ctx):
            return K.sb("g_" + name, shape, dt, c)
        wr = sb("wr", [P, DC, E])
        bias = sb("bias", [P, E])
        w1 = sb("w1", [P, 2, DC, P])
        w2 = sb("w2", [P, 2, D])
        s_, sc, rank = (sb(n, [P, NT, E]) for n in ("s", "sc", "rank"))
        gate = sb("gate", [P, NT, EA])
        gt, eq = (sb(n, [P, NT * E * E]) for n in ("gt", "eq"))
        gs, gr = (sb(n, [P, NT, G]) for n in ("gs", "gr"))
        tot = sb("tot", [P, NT])
        r = sb("r", [P, 2, 512])
        h = sb("h", [P, 2, 512])
        w_r = load(K, "g_r", [wr[:, :, :], bias[:, :]], [features(I["L1_ffn_gate_wT"]), I["L1_ffn_bias_e"].partition_broadcast(P)])
        row_stats(K, "g_ln", K.x, 1e-5, [w_r])
        norm_transpose(K, "g_nt", row_logits(K, wr, E, s_))

        def grouped(t):
            return t[:, :, :].rearrange("p t (g e) -> p (t g) e", g=G)

        def square(t, a, n):
            return t[:, 0:a * n * n].rearrange("p (a n m) -> p a n m", n=n, m=n)
        S = Stage(K, "g_g", 1)
        S.step("act", "sig", lambda e, i: e.activation(s_[:, :, :], s_[:, :, :], ACT.Sigmoid))
        S.step("dve", "sc", lambda e, i: e.tensor_tensor(
            sc[:, :, :], s_[:, :, :], bias[:, :].unsqueeze(1).to_broadcast([P, NT, E]), ALU.add), ["act.sig"])
        top_ranks(S, "a", grouped(rank), square(gt, NT * G, 4), square(eq, NT * G, 4), K.before[:, 0:4, 0:4], grouped(sc), 4, ["dve.sc"])
        S.step("dve", "two", lambda e, i: e.scalar_tensor_tensor(
            rank[:, :, :], rank[:, :, :], 1.5, sc[:, :, :], ALU.is_lt, ALU.mult), ["dve.arank"])
        S.step("dve", "gs", lambda e, i: e.tensor_reduce(
            gs[:, :, :].rearrange("p t g -> p (t g)"), grouped(rank), AX.X, ALU.add), ["dve.two"])
        top_ranks(S, "b", gr[:, :, :], square(gt, NT, G), square(eq, NT, G), K.before[:, 0:G, 0:G], gs[:, :, :], G, ["dve.gs"])
        S.step("dve", "in", lambda e, i: e.tensor_scalar(gr[:, :, :], gr[:, :, :], 1.5, None, ALU.is_lt), ["dve.brank"])
        S.step("dve", "msk", lambda e, i: e.tensor_tensor(
            grouped(sc), grouped(sc), gr[:, :, :].rearrange("p t g -> p (t g)").unsqueeze(2).to_broadcast([P, NT * G, 4]), ALU.mult), ["dve.in"])
        top_ranks(S, "c", rank[:, :, :], square(gt, NT, E), square(eq, NT, E), K.before[:, :, :], sc[:, :, :], E, ["dve.msk"])
        S.step("dve", "pick", lambda e, i: e.scalar_tensor_tensor(
            rank[:, :, :], rank[:, :, :], 3.5, s_[:, :, :], ALU.is_lt, ALU.mult), ["dve.crank"])
        S.step("dve", "sum", lambda e, i: e.tensor_reduce(tot[:, :], rank[:, :, :], AX.X, ALU.add), ["dve.pick"])
        S.step("dve", "eps", lambda e, i: e.tensor_scalar(tot[:, :], tot[:, :], 1e-20, None, ALU.add), ["dve.sum"])
        S.step("dve", "inv", lambda e, i: e.reciprocal(tot[:, :], tot[:, :]), ["dve.eps"])
        S.step("dve", "x25", lambda e, i: e.tensor_scalar(tot[:, :], tot[:, :], 2.5, None, ALU.mult), ["dve.inv"])
        S.step("dve", "gate", lambda e, i: e.tensor_tensor(
            gate[:, :, 0:E], rank[:, :, :], tot[:, :].unsqueeze(2).to_broadcast([P, NT, E]), ALU.mult), ["dve.x25"])
        S.step("dve", "one", lambda e, i: e.memset(gate[:, :, E:EA], 1.0))
        S.run()

        S = Stage(K, "g_e", EA // 2)
        for s in range(2):
            def loads(e, i, s=s):
                sem = S.dma[f"w{s}"][0]
                e.dma_start(w1[:, s, :, :], I["L1_ffn_upT"][bass.ds(2 * i + s, 1), :, :].rearrange(
                    "e (c p) f -> p (e c) f", p=P)).then_inc(sem, 16)
                e.dma_start(w2[:, s, :].unsqueeze(1), I["L1_ffn_downT"][bass.ds(2 * i + s, 1), :, :].rearrange(
                    "e p d -> p e d")).then_inc(sem, 16)
            S.step("sp", f"w{s}", loads, [f"pe.y{4 * s + 3}_1<1"], dmas=2)
        jobs = [(s, g) for s in range(2) for g in range(NG)]

        def hidden(n):
            s, g = jobs[n]

            def product(e, i):
                for c in range(DC):
                    done = e.matmul(K.ps[:, n % 2, :], w1[:, s, c, :], K.xnT[:, c, g * 512:(g + 1) * 512], start=(c == 0), stop=(c == DC - 1))
                return done
            S.step("pe", f"h{n}", product, [f"act.r{n - 2}" if n >= 2 else f"act.r{n + 6}<1", f"sp.w{s}"])
            S.step("act", f"r{n}", lambda e, i: e.activation(r[:, n % 2, :], K.ps[:, n % 2, :], ACT.Relu),
                   [f"pe.h{n}"])
            S.step("act", f"h{n}", lambda e, i: e.activation(h[:, n % 2, :], r[:, n % 2, :], ACT.Square),
                   [f"act.r{n}", f"pe.y{n - 2}_1" if n >= 2 else f"pe.y{n + 6}_1<1"])

        def outputs(n):
            s, g = jobs[n]
            for half in range(2):
                bank = 4 + 2 * (n % 2) + half

                def product(e, i, half=half, bank=bank):
                    for t in range(2):
                        at = (2 * half + t) * P
                        done = e.matmul(K.ps[:, bank, t * D:(t + 1) * D], h[:, n % 2, at:at + P], w2[:, s, :], start=True, stop=True)
                    return done
                S.step("pe", f"y{n}_{half}", product, [f"act.h{n}", f"dve.y{n - 2}_{half}" if n >= 2 else f"dve.y{n + 6}_{half}<1"])

                def add(e, i, half=half, bank=bank):
                    for t in range(2):
                        row = 4 * g + 2 * half + t
                        done = e.scalar_tensor_tensor(K.x[:, row, :], K.ps[:, bank, t * D:(t + 1) * D],
                                                      gate[:, row, bass.ds(2 * i + s, 1)], K.x[:, row, :], ALU.mult, ALU.add)
                    return done
                S.step("dve", f"y{n}_{half}", add, [f"pe.y{n}_{half}"])
        hidden(0)
        for n in range(len(jobs)):
            if n + 1 < len(jobs):
                hidden(n + 1)
            outputs(n)
        S.run()


LAYERS = [cross_attention_0, delta_attention, experts_0, cross_attention_1, self_attention, experts_1]


def program(nc, ins, out):
    with ExitStack() as ctx:
        K = Kern(nc, ctx, ins, out)
        K.pending = []
        K.count = {e: K.sem("count_" + e) for e in ENGINES}
        K.gate = {e: K.sem("gate_" + e) for e in ENGINES}
        K.base = {e: 0 for e in ENGINES}
        K.x = K.sb("x", [P, NT, D])
        K.xnT = K.sb("xnT", [P, DC, ROWS])
        K.xnb = K.sb("xnb", [P, 2, D])
        K.xs = K.sb("xs", [P, 2, DC, P])
        K.stage = K.sb("stage", [P, 2, 8, P])
        K.bn = K.sb("bn", [P, NT, 6])
        K.mv = K.sb("mv", [P, NT, 2])
        K.std = K.sb("std", [P, NT])
        K.rstd = K.sb("rstd", [P, NT])
        K.ident = K.sb("ident", [P, P])
        K.masks = K.sb("masks", [P, MASK_COLS])
        K.before = K.sb("before", [P, 16, 16])
        at = MASK_AT
        K.low, K.eye, K.half, K.blocks, K.upto, K.headsel = (
            K.masks[:, at[n][0]:at[n][1]] for n in ("low", "eye", "half", "blocks", "upto", "headsel"))
        K.head16, K.diag16 = (K.masks[:, at[n][0]:at[n][1]] for n in ("head16", "diag16"))
        K.between = [K.masks[:, at[n][0]:at[n][1]] for n in ("between2", "between4", "between8", "between16")]
        K.ps = ctx.enter_context(nc.psum_tensor("ps", [P, 8, 512], F32))
        constants(K)
        for layer in LAYERS:
            layer(K)
        store(K)


def shape_masks():
    r, c = np.arange(P) % L, np.arange(L)
    b, bb, cc = np.arange(P)[:, None] // L, np.arange(P)[None, :] // L, np.arange(P)[None, :] % L
    i = r[:, None]
    parts = {
        "low": c[None, :] < i,
        "eye": c[None, :] == i,
        "half": (i % 2 == 1) & (c[None, :] == i - 1),
        "blocks": b == bb,
        "upto": (b == bb) & (i <= cc),
        "headsel": np.arange(P)[:, None] // 64 == np.arange(2)[None, :],
    }
    parts["head16"] = np.arange(P)[:, None] // 16 == np.arange(8)[None, :]
    parts["diag16"] = b == np.arange(64)[None, :] // 16
    for m in (2, 4, 8, 16):
        parts[f"between{m}"] = (b == bb) & (i // (2 * m) == cc // (2 * m)) & (i % (2 * m) < m) & (cc % (2 * m) >= m)
    at, n = {}, 0
    for k, v in parts.items():
        at[k] = (n, n + v.shape[1])
        n += v.shape[1]
    return np.concatenate([v.astype(np.float32) for v in parts.values()], axis=1), at, n


MASKS, MASK_AT, MASK_COLS = shape_masks()


def rope_rows():
    inv = np.float32(1.0) / np.float32(10000.0) ** (np.arange(0, 64, 2, dtype=np.float32) / np.float32(64))
    angle = (np.arange(L - 1, dtype=np.float32)[:, None] * inv[None, :].astype(np.float32)).astype(np.float32)
    table = np.zeros((L, 2, 64), np.float32)
    table[0, 0] = 1.0
    table[1:, 0] = np.cos(np.concatenate([angle, angle], axis=1))
    table[1:, 1] = np.concatenate([-np.sin(angle), np.sin(angle)], axis=1)
    return np.tile(table, (BT, 1, 1))


def columns(v):
    return v.reshape(-1, P).T


def kernel(**inputs):
    import concourse.bacc as bacc
    from concourse.bass_utils import run_bass_kernel_spmd

    a = {k: np.asarray(v) for k, v in inputs.items()}
    laid = {
        "x": a["x"].reshape(ROWS, D),
        "ctx": a["ctx_1024"],
        "ctxT": a["ctx_1024"].transpose(0, 2, 1),
        "mask": a["mask_Bx1xS2_ik1"],
        "L0_xattn_WkT": a["L0_xattn_Wk"].T,
    }
    for n in ("Wq", "Wv", "Wo", "bo", "g0", "beta0"):
        laid["L0_xattn_" + n] = a["L0_xattn_" + n]
    laid["masks"] = MASKS
    laid["before"] = (np.arange(16)[None, :] < np.arange(16)[:, None]).astype(np.float32)
    for n in ("W_q", "W_k", "W_v", "W_b", "W_fuse1", "W_fuse2", "b_fuse2", "others_log_tau", "W_o"):
        laid["L0_attn_" + n] = a["L0_attn_" + n]
    laid["L0_attn_b_fuse1"] = columns(a["L0_attn_b_fuse1"])
    laid["L0_attn_conv"] = np.stack([a["L0_attn_conv_w_" + n].reshape(DC, P, TAPS).transpose(1, 0, 2) for n in "qkv"], axis=1)
    laid["L0_attn_fir"] = np.concatenate([a["L0_attn_fir_short_w"].reshape(DC, P, SHORT),
                                          a["L0_attn_fir_long_w"].reshape(DC, P, LONG)], axis=2).transpose(1, 0, 2)
    laid["L0_attn_norm_w"] = np.tile(a["L0_attn_norm_w"], 2).reshape(P, 1)
    for n in ("Wq", "Wk", "Wv", "Wo"):
        laid[f"L1_xattn_{n}T"] = a["L1_xattn_" + n].T
    for n in ("bq", "bk", "bv"):
        laid["L1_xattn_" + n] = columns(a["L1_xattn_" + n])
    laid["L1_xattn_bo"] = a["L1_xattn_bo"]
    order = [4 * (2 * g + r) + h for g in range(2) for h in range(4) for r in range(2)]
    wq = a["L1_attn_Wq"].reshape(16, 64, D)[order].reshape(1024, D)
    laid["L1_attn_WqkvT"] = np.concatenate([wq, a["L1_attn_Wk"], a["L1_attn_Wv"]], axis=0).T
    laid["L1_attn_WoT"] = a["L1_attn_Wo"].reshape(D, 16, 64)[:, order].reshape(D, 1024).T
    laid["rope"] = rope_rows()
    for n in ("q_norm_w", "k_norm_w"):
        laid["L1_attn_" + n] = a["L1_attn_" + n]
    laid["L1_ffn_gate_wT"] = a["L1_ffn_gate_w"].T
    laid["L1_ffn_bias_e"] = a["L1_ffn_bias_e"]
    up = np.concatenate([a["L1_ffn_up_w"], a["L1_ffn_shared_up"].reshape(4, P, D)], axis=0)
    down = np.concatenate([a["L1_ffn_down_w"], a["L1_ffn_shared_down"].reshape(D, 4, P).transpose(1, 0, 2)], axis=0)
    laid["L1_ffn_upT"], laid["L1_ffn_downT"] = up.transpose(0, 2, 1), down.transpose(0, 2, 1)
    laid["L0_ffn_WrT"] = a["L0_ffn_Wr"].T
    laid["L0_ffn_W1T"] = a["L0_ffn_W1"].transpose(0, 2, 1)
    laid["L0_ffn_W2T"] = a["L0_ffn_W2"].transpose(0, 2, 1)
    for n in ("bq", "bk", "bv"):
        laid["L0_xattn_" + n] = columns(a["L0_xattn_" + n])
    nc = bacc.Bacc("TRN2", target_bir_lowering=False, num_devices=1)
    arrays, ins = {}, {}
    for name, v in laid.items():
        v = np.ascontiguousarray(v)
        arrays["in_" + name] = v
        ins[name] = nc.dram_tensor("in_" + name, v.shape, mybir.dt.from_np(v.dtype), kind="ExternalInput").ap()
    out = nc.dram_tensor("out_0", (ROWS, D), F32, kind="ExternalOutput").ap()
    program(nc, ins, out)
    r = run_bass_kernel_spmd(nc, [arrays], core_ids=[0])
    return r.results[0]["out_0"].reshape(B, L, D)
```

```python
from contextlib import ExitStack

import numpy as np

import concourse.bass as bass
from concourse import mybir

F32 = mybir.dt.float32
F32R = mybir.dt.float32r
I32 = mybir.dt.int32
ALU = mybir.AluOpType
ACT = mybir.ActivationFunctionType
AX = mybir.AxisListType

P = 128
B, L, D = 64, 32, 256
DC = D // P
NK = 257
ROWS = B * L
NT = ROWS // P
BT = P // L
NG = ROWS // 512

ENGINES = ("pe", "act", "dve", "pool", "sp")


class Stage:

    def __init__(self, K, name, turns, oldest_first=False):
        self.K, self.name, self.turns = K, name, turns
        self.steps = {e: [] for e in ENGINES}
        self.first = {e: [] for e in ENGINES}
        self.dma, self.lag, self.oldest_first = {}, 0, oldest_first

    def step(self, engine, name, emit, needs=(), dmas=0, lag=0):
        self.steps[engine].append((name, emit, tuple(needs), lag))
        self.lag = max(self.lag, lag)
        if dmas:
            self.dma[name] = (self.K.sem(f"{self.name}_{name}"), 16 * dmas)

    def before(self, engine, emit, needs=()):
        self.first[engine].append((emit, needs))

    def wanted(self, need, turn, lag):
        what, _, back = need.partition("<")
        engine, _, name = what.partition(".")
        back = int(back or 0)
        if name in self.dma:
            sem, per = self.dma[name]
            return sem, (turn - lag + 1 - back) * per
        names = [s[0] for s in self.steps[engine]]
        at, per = names.index(name), len(names)
        back += lag - self.steps[engine][at][3]
        assert back >= 0, (need, "is done only later")
        return self.K.count[engine], (turn + 2 - back) * per + at + 1 + self.base[engine]

    def turn(self, eng, key, i, t=None):
        for name, emit, needs, lag in self.steps[key]:
            if t is not None and not lag <= t < self.turns + lag:
                if name not in self.dma:
                    eng.drain().then_inc(self.K.count[key], 1)
                continue
            latest = {}
            for need in needs:
                source = need if need.partition("<")[0].partition(".")[2] in self.dma else need[:need.index(".")]
                if source not in latest or self.wanted(need, 0, lag)[1] > self.wanted(latest[source], 0, lag)[1]:
                    latest[source] = need
            for need in latest.values():
                eng.wait_ge(*self.wanted(need, i, lag))
                if key == "sp" and not isinstance(i, int):
                    eng.sem_inc(self.K.gate[key], 1)
            if needs and key != "sp" and not isinstance(i, int):
                eng.sem_inc(self.K.gate[key], 1)
            done = emit(eng, i - lag if lag else i)
            if name not in self.dma:
                done.then_inc(self.K.count[key], 1)

    def run(self):
        used = [e for e in ENGINES if self.steps[e] or self.first[e]]
        self.base = dict(self.K.base)
        for e in used:
            self.K.base[e] += (self.turns + 2 + self.lag) * len(self.steps[e])
            if self.oldest_first:
                self.steps[e].sort(key=lambda step: -step[3])
        with self.K.nc.Block() as block:
            def program(key):
                def body(eng):
                    for emit, needs in self.first[key]:
                        for sem, value in needs:
                            eng.wait_ge(sem, value)
                        emit(eng)
                    if not self.steps[key]:
                        return
                    eng.sem_inc(self.K.count[key], 2 * len(self.steps[key]))
                    if self.turns == 1:
                        self.turn(eng, key, 0)
                        return
                    for t in range(self.lag):
                        self.turn(eng, key, t, t)
                    with eng.Fori(self.lag, self.turns) as i:
                        self.turn(eng, key, i)
                    for t in range(self.turns, self.turns + self.lag):
                        self.turn(eng, key, t, t)
                return body
            for key, where in (("sp", block.sync), ("pool", block.gpsimd), ("act", block.scalar),
                               ("pe", block.tensor), ("dve", block.vector)):
                if key in used:
                    where(program(key))


class Kern:

    def __init__(self, nc, ctx, ins, out):
        self.nc, self.ctx, self.ins, self.out = nc, ctx, ins, out

    def sem(self, name):
        return self.ctx.enter_context(self.nc.semaphore(name))

    def sb(self, name, shape, dt=F32, ctx=None):
        return (ctx or self.ctx).enter_context(self.nc.sbuf_tensor(name, shape, dt))


def product3(e, out, w, x, start, stop):
    (wh, wl), (xh, xl) = w, x
    e.matmul(out, wh, xh, start=start, stop=False)
    e.matmul(out, wh, xl, start=False, stop=False)
    return e.matmul(out, wl, xh, start=False, stop=stop)


def features(w):
    return w.rearrange("(c p) m -> p c m", p=P)


def tile_at(i, s):
    return bass.ds(2 * i + s, 1)


def cols_at(i, s, width=P):
    return bass.ds((2 * i + s) * width, width)


def load(K, name, dst, srcs):
    sem = K.sem("ld_" + name)
    for d, s in zip(dst, srcs):
        K.pending.append((d, s, sem))
    return sem, 16 * len(dst)


def start_loads(K, stage):
    pending, K.pending = K.pending, []

    def emit(eng):
        for d, s, sem in pending:
            eng.dma_start(d, s).then_inc(sem, 16)
    stage.before("sp", emit)


def row_stats(K, tag, src, eps, wait=()):
    S = Stage(K, tag, 1)
    S.before("dve", lambda e: None, wait)
    start_loads(K, S)

    def stats(e, i):
        for t in range(NT):
            done = e.bn_stats(K.bn[:, t, :], src[:, t, :])
        return done

    def aggregate(e, i):
        for t in range(NT):
            done = e.bn_aggr(K.mv[:, t, :], K.bn[:, t, :])
        return done
    S.step("dve", "stats", stats)
    S.step("dve", "aggr", aggregate, ["dve.stats"])
    S.step("dve", "eps", lambda e, i: e.tensor_scalar(K.std[:, :], K.mv[:, :, 1], eps, None, ALU.add), ["dve.aggr"])
    S.step("act", "root", lambda e, i: e.activation(K.std[:, :], K.std[:, :], ACT.Sqrt), ["dve.eps"])
    S.step("dve", "inv", lambda e, i: e.reciprocal(K.rstd[:, :], K.std[:, :]), ["act.root"])
    S.run()


def norm_transpose(K, tag, extra=None, split=None, wait=None):
    S = Stage(K, tag, NT // 2, oldest_first=True)
    if wait:
        S.before("sp", lambda e: None, [wait])
    for s in range(2):
        S.step("dve", f"xn{s}", lambda e, i, s=s: e.tensor_scalar(
            K.xnb[:, s, :], K.x[:, tile_at(i, s), :], K.mv[:, tile_at(i, s), 0], K.rstd[:, tile_at(i, s)],
            ALU.subtract, ALU.mult), [f"pe.tr{s}<1"])

        def transposes(e, i, s=s):
            for c in range(DC):
                done = e.transpose(K.ps[:, s, c * P:(c + 1) * P], K.xnb[:, s, c * P:(c + 1) * P], K.ident[:, :])
            return done
        S.step("pe", f"tr{s}", transposes, [f"dve.xn{s}", f"act.ev{s}<1"], lag=1)
    last = extra(S) if extra else []
    for s, mover in enumerate(("pool", "dve")):
        turned = K.ps[:, s, 0:D].rearrange("p (c n) -> p c n", c=DC)
        if not extra and not split:
            S.step("act", f"ev{s}", lambda e, i, s=s, turned=turned: e.activation(
                K.xnT[:, :, cols_at(i, s)], turned, ACT.Copy), [f"pe.tr{s}"], lag=1)
            continue
        S.step("act", f"ev{s}", lambda e, i, s=s, turned=turned: e.activation(K.xs[:, s, :, :], turned, ACT.Copy),
               [f"pe.tr{s}", f"{mover}.cp{s}<1"] + ([f"dve.lo{s}<1"] if split else []) + [n.format(s=s) + "<1" for n in last], lag=1)
        S.step(mover, f"cp{s}", lambda e, i, s=s: e.tensor_copy(
            (split[0] if split else K.xnT)[:, :, cols_at(i, s)], K.xs[:, s, :, :]), [f"act.ev{s}"], lag=1)
        if split:
            S.step("dve", f"lo{s}", lambda e, i, s=s: e.tensor_tensor(
                split[1][:, :, cols_at(i, s)], K.xs[:, s, :, :], split[0][:, :, cols_at(i, s)].bitcast(F32), ALU.subtract),
                [f"{mover}.cp{s}"], lag=2)
    S.run()


def feature_gemm(K, tag, outT, w, inT, kc, mc, finish, needs=(), pre=None):
    S = Stage(K, tag, NG)
    S.before("pe", lambda e: None, needs)
    nb = min(4, mc)
    assert mc % nb == 0
    for m in range(mc):
        bank = K.ps[:, m % nb, :]
        key, emit = finish(m)
        free = f"{key if m >= nb else finish(m + mc - nb)[0]}.ev{m - nb if m >= nb else m + mc - nb}" + ("" if m >= nb else "<1")
        if m >= nb:
            free = f"{finish(m - nb)[0]}.ev{m - nb}"

        def product(e, i, m=m, bank=bank):
            for k in range(kc):
                done = e.matmul(bank, w[:, k, m * P:(m + 1) * P], inT(k, i), start=(k == 0), stop=(k == kc - 1))
            return done
        S.step("pe", f"mm{m}", product, [free])
        S.step(key, f"ev{m}", lambda e, i, emit=emit, bank=bank: emit(e, i, bank), [f"pe.mm{m}"])
    if pre:
        pre(S)
    S.run()


def rows_of(t):
    return lambda k, i: t[:, k, bass.ds(i * 512, 512)]


def cross_attention_0(K):
    I = K.ins
    with ExitStack() as ctx:
        def sb(name, shape, dt=F32):
            return K.sb("a0_" + name, shape, dt, ctx)
        K.xnT = sb("xnT", [P, DC, ROWS])
        K.stage = sb("stage", [P, 2, DC, P])
        wq, wkT, wv, wo = (sb(n, [P, DC, D]) for n in ("wq", "wkT", "wv", "wo"))
        bq, bk, bv = (sb(n, [P, DC]) for n in ("bq", "bk", "bv"))
        bo, g0, beta0 = (sb(n, [P, D]) for n in ("bo", "g0", "beta0"))
        qT, kqT = (sb(n, [P, DC, ROWS]) for n in ("qT", "kqT"))
        ctxT = sb("ctxT", [P, 2, DC, BT, NK])
        ctxR = sb("ctxR", [P, 2, 2, BT, D])
        ctxL = sb("ctxL", [1, 2, BT, D])
        mask = sb("mask", [P, 2, NK], I32)
        off = sb("off", [P, 2, NK])
        keep = sb("keep", [P, 2, NK])
        qs = sb("qs", [P, 2, DC, P])
        kqs = sb("kqs", [P, 2, DC, P])
        qbk = sb("qbk", [P, 2])
        sc = sb("sc", [P, 2, NK])
        sm = sb("sm", [P, 2, NK])
        pr = sb("pr", [P, 2, NK])
        prT = sb("prT", [P, 2, 2, P])
        prL = sb("prL", [1, 2, P])
        neg, tot, inv = (sb(n, [P, 2]) for n in ("neg", "tot", "inv"))
        mix = sb("mix", [P, 2, D])
        y = sb("y", [P, NT, D])

        w_qk = load(K, "a0_qk", [wq[:, :, :], wkT[:, :, :]], [features(I["L0_xattn_Wq"]), features(I["L0_xattn_WkT"])])
        w_b = load(K, "a0_b", [bq[:, :], bk[:, :], bv[:, :], bo[:, :], g0[:, :], beta0[:, :]],
                   [I["L0_xattn_" + n] for n in ("bq", "bk", "bv")]
                   + [I["L0_xattn_" + n].partition_broadcast(P) for n in ("bo", "g0", "beta0")])
        w_vo = load(K, "a0_vo", [wv[:, :, :], wo[:, :, :]], [features(I["L0_xattn_Wv"]), features(I["L0_xattn_Wo"])])
        row_stats(K, "a0_ln", K.x, 1e-5, [K.x_loaded])
        norm_transpose(K, "a0_nt")

        def q_finish(m):
            return "dve", lambda e, i, ps, m=m: e.tensor_scalar(
                qT[:, m, bass.ds(i * 512, 512)], ps, bq[:, m:m + 1], 1.0 / 16.0, ALU.add, ALU.mult)
        feature_gemm(K, "a0_q", qT, wq, rows_of(K.xnT), DC, DC, q_finish, [w_qk, w_b])

        def kq_finish(m):
            return ("dve", "act")[m], lambda e, i, ps, m=m: copy(e, kqT[:, m, bass.ds(i * 512, 512)], ps)
        feature_gemm(K, "a0_kq", kqT, wkT, rows_of(qT), DC, DC, kq_finish)

        S = Stage(K, "a0_at", NT // 2)
        mask_rows = I["mask"].rearrange("b q k -> b (q k)")

        def load_keys(s):
            def emit(e, i):
                at, sem = bass.ds((2 * i + s) * BT, BT), S.dma[f"ctxT{s}"][0]
                for c in range(DC):
                    e.dma_start(ctxT[:, s, c, :, :], I["ctxT"][at, c * P:(c + 1) * P, :].rearrange(
                        "b p k -> p b k")).then_inc(sem, 16)
            S.step("sp", f"ctxT{s}", emit, [f"pe.sc{s}<1"], dmas=DC)

            def emit_mask(e, i):
                for b in range(BT):
                    e.dma_start(mask[L * b:L * b + L, s, :], mask_rows[bass.ds((2 * i + s) * BT + b, 1), :].rearrange(
                        "a k -> (a k)").partition_broadcast(L)).then_inc(S.dma[f"mask{s}"][0], 16)
            S.step("sp", f"mask{s}", emit_mask, [f"pool.off{s}<1"], dmas=BT)

        def load_values(s):
            def emit(e, i):
                at, sem = bass.ds((2 * i + s) * BT, BT), S.dma[f"ctx{s}"][0]
                for c in range(2):
                    e.dma_start(ctxR[:, s, c, :, :], I["ctx"][at, c * P:(c + 1) * P, :].rearrange(
                        "b p d -> p b d")).then_inc(sem, 16)
                e.dma_start(ctxL[:, s, :, :], I["ctx"][at, NK - 1:NK, :].rearrange("b k d -> k b d")).then_inc(sem, 16)
            S.step("sp", f"ctx{s}", emit, [f"pe.pv{s}<1"], dmas=3, lag=1)

        def masks_and_queries(s):
            S.step("act", f"kqs{s}", lambda e, i: e.activation(kqs[:, s, :, :], kqT[:, :, cols_at(i, s)], ACT.Copy),
                   [f"pe.sc{s}<1"])
            S.step("pool", f"qs{s}", lambda e, i: e.tensor_copy(qs[:, s, :, :], qT[:, :, cols_at(i, s)]),
                   [f"pe.sc{s}<1"])
            S.step("pool", f"off{s}", lambda e, i: e.tensor_scalar(
                off[:, s, :], mask[:, s, :], 0.0, -1e9, ALU.is_equal, ALU.mult), [f"sp.mask{s}", f"dve.sm{s}<1"])
            S.step("pool", f"keep{s}", lambda e, i: e.tensor_scalar(
                keep[:, s, :], off[:, s, :], 0.0, None, ALU.is_equal), [f"pool.off{s}", f"dve.sc{s}<1"])

        def scores(s):
            def emit(e, i):
                for c in range(DC):
                    e.matmul(K.ps[:, s, 300:301], qs[:, s, c, :], bk[:, c:c + 1], start=(c == 0), stop=(c == DC - 1))
                for c in range(DC):
                    for b in range(BT):
                        done = e.matmul(K.ps[L * b:L * b + L, s, 0:NK], kqs[:, s, c, L * b:L * b + L],
                                        ctxT[:, s, c, b, :], start=(c == 0), stop=(c == DC - 1))
                return done
            S.step("pe", f"sc{s}", emit, [f"sp.ctxT{s}", f"pool.qs{s}", f"act.kqs{s}", f"dve.sc{s}<1"])

        def softmax(s):
            S.step("dve", f"qbk{s}", lambda e, i: e.tensor_copy(qbk[:, s:s + 1], K.ps[:, s, 300:301]),
                   [f"pe.sc{s}", f"dve.sc{s}<1"])
            S.step("dve", f"sc{s}", lambda e, i: e.scalar_tensor_tensor(
                sc[:, s, :], K.ps[:, s, 0:NK], qbk[:, s:s + 1], keep[:, s, :], ALU.add, ALU.mult),
                [f"dve.qbk{s}", f"pool.keep{s}"])
            S.step("dve", f"sm{s}", lambda e, i: e.tensor_tensor(
                sm[:, s, :], sc[:, s, :], off[:, s, :], ALU.add), [f"dve.sc{s}", f"act.exp{s}<1"])
            S.step("dve", f"mx{s}", lambda e, i: e.tensor_reduce(
                neg[:, s:s + 1], sm[:, s, :], AX.X, ALU.max, negate=True), [f"dve.sm{s}"])
            S.step("act", f"exp{s}", lambda e, i: e.activation(
                pr[:, s, :], sm[:, s, :], ACT.Exp, bias=neg[:, s:s + 1], accum_out=tot[:, s:s + 1]),
                [f"dve.mx{s}", f"pe.prT{s}<1", f"dve.inv{s}<1"])

        def turn_probs(s):
            S.step("dve", f"inv{s}", lambda e, i: e.reciprocal(inv[:, s:s + 1], tot[:, s:s + 1]),
                   [f"act.exp{s}", f"act.mix{s}<1"], lag=1)

            def emit(e, i):
                e.transpose(K.ps[:, 2 + s, 0:P], pr[:, s, 0:P], K.ident[:, :])
                e.transpose(K.ps[:, 2 + s, P:2 * P], pr[:, s, P:2 * P], K.ident[:, :])
                return e.transpose(K.ps[0:1, 2 + s, 2 * P:3 * P], pr[:, s, 2 * P:NK], K.ident[:, :])
            S.step("pe", f"prT{s}", emit, [f"act.exp{s}", f"act.prL{s}<1"], lag=1)
            S.step("dve", f"prT{s}", lambda e, i: e.tensor_copy(
                prT[:, s, :, :], K.ps[:, 2 + s, 0:2 * P].rearrange("p (c n) -> p c n", c=2)),
                [f"pe.prT{s}", f"pe.pv{s}<1"], lag=1)
            S.step("act", f"prL{s}", lambda e, i: e.activation(
                prL[:, s, :], K.ps[0:1, 2 + s, 2 * P:3 * P], ACT.Copy), [f"dve.prT{s}"], lag=1)

        def mixing(s):
            def emit(e, i):
                for b in range(BT):
                    rows = slice(L * b, L * b + L)
                    e.matmul(K.ps[rows, 4 + s, 0:D], prT[:, s, 0, rows], ctxR[:, s, 0, b, :], start=True, stop=False)
                    e.matmul(K.ps[rows, 4 + s, 0:D], prT[:, s, 1, rows], ctxR[:, s, 1, b, :], start=False, stop=False)
                    done = e.matmul(K.ps[rows, 4 + s, 0:D], prL[:, s, rows], ctxL[:, s, b, :], start=False, stop=True)
                return done
            S.step("pe", f"pv{s}", emit, [f"sp.ctx{s}", f"act.prL{s}", f"act.mix{s}<1"], lag=1)
            S.step("act", f"mix{s}", lambda e, i: e.activation(
                mix[:, s, :], K.ps[:, 4 + s, 0:D], ACT.Copy, scale=inv[:, s:s + 1]),
                [f"pe.pv{s}", f"dve.inv{s}", f"pe.mixT{s}<1"], lag=1)

        def turn_mix(s):
            def emit(e, i):
                for c in range(DC):
                    done = e.transpose(K.ps[:, 6 + s, c * P:(c + 1) * P], mix[:, s, c * P:(c + 1) * P], K.ident[:, :])
                return done
            S.step("pe", f"mixT{s}", emit, [f"act.mix{s}", f"dve.mixT{s}<1"], lag=2)
            S.step("dve", f"mixT{s}", lambda e, i: e.tensor_copy(
                kqT[:, :, cols_at(i, s)], K.ps[:, 6 + s, 0:D].rearrange("p (c n) -> p c n", c=DC)),
                [f"pe.mixT{s}", f"act.kqs{s}"], lag=2)
        for part in (load_keys, load_values, masks_and_queries, turn_probs, turn_mix, scores, softmax, mixing):
            for s in range(2):
                part(s)
        S.run()

        def v_finish(m):
            return ("dve", "act")[m], lambda e, i, ps, m=m: add_bias(e, qT[:, m, bass.ds(i * 512, 512)], ps, bv[:, m:m + 1])
        feature_gemm(K, "a0_v", qT, wv, rows_of(kqT), DC, DC, v_finish, [w_vo])
        output_rows(K, "a0_o", qT, wo, DC, lambda e, t, ps: e.tensor_tensor(y[:, t, :], ps, bo[:, :], ALU.add))

        row_stats(K, "a0_ln2", y, 1e-5)
        S = Stage(K, "a0_res", NT // 2)
        for s in range(2):
            S.step("dve", f"g{s}", lambda e, i, s=s: e.scalar_tensor_tensor(
                y[:, tile_at(i, s), :], y[:, tile_at(i, s), :], K.mv[:, tile_at(i, s), 0], g0[:, :], ALU.subtract, ALU.mult))
            S.step("pool", f"b{s}", lambda e, i, s=s: e.tensor_tensor(
                K.x[:, tile_at(i, s), :], K.x[:, tile_at(i, s), :], beta0[:, :], ALU.add))
        for s in range(2):
            S.step("dve", f"r{s}", lambda e, i, s=s: e.scalar_tensor_tensor(
                K.x[:, tile_at(i, s), :], y[:, tile_at(i, s), :], K.rstd[:, tile_at(i, s)], K.x[:, tile_at(i, s), :],
                ALU.mult, ALU.add), [f"dve.g{s}", f"pool.b{s}"])
        S.run()


def split(S, high, low, name, src, parts, needs, free, lag=0):
    def emit_high(e, i):
        return copy(e, parts[0], src)
    S.step(high, "h" + name, emit_high, list(needs) + list(free), lag=lag)
    S.step(low, "l" + name, lambda e, i: e.tensor_tensor(parts[1], src, parts[0].bitcast(F32), ALU.subtract),
           [f"{high}.h{name}"] + list(free), lag=lag)


def copy(e, out, ps):
    if e.engine == mybir.EngineType.Activation:
        return e.activation(out, ps, ACT.Copy)
    return e.tensor_copy(out, ps)


def add_bias(e, out, ps, bias):
    if e.engine == mybir.EngineType.Activation:
        return e.activation(out, ps, ACT.Identity, bias=bias)
    return e.tensor_scalar(out, ps, bias, None, ALU.add)


def output_rows(K, tag, inT, w, kc, finish, needs=(), pre=None, after=None):
    S = Stage(K, tag, NT // 2, oldest_first=True)
    S.before("pe", lambda e: None, needs)
    if pre:
        pre(S)
    for s in range(2):
        S.step("act", f"st{s}", lambda e, i, s=s: e.activation(
            K.stage[:, s, 0:kc, :], inT[:, 0:kc, cols_at(i, s)], ACT.Copy), [f"pe.mm{s}<1"])

        def product(e, i, s=s):
            for k in range(kc):
                done = e.matmul(K.ps[:, s, 0:D], K.stage[:, s, k, :], w[:, k, :], start=(k == 0), stop=(k == kc - 1))
            return done
        S.step("pe", f"mm{s}", product, [f"act.st{s}", f"dve.ev{s}<1"])
        S.step("dve", f"ev{s}", lambda e, i, s=s: finish(e, tile_at(i, s), K.ps[:, s, 0:D]),
               [f"pe.mm{s}"] + ([after.format(s=s)] if after else []), lag=1)
    S.run()


def constants(K):
    S = Stage(K, "cst", 1)
    S.step("pool", "zero", lambda e, i: e.memset(K.ident[:, :], 0.0))
    S.step("pool", "one", lambda e, i: e.affine_select(
        out=K.ident[:, :], in_=K.ident[:, :], compare_op=ALU.not_equal, fill=1.0, base=0,
        pattern=[[-1, P]], channel_multiplier=1), ["pool.zero"])
    sem = K.sem("ld_x")
    x_rows = K.ins["x"].rearrange("(t p) d -> p t d", p=P)
    S.before("sp", lambda e: e.dma_start(K.x[:, :, :], x_rows).then_inc(sem, 16))
    S.before("sp", lambda e: e.dma_start(K.masks[:, :], K.ins["masks"]).then_inc(sem, 16))
    S.before("sp", lambda e: e.dma_start(K.before[:, :, :], K.ins["before"].partition_broadcast(P)).then_inc(sem, 16))
    K.x_loaded = (sem, 48)
    S.run()


def store(K):
    S = Stage(K, "out", 1)
    sem = K.sem("st_out")
    S.before("sp", lambda e: (e.dma_start(K.out.rearrange("(t p) d -> p t d", p=P), K.x[:, :, :]).then_inc(sem, 16),
                              e.wait_ge(sem, 16)))
    S.run()


H0, DV0 = 4, 64
TAPS, SHORT, LONG = 4, 3, 31
TAP_STEPS = DC * (SHORT + LONG - 2)


def row_logits(K, w, n, dst):
    def extra(S):
        for s in range(2):
            def product(e, i, s=s):
                for c in range(DC):
                    done = e.matmul(K.ps[:, 2 + s, 0:n], K.xs[:, s, c, :], w[:, c, :], start=(c == 0), stop=(c == DC - 1))
                return done
            S.step("pe", f"lg{s}", product, [f"act.ev{s}", f"dve.lg{s}<1"], lag=2)
            S.step("dve", f"lg{s}", lambda e, i, s=s: e.tensor_copy(dst[:, tile_at(i, s), :], K.ps[:, 2 + s, 0:n]),
                   [f"pe.lg{s}"], lag=2)
        return ["pe.lg{s}"]
    return extra


def delta_attention(K):
    I = K.ins
    with ExitStack() as ctx:
        def sb(name, shape, dt=F32, c=ctx):
            return K.sb("b0_" + name, shape, dt, c)
        K.xnT = sb("xnT", [P, DC, ROWS])
        wqkv = sb("wqkv", [P, 3, DC, D])
        wo = sb("wo", [P, DC, D])
        wb = sb("wb", [P, DC, H0])
        conv = sb("conv", [P, 3, DC, TAPS])
        fir = sb("fir", [P, DC, SHORT + LONG])
        bf1 = sb("bf1", [P, 4])
        f2 = sb("f2", [P, 4, 16])
        bf2 = sb("bf2", [P, 16])
        ltau = sb("ltau", [P, H0])
        nw = sb("nw", [P, 1])
        beta = sb("beta", [P, NT, H0])
        qk = sb("qk", [P, 4, ROWS])
        F = sb("F", [P, 6, ROWS])
        dr = sb("dr", [P, NT, D])
        lg = sb("lg", [P, NT, H0, 4])
        gates = sb("gates", [P, NT, H0, 4])
        rn = sb("rn", [P, NT, 8])
        cb = sb("cb", [P, NT, H0])
        ab = sb("ab", [P, NT, H0])

        w_beta = load(K, "b0_0", [wb[:, :, :]], [features(I["L0_attn_W_b"])])
        w_1 = load(K, "b0_1", [wqkv[:, j, :, :] for j in range(3)] + [conv[:, :, :, :], fir[:, :, :]],
                   [features(I["L0_attn_W_" + n]) for n in ("q", "k", "v")] + [I["L0_attn_conv"], I["L0_attn_fir"]])
        w_2 = load(K, "b0_2", [bf1[:, :], f2[:, :, :], bf2[:, :], ltau[:, :], nw[:, :], wo[:, :, :]],
                   [I["L0_attn_b_fuse1"], features(I["L0_attn_W_fuse2"]),
                    I["L0_attn_b_fuse2"].partition_broadcast(P), I["L0_attn_others_log_tau"].partition_broadcast(P),
                    I["L0_attn_norm_w"], features(I["L0_attn_W_o"])])
        row_stats(K, "b0_ln", K.x, 1e-5, [w_beta])
        norm_transpose(K, "b0_nt", row_logits(K, wb, H0, beta), wait=w_1)

        with ExitStack() as c1:
            cv = sb("cv", [P, 6, 512], c=c1)
            S = Stage(K, "b0_qkv", NG)
            S.before("act", lambda e: e.activation(beta[:, :, :], beta[:, :, :], ACT.Sigmoid))
            jobs = [(j, m) for j in range(3) for m in range(DC)]
            for n, (j, m) in enumerate(jobs):
                def product(e, i, j=j, m=m, n=n):
                    for k in range(DC):
                        done = e.matmul(K.ps[:, n, :], wqkv[:, j, k, m * P:(m + 1) * P], K.xnT[:, k, bass.ds(i * 512, 512)],
                                        start=(k == 0), stop=(k == DC - 1))
                    return done
                S.step("pe", f"mm{n}", product, [f"dve.tap{n}_2<1"])
                S.step("act", f"tap{n}", lambda e, i, j=j, m=m, n=n: e.activation(
                    cv[:, n, :], K.ps[:, n, :], ACT.Copy, scale=conv[:, j, m, TAPS - 1:TAPS]),
                    [f"pe.mm{n}", f"act.silu{n}<1"])
                if n >= 2:
                    silu(S, jobs[n - 2], n - 2, cv, qk, F)
            silu(S, jobs[4], 4, cv, qk, F)
            silu(S, jobs[5], 5, cv, qk, F)
            for pair in (0, 2, 4):
                for sh in range(1, TAPS):
                    for n in (pair, pair + 1):
                        j, m = jobs[n]

                        def tap(e, i, j=j, m=m, n=n, sh=sh):
                            src = K.ps[:, n, :].rearrange("p (b l) -> p b l", l=L)[:, :, 0:L - sh]
                            acc = cv[:, n, :].rearrange("p (b l) -> p b l", l=L)[:, :, sh:L]
                            return e.scalar_tensor_tensor(acc, src, conv[:, j, m, TAPS - 1 - sh:TAPS - sh], acc,
                                                          ALU.mult, ALU.add)
                        S.step("dve", f"tap{n}_{sh - 1}", tap,
                               [f"act.tap{n}"] if sh == 1 else [f"dve.tap{n}_{sh - 2}"])
            S.run()

        with ExitStack() as c1:
            sq = sb("sq", [P, 2, 4, P], c=c1)
            S = Stage(K, "b0_n2", NT // 2, oldest_first=True)
            for s in range(2):
                S.step("act", f"sq{s}", lambda e, i, s=s: e.activation(sq[:, s, :, :], qk[:, :, cols_at(i, s)], ACT.Square),
                       [f"pe.n{s}<1"])

                def sums(e, i, s=s):
                    for c in range(4):
                        done = e.matmul(K.ps[:, s, 2 * c:2 * c + 2], sq[:, s, c, :], K.headsel, start=True, stop=True)
                    return done
                S.step("pe", f"n{s}", sums, [f"act.sq{s}", f"dve.n{s}<1"], lag=1)
                S.step("dve", f"n{s}", lambda e, i, s=s: e.tensor_scalar(
                    rn[:, tile_at(i, s), :], K.ps[:, s, 0:8], 1e-6, None, ALU.add), [f"pe.n{s}"], lag=2)
            S.run()
        S = Stage(K, "b0_rn", 1)
        S.step("act", "root", lambda e, i: e.activation(rn[:, :, :], rn[:, :, :], ACT.Sqrt))
        S.step("dve", "inv", lambda e, i: e.reciprocal(rn[:, :, :], rn[:, :, :]), ["act.root"])
        S.step("dve", "ab", lambda e, i: e.tensor_tensor(ab[:, :, :], beta[:, :, :], rn[:, :, 4:8], ALU.mult), ["dve.inv"])
        S.step("dve", "cb", lambda e, i: e.tensor_tensor(cb[:, :, :], ab[:, :, :], rn[:, :, 4:8], ALU.mult), ["dve.ab"])
        S.run()
        delta_solve(K, sb, qk, F, fir, dr, rn, cb, ab, wqkv)

        with ExitStack() as c1:
            hid = sb("hid", [P, 4, 512], c=c1)
            f1 = sb("f1", [P, 8, 512], c=c1)
            w_f1 = load(K, "b0_f1", [f1[:, :, :]], [features(I["L0_attn_W_fuse1"])])
            S = Stage(K, "b0_fuse", NG)
            start_loads(K, S)
            S.before("pe", lambda e: None, [w_f1])
            S.before("pe", lambda e: None, [w_2])
            S.before("act", lambda e: None, [w_2])
            S.before("dve", lambda e: None, [w_2])

            def source(k, i):
                at = bass.ds(i * 512, 512)
                return (K.xnT[:, k, at] if k < 2 else F[:, k, at] if k < 6 else qk[:, k - 6, at])
            for m in range(4):
                def product(e, i, m=m):
                    for k in range(8):
                        done = e.matmul(K.ps[:, m, :], f1[:, k, m * P:(m + 1) * P], source(k, i), start=(k == 0), stop=(k == 7))
                    return done
                S.step("pe", f"h{m}", product, [f"act.h{m}<1"])
                S.step("act", f"h{m}", lambda e, i, m=m: e.activation(
                    hid[:, m, :], K.ps[:, m, :], ACT.Gelu, bias=bf1[:, m:m + 1]), [f"pe.h{m}", "pe.lg<1"])

            def logits(e, i):
                for t in range(4):
                    for k in range(4):
                        done = e.matmul(K.ps[:, 4, 16 * t:16 * t + 16], hid[:, k, t * P:(t + 1) * P], f2[:, k, :],
                                        start=(k == 0), stop=(k == 3))
                return done
            S.step("pe", "lg", logits, ["act.h3", "dve.lg<1"])
            S.step("dve", "lg", lambda e, i: e.tensor_tensor(
                lg[:, bass.ds(4 * i, 4), :, :].rearrange("p t h g -> p t (h g)"), K.ps[:, 4, 0:64].rearrange("p (t g) -> p t g", t=4),
                bf2[:, :].unsqueeze(1).to_broadcast([P, 4, 16]), ALU.add), ["pe.lg"])
            S.run()
        mixture_gates(K, sb, lg, gates, ltau)
        delta_mix(K, sb, F, dr, gates, wo, nw)


def silu(S, job, n, cv, qk, F):
    j, m = job
    dst = (qk[:, m, :], qk[:, 2 + m, :], F[:, m, :])[j]
    S.step("act", f"silu{n}", lambda e, i, n=n: e.activation(dst[:, bass.ds(i * 512, 512)], cv[:, n, :], ACT.Silu),
           [f"dve.tap{n}_2"])


def fir_steps(S, F, fir):
    lanes = [(m, 2 + m, 0, SHORT) for m in range(DC)] + [(m, 4 + m, SHORT, LONG) for m in range(DC)]
    for n, (src, dst, at, taps) in enumerate(lanes):
        S.step("act", f"t{n}_0", lambda e, i, src=src, dst=dst, at=at, taps=taps: e.activation(
            F[:, dst, bass.ds(i * 2 * P, 2 * P)], F[:, src, bass.ds(i * 2 * P, 2 * P)], ACT.Copy,
            scale=fir[:, src, at + taps - 1:at + taps]))
    for sh in range(1, LONG):
        for n, (src, dst, at, taps) in enumerate(lanes):
            if sh < taps:
                def tap(e, i, src=src, dst=dst, at=at, taps=taps, sh=sh):
                    x = F[:, src, bass.ds(i * 2 * P, 2 * P)].rearrange("p (b l) -> p b l", l=L)[:, :, 0:L - sh]
                    acc = F[:, dst, bass.ds(i * 2 * P, 2 * P)].rearrange("p (b l) -> p b l", l=L)[:, :, sh:L]
                    return e.scalar_tensor_tensor(acc, x, fir[:, src, at + taps - 1 - sh:at + taps - sh], acc, ALU.mult, ALU.add)
                yield lambda n=n, sh=sh, tap=tap: S.step("dve", f"t{n}_{sh}", tap, [f"act.t{n}_0" if sh == 1 else f"dve.t{n}_{sh - 1}"])


def delta_solve(K, sb, qk, F, fir, dr, rn, cb, ab, free):
    with ExitStack() as ctx:
        kqs = free[:, 1:3, :, :].rearrange("p s c (h n) -> p s (c h) n", n=P)
        vs = free[:, 0, :, :].rearrange("p s (c n) -> p s c n", n=P)
        cm, Ac, At, XA, X, Y, Yl, P1 = (sb(n, [P, 2, H0, L], c=ctx) for n in ("cm", "Ac", "At", "XA", "X", "Y", "Yl", "P1"))
        Lc, ATc = (sb(n, [P, NT, H0 * L], c=ctx) for n in ("Lc", "ATc"))
        Lbd, Ybd, Zbd = (sb(n, [P, 2, H0, P], c=ctx) for n in ("Lbd", "Ybd", "Zbd"))
        AT = [sb(f"AT{m}", [P, 2, H0, P], c=ctx) for m in range(3)]
        AT = [AT[0], AT[1], AT[0], AT[2]]
        w1, w2, u, od = (sb(n, [P, 2, D], c=ctx) for n in ("w1", "w2", "u", "od"))
        S = Stage(K, "b0_ds", NT // 2)
        low = K.low.unsqueeze(1).to_broadcast([P, H0, L])
        one = K.eye.unsqueeze(1).to_broadcast([P, H0, L])
        half = K.half.unsqueeze(1).to_broadcast([P, H0, L])
        parts = ([], [], [])

        def add(lag, engine, name, emit, needs):
            for s in range(2):
                parts[lag].append((engine, lambda s=s: S.step(engine, f"{name}{s}", lambda e, i: emit(e, i, s),
                                                     [n.format(s=s) for n in needs], lag=lag)))

        def flat(ap):
            return ap.rearrange("p h l -> p (h l)")

        def heads(ap):
            return ap.rearrange("p (h l) -> p h l", h=H0)

        def tile_heads(t, i, s):
            return t[:, tile_at(i, s), :].rearrange("p t (h l) -> p (t h) l", h=H0)

        def by_head(t, i, s, n):
            return t.rearrange("p t h -> p (t h)").unsqueeze(2).to_broadcast([P, H0, n])

        def by_bank(ap):
            return ap.rearrange("p (c b) l -> p c b l", b=2)

        def spread(e, out, compact, mask):
            shape = [P, compact.shape[1], BT, L]
            return e.tensor_tensor(out.rearrange("p h (b l) -> p h b l", b=BT), compact.unsqueeze(2).to_broadcast(shape),
                                   mask.rearrange("p (b l) -> p b l", b=BT).unsqueeze(1).to_broadcast(shape), ALU.mult)

        def bank(s, n):
            return K.ps[:, 4 * s + n, :]

        add(0, "act", "kq", lambda e, i, s: e.activation(kqs[:, s, :, :], qk[:, :, cols_at(i, s)], ACT.Copy), ["pe.G{s}<1"])
        add(0, "pool", "cm", lambda e, i, s: e.tensor_tensor(
            cm[:, s, :, :], low, by_head(cb[:, tile_at(i, s), :], i, s, L), ALU.mult), ["dve.A{s}<1"])

        def grams(e, i, s):
            for h in range(H0):
                rows = slice(64 * (h % 2), 64 * (h % 2) + 64)
                for b in range(BT):
                    own = slice(L * b, L * b + L)
                    out, col = bank(s, h % 2), L * (h // 2)
                    e.matmul(out[own, col:col + L], kqs[rows, s, 2 + h // 2, own],
                             kqs[rows, s, 2 + h // 2, own], start=True, stop=True)
                    done = e.matmul(out[own, P + col:P + col + L], kqs[rows, s, 2 + h // 2, own],
                                    kqs[rows, s, h // 2, own], start=True, stop=True)
            return done
        add(0, "pe", "G", grams, ["act.kq{s}", "dve.v0{s}<1", "act.L{s}<1"])
        add(0, "act", "v", lambda e, i, s: e.activation(vs[:, s, :, :], F[:, 0:2, cols_at(i, s)], ACT.Copy), ["pe.vT{s}<1"])

        def turn_v(e, i, s):
            for c in range(DC):
                done = e.transpose(bank(s, 0)[:, D + c * P:D + (c + 1) * P], vs[:, s, c, :], K.ident[:, :])
            return done
        add(0, "pe", "vT", turn_v, ["act.v{s}"])
        add(0, "dve", "A", lambda e, i, s: e.tensor_tensor(
            by_bank(Ac[:, s, :, :]), K.ps[:, 4 * s:4 * s + 2, 0:2 * L].rearrange("p b (c l) -> p c b l", c=2),
            by_bank(cm[:, s, :, :]), ALU.mult), ["pe.vT{s}", "pool.cm{s}"])
        add(0, "act", "L", lambda e, i, s: e.activation(
            by_bank(tile_heads(Lc, i, s)), K.ps[:, 4 * s:4 * s + 2, P:P + 2 * L].rearrange("p b (c l) -> p c b l", c=2), ACT.Copy),
            ["dve.A{s}"])
        add(0, "dve", "AT", lambda e, i, s: e.transpose(flat(At[:, s, :, :]), flat(Ac[:, s, :, :])), ["dve.A{s}", "act.AT{s}<1"])
        add(0, "act", "AT", lambda e, i, s: e.activation(ATc[:, tile_at(i, s), :], flat(At[:, s, :, :]).unsqueeze(1), ACT.Copy),
            ["dve.AT{s}"])
        add(0, "dve", "v0", lambda e, i, s: e.tensor_tensor(
            tile_heads(dr, i, s), heads(bank(s, 0)[:, D:2 * D]), by_head(ab[:, tile_at(i, s), :], i, s, DV0), ALU.mult), ["act.L{s}"])
        add(0, "dve", "X0", lambda e, i, s: e.tensor_tensor(XA[:, s, :, :], Ac[:, s, :, :], half, ALU.mult),
            ["dve.A{s}", "dve.X2{s}<1", "dve.Y0{s}<1", "pe.P0{s}<1"])
        add(0, "dve", "X1", lambda e, i, s: e.tensor_tensor(XA[:, s, :, :], one, XA[:, s, :, :], ALU.subtract), ["dve.X0{s}"])

        def spread_at(m, lag):
            add(lag, "pool", f"AT{m}", lambda e, i, s: spread(e, AT[m][:, s, :, :], tile_heads(ATc, i, s), K.between[m]),
                ["act.AT{s}", ("pe.P2{s}<1", "pe.P1{s}<1", "pe.P0{s}", "pe.w2{s}<1")[m]])
        spread_at(0, 1)

        def transposed(m, src):
            add(1, "dve", f"Y{m}", lambda e, i, s: e.transpose(flat((Yl if m == 3 else Y)[:, s, :, :]), flat(src[:, s, :, :])),
                [f"dve.X{m + 1}{{s}}"] + (["dve.Yb3{s}<1"] if m == 3 else []))
            if m < 3:
                add(1, "dve", f"Yb{m}", lambda e, i, s: spread(e, Ybd[:, s, :, :], Y[:, s, :, :], K.blocks),
                    [f"dve.Y{m}{{s}}", f"pe.XP{m - 1}{{s}}" if m else "pe.XP2{s}<1"])
        transposed(0, XA)
        for m in range(3):
            src = X if m else XA

            def p1(e, i, s, m=m, src=src):
                for h in range(H0):
                    done = e.matmul(bank(s, 2)[:, L * h:L * h + L], AT[m][:, s, h, :], src[:, s, h, :], start=True, stop=True)
                return done
            add(1, "pe", f"P{m}", p1, [f"pool.AT{m}{{s}}", f"dve.X{m + 1}{{s}}"] + ([] if m else ["dve.X4{s}<1"]))
            add(1, "act", f"P{m}", lambda e, i, s: e.activation(P1[:, s, :, :], heads(bank(s, 2)[:, 0:P]), ACT.Copy),
                [f"pe.P{m}{{s}}"])
            if m < 2:
                spread_at(m + 1, 1)

            def xp(e, i, s):
                for h in range(H0):
                    done = e.matmul(bank(s, 2)[:, P + L * h:P + L * h + L], Ybd[:, s, h, :], P1[:, s, h, :], start=True, stop=True)
                return done
            add(1, "pe", f"XP{m}", xp, [f"act.P{m}{{s}}", f"dve.Yb{m}{{s}}"])
            add(1, "dve", f"X{m + 2}", lambda e, i, s, src=src: e.tensor_tensor(
                X[:, s, :, :], src[:, s, :, :], heads(bank(s, 2)[:, P:2 * P]), ALU.subtract), [f"pe.XP{m}{{s}}"])
            transposed(m + 1, X)

        add(2, "dve", "Yb3", lambda e, i, s: spread(e, Zbd[:, s, :, :], Yl[:, s, :, :], K.blocks), ["dve.Y3{s}", "pe.w3{s}<1"])

        def apply(name, at, lhs, rhs, needs):
            def emit(e, i, s):
                for h in range(H0):
                    done = e.matmul(bank(s, 3)[:, at + DV0 * h:at + DV0 * h + DV0], lhs[:, s, h, :], rhs(i, s, h), start=True, stop=True)
                return done
            add(2, "pe", name, emit, needs)

        def head_of(t):
            return lambda i, s, h: t[:, s, DV0 * h:DV0 * h + DV0]
        apply("w1", 0, Zbd, lambda i, s, h: dr[:, tile_at(i, s), DV0 * h:DV0 * h + DV0].rearrange("p t v -> p (t v)"),
              ["dve.Yb3{s}", "dve.v0{s}", "act.oT{s}<1"])
        spread_at(3, 2)
        add(2, "act", "w1", lambda e, i, s: e.activation(w1[:, s, :], bank(s, 3)[:, 0:D], ACT.Copy), ["pe.w1{s}"])
        add(2, "dve", "Lb", lambda e, i, s: spread(e, Lbd[:, s, :, :], tile_heads(Lc, i, s), K.upto), ["act.L{s}", "pe.o{s}<1"])
        apply("w2", D, AT[3], head_of(w1), ["act.w1{s}", "pool.AT3{s}"])
        add(2, "act", "w2", lambda e, i, s: e.activation(w2[:, s, :], bank(s, 3)[:, D:2 * D], ACT.Copy), ["pe.w2{s}"])
        apply("w3", 0, Zbd, head_of(w2), ["act.w2{s}"])
        add(2, "dve", "u", lambda e, i, s: e.tensor_tensor(u[:, s, :], w1[:, s, :], bank(s, 3)[:, 0:D], ALU.subtract), ["pe.w3{s}"])
        apply("o", D, Lbd, head_of(u), ["dve.u{s}", "dve.Lb{s}"])
        add(2, "dve", "o", lambda e, i, s: e.tensor_tensor(
            heads(od[:, s, :]), heads(bank(s, 3)[:, D:2 * D]), by_head(rn[:, tile_at(i, s), 0:4], i, s, DV0), ALU.mult),
            ["pe.o{s}", "pe.oT{s}<1", "pool.dr{s}<1"])
        add(2, "pool", "dr", lambda e, i, s: e.tensor_copy(dr[:, tile_at(i, s), :], od[:, s, :].unsqueeze(1)), ["dve.o{s}"])

        def turn_o(e, i, s):
            for c in range(DC):
                done = e.transpose(bank(s, 3)[:, c * P:(c + 1) * P], od[:, s, c * P:(c + 1) * P], K.ident[:, :])
            return done
        add(2, "pe", "oT", turn_o, ["dve.o{s}"])
        add(2, "act", "oT", lambda e, i, s: e.activation(
            qk[:, 0:2, cols_at(i, s)], bank(s, 3)[:, 0:D].rearrange("p (c n) -> p c n", c=DC), ACT.Copy), ["pe.oT{s}"])
        taps = list(fir_steps(S, F, fir))
        order = sorted((((n + 0.5) / len(chain), -lag, engine, put) for lag, chain in enumerate(parts)
                        for n, (engine, put) in enumerate(chain)), key=lambda step: step[:2])
        turns, done = sum(step[2] == "dve" for step in order), 0
        for _, _, engine, put in order:
            put()
            if engine == "dve":
                done += 1
                while taps and len(taps) > TAP_STEPS * (turns - done) / turns:
                    taps.pop(0)()
        S.run()


def mixture_gates(K, sb, lg, gates, ltau):
    with ExitStack() as ctx:
        raw, fl, mx, tot = (sb(n, [P, NT, H0], c=ctx) for n in ("raw", "fl", "mx", "tot"))
        tau = sb("tau", [P, H0], c=ctx)
        oth = sb("oth", [P, NT, H0, 3], c=ctx)
        S = Stage(K, "b0_g", 1)
        S.step("act", "sig", lambda e, i: e.activation(raw[:, :, :], lg[:, :, :, 3], ACT.Sigmoid))
        S.step("act", "tau", lambda e, i: e.activation(tau[:, :], ltau[:, :], ACT.Exp))
        S.step("dve", "itau", lambda e, i: e.reciprocal(tau[:, :], tau[:, :]), ["act.tau"])
        S.step("dve", "scl", lambda e, i: e.tensor_tensor(
            oth[:, :, :, :], lg[:, :, :, 0:3], tau[:, :].unsqueeze(1).unsqueeze(3).to_broadcast([P, NT, H0, 3]), ALU.mult), ["dve.itau"])
        S.step("dve", "max", lambda e, i: e.tensor_reduce(mx[:, :, :], oth[:, :, :, :], AX.X, ALU.max), ["dve.scl"])
        S.step("dve", "sub", lambda e, i: e.tensor_tensor(
            oth[:, :, :, :], oth[:, :, :, :], mx[:, :, :].unsqueeze(3).to_broadcast([P, NT, H0, 3]), ALU.subtract), ["dve.max"])
        S.step("act", "exp", lambda e, i: e.activation(oth[:, :, :, :], oth[:, :, :, :], ACT.Exp), ["dve.sub"])
        S.step("dve", "sum", lambda e, i: e.tensor_reduce(tot[:, :, :], oth[:, :, :, :], AX.X, ALU.add), ["act.exp"])
        S.step("dve", "inv", lambda e, i: e.reciprocal(tot[:, :, :], tot[:, :, :]), ["dve.sum"])
        S.step("dve", "floor", lambda e, i: e.tensor_scalar(fl[:, :, :], raw[:, :, :], 0.09, 0.9, ALU.mult, ALU.add), ["act.sig"])
        S.step("dve", "pval", lambda e, i: e.tensor_tensor(raw[:, :, :], raw[:, :, :], fl[:, :, :], ALU.mult), ["dve.floor"])
        S.step("dve", "put", lambda e, i: e.tensor_copy(gates[:, :, :, 3], raw[:, :, :]), ["dve.pval"])
        S.step("dve", "rest", lambda e, i: e.tensor_scalar(fl[:, :, :], raw[:, :, :], -1.0, 1.0, ALU.mult, ALU.add), ["dve.pval"])
        S.step("dve", "scale", lambda e, i: e.tensor_tensor(tot[:, :, :], tot[:, :, :], fl[:, :, :], ALU.mult), ["dve.rest", "dve.inv"])
        S.step("dve", "ctx", lambda e, i: e.tensor_tensor(
            gates[:, :, :, 0:3], oth[:, :, :, :], tot[:, :, :].unsqueeze(3).to_broadcast([P, NT, H0, 3]), ALU.mult), ["dve.scale"])
        S.run()


def delta_mix(K, sb, F, dr, gates, wo, nw):
    with ExitStack() as ctx:
        fs = sb("fs", [P, 2, 6, P], c=ctx)
        pm = sb("pm", [P, 2, 4, D], c=ctx)
        ss = sb("ss", [P, NT, H0], c=ctx)
        sq = sb("sq2", [P, 2, D], c=ctx)
        S = Stage(K, "b0_mx", NT // 2)

        def by_head(ap):
            return ap.rearrange("p (h v) -> p h v", h=H0)

        def gate(i, s, g):
            return gates[:, tile_at(i, s), :, g].rearrange("p t h -> p (t h)").unsqueeze(2).to_broadcast([P, H0, DV0])
        for s in range(2):
            S.step("act", f"fs{s}", lambda e, i, s=s: e.activation(fs[:, s, :, :], F[:, :, cols_at(i, s)], ACT.Copy), [f"pe.T{s}<1"])

            def turns(e, i, s=s):
                for c in range(6):
                    done = e.transpose(K.ps[:, 2 * s + c // 4, (c % 4) * P:(c % 4 + 1) * P], fs[:, s, c, :], K.ident[:, :])
                return done
            S.step("pe", f"T{s}", turns, [f"act.fs{s}", f"dve.p2{s}<1"])
        for s in range(2):
            S.step("pool", f"p3{s}", lambda e, i, s=s: e.tensor_tensor(
                by_head(pm[:, s, 3, :]), dr[:, tile_at(i, s), :].rearrange("p t (h v) -> p (t h) v", h=H0), gate(i, s, 2), ALU.mult),
                [f"dve.a1{s}<1"], lag=1)
            for n, (col, g) in enumerate(((0, 3), (256, 0), (512, 1))):
                S.step("dve", f"p{n}{s}", lambda e, i, s=s, n=n, col=col, g=g: e.tensor_tensor(
                    by_head(pm[:, s, n, :]), by_head(K.ps[:, 2 * s + col // 512, col % 512:col % 512 + D]), gate(i, s, g), ALU.mult),
                    [f"pe.T{s}", f"dve.a1{s}<1"], lag=1)
        for s in range(2):
            S.step("dve", f"a0{s}", lambda e, i, s=s: e.tensor_tensor(
                pm[:, s, 0:2, :], pm[:, s, 0:2, :], pm[:, s, 2:4, :], ALU.add), [f"dve.p2{s}", f"pool.p3{s}"], lag=1)
            S.step("dve", f"a1{s}", lambda e, i, s=s: e.tensor_tensor(
                dr[:, tile_at(i, s), :], pm[:, s, 0:1, :], pm[:, s, 1:2, :], ALU.add), [f"dve.a0{s}"], lag=1)
            S.step("act", f"sq{s}", lambda e, i, s=s: e.activation(sq[:, s, :].unsqueeze(1), dr[:, tile_at(i, s), :], ACT.Square),
                   [f"dve.a1{s}", f"dve.ss{s}<1"], lag=1)
            S.step("dve", f"ss{s}", lambda e, i, s=s: e.tensor_reduce(
                ss[:, tile_at(i, s), :].rearrange("p t h -> p (t h)"), by_head(sq[:, s, :]), AX.X, ALU.add), [f"act.sq{s}"], lag=2)
        S.run()
        S = Stage(K, "b0_rm", 1)
        S.step("dve", "eps", lambda e, i: e.tensor_scalar(ss[:, :, :], ss[:, :, :], 1.0 / DV0, 1e-5, ALU.mult, ALU.add))
        S.step("act", "root", lambda e, i: e.activation(ss[:, :, :], ss[:, :, :], ACT.Sqrt), ["dve.eps"])
        S.step("dve", "inv", lambda e, i: e.reciprocal(ss[:, :, :], ss[:, :, :]), ["act.root"])
        S.run()
        S = Stage(K, "b0_o", NT // 2, oldest_first=True)
        for s in range(2):
            S.step("dve", f"n{s}", lambda e, i, s=s: e.tensor_tensor(
                by_head(K.xnb[:, s, :]), dr[:, tile_at(i, s), :].rearrange("p t (h v) -> p (t h) v", h=H0),
                ss[:, tile_at(i, s), :].rearrange("p t h -> p (t h)").unsqueeze(2).to_broadcast([P, H0, DV0]), ALU.mult), [f"pe.T{s}<1"])

            def turn_o(e, i, s=s):
                for c in range(DC):
                    done = e.transpose(K.ps[:, s, c * P:(c + 1) * P], K.xnb[:, s, c * P:(c + 1) * P], K.ident[:, :])
                return done
            S.step("pe", f"T{s}", turn_o, [f"dve.n{s}", f"act.T{s}<1"], lag=1)
            S.step("act", f"T{s}", lambda e, i, s=s: e.activation(
                K.xs[:, s, :, :], K.ps[:, s, 0:D].rearrange("p (c n) -> p c n", c=DC), ACT.Copy, scale=nw[:, 0:1]), [f"pe.T{s}", f"pe.mm{s}<1"], lag=1)
        for s in range(2):
            def product(e, i, s=s):
                for c in range(DC):
                    done = e.matmul(K.ps[:, 2 + s, 0:D], K.xs[:, s, c, :], wo[:, c, :], start=(c == 0), stop=(c == DC - 1))
                return done
            S.step("pe", f"mm{s}", product, [f"act.T{s}", f"dve.x{s}<1"], lag=2)
            S.step("dve", f"x{s}", lambda e, i, s=s: e.tensor_tensor(
                K.x[:, tile_at(i, s), :], K.x[:, tile_at(i, s), :], K.ps[:, 2 + s, 0:D].unsqueeze(1), ALU.add), [f"pe.mm{s}"], lag=3)
        S.run()


def top_ranks(S, prefix, rank, gt, eq, before, p, n, needs):
    T = p.shape[1]
    shape = [P, T, n, n]
    own = p.unsqueeze(3).to_broadcast(shape)
    other = p.unsqueeze(2).to_broadcast(shape)
    S.step("dve", prefix + "gt", lambda e, i: e.tensor_tensor(gt, other, own, ALU.is_gt), needs)
    S.step("dve", prefix + "eq", lambda e, i: e.tensor_tensor(eq, other, own, ALU.is_equal), needs)
    S.step("dve", prefix + "tie", lambda e, i: e.tensor_tensor(
        eq, eq, before.unsqueeze(1).to_broadcast(shape), ALU.mult), ["dve." + prefix + "eq"])
    S.step("dve", prefix + "or", lambda e, i: e.tensor_tensor(gt, gt, eq, ALU.add), ["dve." + prefix + "tie", "dve." + prefix + "gt"])
    S.step("dve", prefix + "rank", lambda e, i: e.tensor_reduce(rank, gt, AX.X, ALU.add), ["dve." + prefix + "or"])


def router_0(K, sb, rl, rank, gate, mx, tot, E):
    with ExitStack() as c1:
        gt, eq = (sb(n, [P, NT, E, E], c=c1) for n in ("gt", "eq"))
        def over(t):
            return t[:, :].unsqueeze(2).to_broadcast([P, NT, E])
        S = Stage(K, "f0_g", 1)
        S.step("dve", "max", lambda e, i: e.tensor_reduce(mx[:, :], rl[:, :, :], AX.X, ALU.max))
        S.step("dve", "sub", lambda e, i: e.tensor_tensor(rl[:, :, :], rl[:, :, :], over(mx), ALU.subtract), ["dve.max"])
        S.step("act", "exp", lambda e, i: e.activation(rl[:, :, :], rl[:, :, :], ACT.Exp), ["dve.sub"])
        S.step("dve", "sum", lambda e, i: e.tensor_reduce(tot[:, :], rl[:, :, :], AX.X, ALU.add), ["act.exp"])
        S.step("dve", "inv", lambda e, i: e.reciprocal(tot[:, :], tot[:, :]), ["dve.sum"])
        S.step("dve", "p", lambda e, i: e.tensor_tensor(rl[:, :, :], rl[:, :, :], over(tot), ALU.mult), ["dve.inv"])
        top_ranks(S, "e", rank[:, :, :], gt[:, :, :, :], eq[:, :, :, :], K.before[0:P, 0:E, 0:E], rl[:, :, :], E, ["dve.p"])
        S.step("dve", "pick", lambda e, i: e.scalar_tensor_tensor(
            gate[:, :, :], rank[:, :, :], 1.5, rl[:, :, :], ALU.is_lt, ALU.mult), ["dve.erank"])
        S.step("dve", "sum2", lambda e, i: e.tensor_reduce(tot[:, :], gate[:, :, :], AX.X, ALU.add), ["dve.pick"])
        S.step("dve", "inv2", lambda e, i: e.reciprocal(tot[:, :], tot[:, :]), ["dve.sum2"])
        S.step("dve", "gate", lambda e, i: e.tensor_tensor(gate[:, :, :], gate[:, :, :], over(tot), ALU.mult), ["dve.inv2"])
        S.run()


def experts_0(K):
    I = K.ins
    E, FC = 8, 8
    with ExitStack() as ctx:
        def sb(name, shape, dt=F32, c=ctx):
            return K.sb("f0_" + name, shape, dt, c)
        wr = sb("wr", [P, DC, E])
        xnH, xnL = (sb(n, [P, DC, ROWS], F32R) for n in ("xnH", "xnL"))
        rl, rank, gate = (sb(n, [P, NT, E]) for n in ("rl", "rank", "gate"))
        mx, tot = (sb(n, [P, NT]) for n in ("mx", "tot"))
        w_r = load(K, "f0_r", [wr[:, :, :]], [features(I["L0_ffn_WrT"])])
        row_stats(K, "f0_ln", K.x, 1e-5, [w_r])
        norm_transpose(K, "f0_nt", row_logits(K, wr, E, rl), (xnH, xnL))
        router_0(K, sb, rl, rank, gate, mx, tot, E)

        raw = sb("raw", [P, FC * D])
        w1 = [sb(f"w1{n}", [P, 2, DC, FC * P], F32R) for n in "HL"]
        w2 = [sb(f"w2{n}", [P, 2, FC, D], F32R) for n in "HL"]
        hr = sb("hr", [P, 4, 512])
        h = [sb(f"h{n}", [P, 2, FC, 512], F32R) for n in "HL"]
        S = Stage(K, "f0_e", E // 2)
        for s in range(2):
            for n, (w, source) in enumerate(((w1, "L0_ffn_W1T"), (w2, "L0_ffn_W2T"))):
                S.step("sp", f"w{n}{s}", lambda e, i, s=s, n=n, source=source: e.dma_start(
                    raw[:, :].rearrange("p (c m) -> p c m", c=DC if n == 0 else FC),
                    I[source][bass.ds(2 * i + s, 1), :, :].rearrange("e (c p) m -> p (e c) m", p=P)).then_inc(
                        S.dma[f"w{n}{s}"][0], 16), [f"pool.lo0{s}" if n else ("pool.lo11<1", "pool.lo10")[s]], dmas=1)
                flat = [t[:, s, :, :].rearrange("p c m -> p (c m)") for t in w]
                S.step("pool", f"hi{n}{s}", lambda e, i, flat=flat: e.tensor_copy(flat[0], raw[:, :]),
                       [f"sp.w{n}{s}", f"pe.y{4 * s + 3}_1<1"])
                S.step("pool", f"lo{n}{s}", lambda e, i, flat=flat: e.tensor_tensor(
                    flat[1], raw[:, :], flat[0].bitcast(F32), ALU.subtract), [f"pool.hi{n}{s}"])
        jobs = [(s, g) for s in range(2) for g in range(NG)]

        def hidden(n):
            s, g = jobs[n]
            for f in range(FC):
                def product(e, i, f=f):
                    for c in range(DC):
                        done = product3(e, K.ps[:, f % 4, :], [w[:, s, c, f * P:(f + 1) * P] for w in w1],
                                        [x[:, c, g * 512:(g + 1) * 512] for x in (xnH, xnL)], c == 0, c == DC - 1)
                    return done
                free = f"act.h{n}_{f - 4}" if f >= 4 else f"act.h{n - 1}_{f + 4}" if n else f"act.h{len(jobs) - 1}_{f + 4}<1"
                S.step("pe", f"h{n}_{f}", product, [free, f"pool.lo0{s}"])
                drawn = f"dve.l{n}_{f - 4}" if f >= 4 else f"dve.l{n - 1}_{f + 4}" if n else f"dve.l{len(jobs) - 1}_{f + 4}<1"
                S.step("act", f"h{n}_{f}", lambda e, i, f=f: e.activation(hr[:, f % 4, :], K.ps[:, f % 4, :], ACT.Silu),
                       [f"pe.h{n}_{f}", drawn])
                if f:
                    high(n, f - 1)
            high(n, FC - 1)

        def high(n, f):
            S.step("act", f"g{n}_{f}", lambda e, i: e.activation(h[0][:, n % 2, f, :], hr[:, f % 4, :], ACT.Copy),
                   [f"act.h{n}_{f}", f"pe.y{n - 2}_1" if n >= 2 else f"pe.y{n + 6}_1<1"])
            S.step("dve", f"l{n}_{f}", lambda e, i: e.tensor_tensor(
                h[1][:, n % 2, f, :], hr[:, f % 4, :], h[0][:, n % 2, f, :].bitcast(F32), ALU.subtract), [f"act.g{n}_{f}"])

        def outputs(n):
            s, g = jobs[n]
            for half in range(2):
                bank = 4 + 2 * (n % 2) + half

                def product(e, i, half=half, bank=bank):
                    for t in range(2):
                        for f in range(FC):
                            at = (2 * half + t) * P
                            done = product3(e, K.ps[:, bank, t * D:(t + 1) * D], [x[:, n % 2, f, at:at + P] for x in h],
                                            [w[:, s, f, :] for w in w2], f == 0, f == FC - 1)
                    return done
                S.step("pe", f"y{n}_{half}", product,
                       [f"dve.l{n}_7", f"pool.lo1{s}", f"dve.y{n - 2}_{half}" if n >= 2 else f"dve.y{n + 6}_{half}<1"])

                def add(e, i, half=half, bank=bank):
                    for t in range(2):
                        row = 4 * g + 2 * half + t
                        done = e.scalar_tensor_tensor(K.x[:, row, :], K.ps[:, bank, t * D:(t + 1) * D],
                                                      gate[:, row, bass.ds(2 * i + s, 1)], K.x[:, row, :], ALU.mult, ALU.add)
                    return done
                S.step("dve", f"y{n}_{half}", add, [f"pe.y{n}_{half}"])
        hidden(0)
        for n in range(len(jobs)):
            if n + 1 < len(jobs):
                hidden(n + 1)
            outputs(n)
        S.run()


def cross_attention_1(K):
    I = K.ins
    HG = 4
    with ExitStack() as ctx:
        def sb(name, shape, dt=F32, c=ctx):
            return K.sb("a1_" + name, shape, dt, c)
        K.xnT = sb("xnT", [P, DC, ROWS])
        K.stage = sb("stage", [P, 2, DC, P])
        wq, wk, wv, wo = (sb(n, [P, DC, D]) for n in ("wq", "wk", "wv", "wo"))
        bq, bk, bv = (sb(n, [P, DC]) for n in ("bq", "bk", "bv"))
        bo = sb("bo", [P, D])
        qT = sb("qT", [P, DC, ROWS])
        NE = NK + 1
        ctxT = sb("ctxT", [P, 2, DC, NE])
        cs = [sb(f"ctx{n}", [P, 2, DC, NE], F32R) for n in "HL"]
        wks, wvs = ([sb(f"{w}{n}", [P, DC, D], F32R) for n in "HL"] for w in ("wk", "wv"))
        qb = sb("qb", [P, 2, DC, 8, L])
        kT = sb("kT", [P, 2, DC, NK])
        v = sb("v", [P, 2, 2, D])
        vL = sb("vL", [P, 2, D])
        pr = sb("pr", [P, 2, HG, NK])
        prT = sb("prT", [P, 2, 2, HG, P])
        neg, tot, inv = (sb(n, [P, 2, HG]) for n in ("neg", "tot", "inv"))
        mr = sb("mr", [P, 2, HG, 64])
        mo = sb("mo", [P, 2, HG, 64])
        w_a = load(K, "a1", [wq[:, :, :], wk[:, :, :], wv[:, :, :], wo[:, :, :], bq[:, :], bk[:, :], bv[:, :], bo[:, :]],
                   [features(I["L1_xattn_" + n + "T"]) for n in ("Wq", "Wk", "Wv", "Wo")]
                   + [I["L1_xattn_" + n] for n in ("bq", "bk", "bv")] + [I["L1_xattn_bo"].partition_broadcast(P)])
        row_stats(K, "a1_ln", K.x, 1e-5)
        norm_transpose(K, "a1_nt", wait=w_a)

        def q_finish(m):
            return "dve", lambda e, i, ps, m=m: e.tensor_scalar(
                qT[:, m, bass.ds(i * 512, 512)], ps, bq[:, m:m + 1], 0.25, ALU.add, ALU.mult)
        feature_gemm(K, "a1_q", qT, wq, rows_of(K.xnT), DC, DC, q_finish, [w_a])

        S = Stage(K, "a1_w", 1)
        for name, w, parts in (("k", wk, wks), ("v", wv, wvs)):
            split(S, "pool", "dve", name, w[:, :, :], [t[:, :, :] for t in parts], [], [])
        S.step("pool", "even", lambda e, i: e.memset(ctxT[:, :, :, NK:NE], 0.0))
        S.run()
        S = Stage(K, "a1_at", B // 2)

        def cols(i, s):
            return bass.ds((2 * i + s) * L, L)

        def load_context(s):
            S.step("sp", f"ctx{s}", lambda e, i: e.dma_start(
                ctxT[:, s, :, 0:NK], I["ctxT"][bass.ds(2 * i + s, 1), :, :].rearrange("b (c p) k -> p (b c) k", p=P)).then_inc(
                    S.dma[f"ctx{s}"][0], 16), [f"dve.lctx{s}<1"], dmas=1)

        def split_context(s, lag):
            split(S, "act", "dve", f"ctx{s}", ctxT[:, s, :, :], [t[:, s, :, :] for t in cs], [f"sp.ctx{s}"], [f"pe.VL{s}<1"], lag)

        def queries(s):
            for c in range(DC):
                S.step("pool", f"q{c}{s}", lambda e, i, c=c: e.tensor_tensor(
                    qb[:, s, c, :, :], qT[:, c, cols(i, s)].unsqueeze(1).to_broadcast([P, 8, L]),
                    K.head16.unsqueeze(2).to_broadcast([P, 8, L]), ALU.mult), [f"pe.S{s}<1"], lag=1)

        def keys(s):
            def emit(e, i):
                for m in range(DC):
                    for c in range(DC):
                        done = product3(e, K.ps[:, 4 + m, 0:NE], [w[:, c, m * P:(m + 1) * P] for w in wks],
                                        [t[:, s, c, :] for t in cs], c == 0, c == DC - 1)
                return done
            S.step("pe", f"K{s}", emit, [f"dve.lctx{s}", f"dve.T{s}<1", f"act.T{s}<1"], lag=1)
            for c in range(DC):
                S.step("act", f"K{c}{s}", lambda e, i, c=c: e.activation(
                    kT[:, s, c, :], K.ps[:, 4 + c, 0:NK], ACT.Identity, bias=bk[:, c:c + 1]), [f"pe.K{s}", f"pe.S{s}<1"], lag=1)

        def values(s):
            def emit(e, i):
                for t in range(2):
                    for c in range(DC):
                        done = product3(e, K.ps[:, 6, t * D:(t + 1) * D], [x[:, s, c, t * P:(t + 1) * P] for x in cs],
                                        [w[:, c, :] for w in wvs], c == 0, c == DC - 1)
                return done
            S.step("pe", f"V{s}", emit, ["dve.V1<1" if s == 0 else "dve.V0"], lag=1)
            S.step("dve", f"V{s}", lambda e, i: e.tensor_copy(
                v[:, s, :, :], K.ps[:, 6, :].rearrange("p (t d) -> p t d", t=2)),
                [f"pe.V{s}", f"pe.P{s}<1"], lag=1)

        def last_value(s):
            def emit(e, i):
                for c in range(DC):
                    done = product3(e, K.ps[:, 7, 0:D], [x[:, s, c, 2 * P:NK].to_broadcast([P, P]) for x in cs],
                                    [w[:, c, :] for w in wvs], c == 0, c == DC - 1)
                return done
            S.step("pe", f"VL{s}", emit, [f"act.O{s}<1"], lag=1)
            S.step("dve", f"VL{s}", lambda e, i: e.tensor_copy(vL[:, s, :], K.ps[:, 7, 0:D]), [f"pe.VL{s}", f"dve.U{s}<1"], lag=1)

        def scores(s):
            def emit(e, i):
                for g in range(HG):
                    done = e.matmul(K.ps[:, g, 0:NK], qb[:, s, g // 2, 4 * (g % 2):4 * (g % 2) + 4, :].rearrange("p h q -> p (h q)"),
                                    kT[:, s, g // 2, :], start=True, stop=True)
                return done
            S.step("pe", f"S{s}", emit, [f"pool.q1{s}", f"act.K1{s}", "act.e3_1<1" if s == 0 else "act.e3_0"], lag=1)
            S.step("dve", f"mx{s}", lambda e, i: e.tensor_reduce(neg[:, s, :], K.ps[:, 0:HG, 0:NK], AX.X, ALU.max, negate=True),
                   [f"pe.S{s}", f"act.e3_{s}<1"], lag=1)
            for g in range(HG):
                S.step("act", f"e{g}_{s}", lambda e, i, g=g: e.activation(
                    pr[:, s, g, :], K.ps[:, g, 0:NK], ACT.Exp, bias=neg[:, s, g:g + 1], accum_out=tot[:, s, g:g + 1]),
                    [f"dve.mx{s}", f"dve.inv{s}<1", f"pe.T{s}<1", f"dve.U{s}<1"], lag=1)

        def inverses(s):
            S.step("dve", f"inv{s}", lambda e, i: e.reciprocal(inv[:, s, :], tot[:, s, :]), [f"act.e3_{s}", f"pool.mr{s}<1"], lag=1)
            S.step("pool", f"mr{s}", lambda e, i: e.tensor_tensor(
                mr[:, s, :, :], K.diag16.unsqueeze(1).to_broadcast([P, HG, 64]), inv[:, s, :].unsqueeze(2).to_broadcast([P, HG, 64]),
                ALU.mult), [f"dve.inv{s}", f"dve.M{s}<1"], lag=1)

        def turn_probs(s, lag):
            ahead = "<-1" if lag == 2 else ""
            def emit(e, i):
                for t in range(2):
                    for g in range(HG):
                        done = e.transpose(K.ps[:, 4 + t, g * P:(g + 1) * P], pr[:, s, g, t * P:(t + 1) * P], K.ident[:, :])
                return done
            S.step("pe", f"T{s}", emit, [f"act.e3_{s}", f"act.K1{1 - s}{ahead}"], lag=lag)
            S.step("dve", f"T{s}", lambda e, i: e.tensor_copy(
                prT[:, s, 0, :, :], K.ps[:, 4, :].rearrange("p (g n) -> p g n", g=HG)), [f"pe.T{s}", f"pe.P{s}<1"], lag=lag)
            S.step("act", f"T{s}", lambda e, i: e.activation(
                prT[:, s, 1, :, :], K.ps[:, 5, :].rearrange("p (g n) -> p g n", g=HG), ACT.Copy), [f"pe.T{s}", f"pe.P{s}<1"], lag=lag)

        def weigh(s, lag):
            ahead = "<-1" if lag == 2 else ""
            def emit(e, i):
                for g in range(HG):
                    out = K.ps[:, 7, D + 64 * g:D + 64 * g + 64]
                    own = slice(64 * g, 64 * g + 64)
                    e.matmul(out, prT[:, s, 0, g, :], v[:, s, 0, own], start=True, stop=False)
                    done = e.matmul(out, prT[:, s, 1, g, :], v[:, s, 1, own], start=False, stop=True)
                return done
            S.step("pe", f"P{s}", emit, [f"dve.T{s}", f"act.T{s}", f"dve.VL{1 - s}{ahead}"], lag=lag)

            def add_last(e, i):
                for g in range(HG):
                    own = slice(64 * g, 64 * g + 64)
                    done = e.scalar_tensor_tensor(mo[:, s, g, :], vL[:, s, own], pr[:, s, g, NK - 1:NK],
                                                  K.ps[:, 7, D + 64 * g:D + 64 * g + 64], ALU.mult, ALU.add)
                return done
            S.step("dve", f"U{s}", add_last, [f"pe.P{s}", f"dve.VL{s}", f"pe.O{s}<1"], lag=lag)
            S.step("dve", f"M{s}", lambda e, i: e.tensor_tensor(mo[:, s, :, :], mo[:, s, :, :], mr[:, s, :, :], ALU.mult),
                   [f"dve.U{s}", f"pool.mr{s}"], lag=lag)

        def outputs(s):
            def emit(e, i):
                for g in range(HG):
                    half = slice(64 * (g % 2), 64 * (g % 2) + 64)
                    done = e.matmul(K.ps[half, 7, L * (g // 2):L * (g // 2) + L], mo[:, s, g, :], K.eye, start=True, stop=True)
                return done
            S.step("pe", f"O{s}", emit, [f"dve.M{s}"], lag=2)

            def bias(e, i):
                for c in range(DC):
                    done = e.activation(qT[:, c, cols(i, s)], K.ps[:, 7, L * c:L * c + L], ACT.Identity, bias=bv[:, c:c + 1])
                return done
            S.step("act", f"O{s}", bias, [f"pe.O{s}"], lag=2)
        load_context(0)
        load_context(1)
        queries(0)
        queries(1)
        keys(0)
        values(0)
        outputs(0)
        turn_probs(1, 2)
        last_value(0)
        split_context(1, 1)
        scores(0)
        weigh(1, 2)
        inverses(0)
        keys(1)
        values(1)
        outputs(1)
        turn_probs(0, 1)
        last_value(1)
        split_context(0, 0)
        scores(1)
        weigh(0, 1)
        inverses(1)
        S.run()

        def add_bo(S):
            for s in range(2):
                S.step("pool", f"bo{s}", lambda e, i, s=s: e.tensor_tensor(
                    K.x[:, tile_at(i, s), :], K.x[:, tile_at(i, s), :], bo[:, :].unsqueeze(1), ALU.add))
        output_rows(K, "a1_o", qT, wo, DC, lambda e, t, ps: e.tensor_tensor(
            K.x[:, t, :], K.x[:, t, :], ps.unsqueeze(1), ALU.add), pre=add_bo, after="pool.bo{s}")


def self_attention(K):
    I = K.ins
    HQ, HT, W = 16, 20, 64
    with ExitStack() as ctx:
        def sb(name, shape, dt=F32, c=ctx):
            return K.sb("s_" + name, shape, dt, c)
        K.xnT = sb("xnT", [P, DC, ROWS])
        K.stage = sb("stage", [P, 2, 8, P])
        w = sb("w", [P, DC, 3 * 512])
        wo = sb("wo", [P, 8, D])
        rope = sb("rope", [P, 2, W])
        nw = sb("nw", [P, 2, W])
        cw, sw = (sb(n, [P, HT, W]) for n in ("cw", "sw"))
        qkT = sb("qkT", [P, 10, ROWS])
        vr = sb("vr", [P, NT, D])
        w_a = load(K, "s_w", [w[:, :, :], rope[:, :, :], nw[:, 0, :], nw[:, 1, :]],
                   [features(I["L1_attn_WqkvT"]), I["rope"], I["L1_attn_q_norm_w"].partition_broadcast(P),
                    I["L1_attn_k_norm_w"].partition_broadcast(P)])
        w_o = load(K, "s_wo", [wo[:, :, :]], [features(I["L1_attn_WoT"])])
        row_stats(K, "s_ln", K.x, 1e-5)
        norm_transpose(K, "s_nt", wait=w_a)

        S = Stage(K, "s_tab", 1)
        for n, (lo, hi) in enumerate(((0, HQ), (HQ, HT))):
            heads = [P, hi - lo, W]
            S.step("dve", f"c{n}", lambda e, i, n=n, lo=lo, hi=hi, heads=heads: e.tensor_tensor(
                cw[:, lo:hi, :], rope[:, 0:1, :].to_broadcast(heads), nw[:, n:n + 1, :].to_broadcast(heads), ALU.mult))
            for h in range(2):
                a, b = slice(32 * h, 32 * h + 32), slice(32 - 32 * h, 64 - 32 * h)
                part = [P, hi - lo, 32]
                S.step("dve", f"s{n}{h}", lambda e, i, n=n, lo=lo, hi=hi, a=a, b=b, part=part: e.tensor_tensor(
                    sw[:, lo:hi, a], rope[:, 1:2, a].to_broadcast(part), nw[:, n:n + 1, b].to_broadcast(part), ALU.mult))
        S.run()

        with ExitStack() as c1:
            sq = sb("sq", [P, HT * W], c=c1)
            ta, tb = (sb(n, [P, HT, W], c=c1) for n in ("ta", "tb"))
            tr = sb("tr", [P, 2, HT, W], c=c1)
            ss = sb("ss", [P, 2, HT], c=c1)
            S = Stage(K, "s_qk", NT // 2)
            S.before("pe", lambda e: None, [w_a])
            half = [slice(0, 32), slice(32, 64)]

            def banks(s):
                return K.ps[:, 3 * s:3 * s + 3, :].rearrange("p b n -> p (b n)")[:, 0:HT * W].rearrange("p (h n) -> p h n", n=W)

            def stage_in(s):
                S.step("pool", f"st{s}", lambda e, i: e.tensor_copy(K.stage[:, s, 0:DC, :], K.xnT[:, :, cols_at(i, s)]),
                       [f"pe.mb{s}<1"])

            def project(s):
                for name, parts, needs in (("ma", (0, 1), [f"pool.st{s}", f"dve.r1{s}<1", f"act.v{s}<1"]),
                                           ("mb", (2,), ["act.T1<2" if s == 0 else "act.T0<1"])):
                    def emit(e, i, parts=parts):
                        for n in parts:
                            for c in range(DC):
                                done = e.matmul(K.ps[:, 3 * s + n, :], K.stage[:, s, c, :], w[:, c, n * 512:(n + 1) * 512],
                                                start=(c == 0), stop=(c == DC - 1))
                        return done
                    S.step("pe", f"{name}{s}", emit, needs)

            def squares(s, lag):
                was = f"dve.ss{1 - s}" + ("<1" if s == 0 else "")
                S.step("act", f"sq{s}", lambda e, i: e.activation(
                    sq[:, :].rearrange("p (h n) -> p h n", n=W), banks(s), ACT.Square), [f"pe.mb{s}", was], lag=lag)
                S.step("act", f"v{s}", lambda e, i: e.activation(
                    vr[:, tile_at(i, s), :], K.ps[:, 3 * s + 2, D:2 * D].unsqueeze(1), ACT.Copy), [f"pe.mb{s}"], lag=lag)

            def rotate(s, lag):
                was = f"pool.ad{1 - s}" + ("<1" if s == 0 else "")
                S.step("dve", f"c{s}", lambda e, i: e.tensor_tensor(ta[:, :, :], banks(s), cw[:, :, :], ALU.mult),
                       [f"act.v{s}", was], lag=lag)
                for h in range(2):
                    S.step("dve", f"r{h}{s}", lambda e, i, h=h: e.tensor_tensor(
                        tb[:, :, half[h]], banks(s)[:, :, half[1 - h]], sw[:, :, half[h]], ALU.mult), [f"act.v{s}", was], lag=lag)
                S.step("dve", f"ss{s}", lambda e, i: e.tensor_reduce(
                    ss[:, s, :], sq[:, :].rearrange("p (h n) -> p h n", n=W), AX.X, ALU.add), [f"act.sq{s}", f"dve.n{s}<1"], lag=lag)
                S.step("dve", f"ep{s}", lambda e, i: e.tensor_scalar(
                    ss[:, s, :], ss[:, s, :], 1.0 / W, 1e-6, ALU.mult, ALU.add), [f"dve.ss{s}"], lag=lag)
                S.step("pool", f"ad{s}", lambda e, i: e.tensor_tensor(tr[:, s, :, :], ta[:, :, :], tb[:, :, :], ALU.add),
                       [f"dve.r1{s}", f"pe.T{s}<1"], lag=lag)

            def root(s, lag):
                S.step("act", f"rt{s}", lambda e, i: e.activation(ss[:, s, :], ss[:, s, :], ACT.Sqrt), [f"dve.ep{s}"], lag=lag)

            def normalise(s):
                S.step("dve", f"iv{s}", lambda e, i: e.reciprocal(ss[:, s, :], ss[:, s, :]), [f"act.rt{s}"], lag=1)
                S.step("dve", f"n{s}", lambda e, i: e.tensor_tensor(
                    tr[:, s, :, :], tr[:, s, :, :], ss[:, s, :].unsqueeze(2).to_broadcast([P, HT, W]), ALU.mult),
                    [f"dve.iv{s}", f"pool.ad{s}"], lag=1)

            def turns(s):
                def emit(e, i):
                    for c in range(10):
                        out = (K.ps[:, 6 + c // 4, (c % 4) * P:(c % 4 + 1) * P] if c < 8 else
                               K.ps[:, 3 * (1 - s) + 2, D + (c - 8) * P:D + (c - 7) * P])
                        done = e.transpose(out, tr[:, s, 2 * c:2 * c + 2, :].rearrange("p h n -> p (h n)"), K.ident[:, :])
                    return done
                S.step("pe", f"T{s}", emit, [f"dve.n{s}", "act.T1<1" if s == 0 else "act.T0",
                                             "dve.r11" if s == 0 else "dve.r10<-1"], lag=1)

            def take(s):
                def emit(e, i):
                    e.activation(qkT[:, 8:10, cols_at(i, s)],
                                 K.ps[:, 3 * (1 - s) + 2, D:2 * D].rearrange("p (c n) -> p c n", n=P), ACT.Copy)
                    return e.activation(qkT[:, 0:8, cols_at(i, s)], K.ps[:, 6:8, :].rearrange("p b (c n) -> p (b c) n", n=P), ACT.Copy)
                S.step("act", f"T{s}", emit, [f"pe.T{s}"], lag=1 + s)
            stage_in(0)
            stage_in(1)
            project(0)
            squares(1, 1)
            take(1)
            rotate(1, 1)
            root(1, 1)
            normalise(0)
            turns(0)
            squares(0, 0)
            project(1)
            rotate(0, 0)
            take(0)
            root(0, 0)
            normalise(1)
            turns(1)
            S.run()

        qs = sb("qs", [P, 2, 10, P])
        vs = sb("vs", [P, 2, D])
        sc, pt, pn = (sb(n, [P, 2, 2, 8, L]) for n in ("sc", "pt", "pn"))
        mx, tot = (sb(n, [P, 2, 2, 8]) for n in ("mx", "tot"))
        oT = K.stage
        S = Stage(K, "s_at", NT // 2)
        S.before("pe", lambda e: None, [w_o])

        def stage_in(s):
            S.step("act", f"q{s}", lambda e, i: e.activation(qs[:, s, :, :], qkT[:, :, cols_at(i, s)], ACT.Copy), [f"pe.S{s}<1"])
            S.step("pool", f"v{s}", lambda e, i: e.tensor_copy(vs[:, s, :].unsqueeze(1), vr[:, tile_at(i, s), :]),
                   [f"pe.O{s}<1"], lag=1)

        def scores(s):
            def emit(e, i):
                for c in range(8):
                    for r in range(2):
                        rows = slice(W * r, W * r + W)
                        for b in range(BT):
                            own = slice(L * b, L * b + L)
                            done = e.matmul(K.ps[own, 2 * s + r, L * c:L * c + L], qs[rows, s, c, own],
                                            qs[rows, s, 8 + c // 4, own], start=True, stop=True)
                return done
            S.step("pe", f"S{s}", emit, [f"act.q{s}", f"dve.x{s}<2"])

        def flat(t, s):
            return t[:, s, :, :, :].rearrange("p r c k -> p (r c) k")

        def exponents(s):
            view = K.ps[:, 2 * s:2 * s + 2, 0:256].rearrange("p r (c k) -> p r c k", k=L)
            S.step("dve", f"mx{s}", lambda e, i: e.tensor_reduce(mx[:, s, :, :], view, AX.X, ALU.max), [f"pe.S{s}"])
            S.step("dve", f"sb{s}", lambda e, i: e.tensor_tensor(
                sc[:, s, :, :, :], view, mx[:, s, :, :].unsqueeze(3).to_broadcast([P, 2, 8, L]), ALU.subtract),
                [f"dve.mx{s}", f"pool.pn{s}<1"])
            S.step("act", f"ex{s}", lambda e, i: e.activation(flat(sc, s), flat(sc, s), ACT.Exp), [f"dve.sb{s}"])

        def sums(s):
            S.step("dve", f"su{s}", lambda e, i: e.tensor_reduce(
                tot[:, s, :, :].rearrange("p r c -> p (r c)"), flat(sc, s), AX.X, ALU.add), [f"act.ex{s}", f"pool.pn{s}<1"], lag=1)
            S.step("dve", f"iv{s}", lambda e, i: e.reciprocal(tot[:, s, :, :], tot[:, s, :, :]), [f"dve.su{s}"], lag=1)
            S.step("pool", f"pn{s}", lambda e, i: e.tensor_tensor(
                flat(pn, s), flat(sc, s), tot[:, s, :, :].rearrange("p r c -> p (r c)").unsqueeze(2).to_broadcast([P, 16, L]), ALU.mult),
                [f"dve.iv{s}", f"dve.pt{s}<1"], lag=1)

        def turn_probs(s):
            S.step("dve", f"pt{s}", lambda e, i: e.transpose(
                pt[:, s, :, :, :].rearrange("p r c k -> p (r c k)"), pn[:, s, :, :, :].rearrange("p r c k -> p (r c k)")),
                [f"pool.pn{s}", f"pe.O{s}<1"], lag=1)

        def weigh(s):
            was, o = ("<1" if s == 0 else ""), 1 - s

            def emit(e, i):
                for g in range(2):
                    for r in range(2):
                        for b in range(BT):
                            rows = slice(L * b, L * b + L)
                            done = e.matmul(K.ps[W * r:W * r + W, 4 + b, P * g:P * g + P], vs[rows, s, (2 * g + r) * W:(2 * g + r + 1) * W],
                                            pt[rows, s, r, 4 * g:4 * g + 4, :].rearrange("p c q -> p (c q)"), start=True, stop=True)
                return done
            S.step("pe", f"O{s}", emit, [f"dve.pt{s}", f"pool.v{s}", f"act.o{o}{was}", f"dve.o{o}{was}"], lag=1)
            for key, lo in (("act", 0), ("dve", 2)):
                S.step(key, f"o{s}", lambda e, i, lo=lo: copy(
                    e, oT[:, s, :, :].rearrange("p c (b q) -> p c b q", b=BT)[:, :, lo:lo + 2, :],
                    K.ps[:, 4 + lo:6 + lo, 0:256].rearrange("p b (c q) -> p c b q", q=L)), [f"pe.O{s}", f"pe.W{s}<1"], lag=1)

        def project(s):
            def emit(e, i):
                for c in range(8):
                    done = e.matmul(K.ps[:, 2 * s, D:2 * D], oT[:, s, c, :], wo[:, c, :], start=(c == 0), stop=(c == 7))
                return done
            S.step("pe", f"W{s}", emit, [f"act.o{s}", f"dve.o{s}", f"dve.sb{s}<-1"], lag=1)

        def residual(s):
            S.step("dve", f"x{s}", lambda e, i: e.tensor_tensor(
                K.x[:, tile_at(i, s), :], K.x[:, tile_at(i, s), :], K.ps[:, 2 * s, D:2 * D].unsqueeze(1), ALU.add),
                [f"pe.W{s}"], lag=2)
        for part, s in ((stage_in, 0), (stage_in, 1), (sums, 0), (sums, 1), (turn_probs, 0), (residual, 0), (residual, 1),
                        (scores, 0), (weigh, 0),                        (exponents, 0), (turn_probs, 1), (scores, 1), (weigh, 1), (exponents, 1), (project, 0), (project, 1)):
            part(s)
        S.run()


def experts_1(K):
    I = K.ins
    E, G, EA = 16, 4, 20
    with ExitStack() as ctx:
        def sb(name, shape, dt=F32, c=ctx):
            return K.sb("g_" + name, shape, dt, c)
        wr = sb("wr", [P, DC, E])
        bias = sb("bias", [P, E])
        xnH, xnL = (sb(n, [P, DC, ROWS], F32R) for n in ("xnH", "xnL"))
        raw = sb("raw", [P, 2, 2 * D])
        w1 = [sb(f"w1{n}", [P, 2, 2 * D], F32R) for n in "HL"]
        s_, sc, rank = (sb(n, [P, NT, E]) for n in ("s", "sc", "rank"))
        gate = sb("gate", [P, NT, EA])
        gt, eq = (sb(n, [P, NT * E * E]) for n in ("gt", "eq"))
        gs, gr = (sb(n, [P, NT, G]) for n in ("gs", "gr"))
        tot = sb("tot", [P, NT])
        r, hr = (sb(n, [P, 2, 512]) for n in ("r", "hr"))
        h = [sb(f"h{n}", [P, 4, 512], F32R) for n in "HL"]
        w_r = load(K, "g_r", [wr[:, :, :], bias[:, :]], [features(I["L1_ffn_gate_wT"]), I["L1_ffn_bias_e"].partition_broadcast(P)])
        row_stats(K, "g_ln", K.x, 1e-5, [w_r])
        norm_transpose(K, "g_nt", row_logits(K, wr, E, s_), (xnH, xnL))

        def grouped(t):
            return t[:, :, :].rearrange("p t (g e) -> p (t g) e", g=G)

        def square(t, a, n):
            return t[:, 0:a * n * n].rearrange("p (a n m) -> p a n m", n=n, m=n)
        S = Stage(K, "g_g", 1)
        S.step("act", "sig", lambda e, i: e.activation(s_[:, :, :], s_[:, :, :], ACT.Sigmoid))
        S.step("dve", "sc", lambda e, i: e.tensor_tensor(
            sc[:, :, :], s_[:, :, :], bias[:, :].unsqueeze(1).to_broadcast([P, NT, E]), ALU.add), ["act.sig"])
        top_ranks(S, "a", grouped(rank), square(gt, NT * G, 4), square(eq, NT * G, 4), K.before[:, 0:4, 0:4], grouped(sc), 4, ["dve.sc"])
        S.step("dve", "two", lambda e, i: e.scalar_tensor_tensor(
            rank[:, :, :], rank[:, :, :], 1.5, sc[:, :, :], ALU.is_lt, ALU.mult), ["dve.arank"])
        S.step("dve", "gs", lambda e, i: e.tensor_reduce(
            gs[:, :, :].rearrange("p t g -> p (t g)"), grouped(rank), AX.X, ALU.add), ["dve.two"])
        top_ranks(S, "b", gr[:, :, :], square(gt, NT, G), square(eq, NT, G), K.before[:, 0:G, 0:G], gs[:, :, :], G, ["dve.gs"])
        S.step("dve", "in", lambda e, i: e.tensor_scalar(gr[:, :, :], gr[:, :, :], 1.5, None, ALU.is_lt), ["dve.brank"])
        S.step("dve", "msk", lambda e, i: e.tensor_tensor(
            grouped(sc), grouped(sc), gr[:, :, :].rearrange("p t g -> p (t g)").unsqueeze(2).to_broadcast([P, NT * G, 4]), ALU.mult), ["dve.in"])
        top_ranks(S, "c", rank[:, :, :], square(gt, NT, E), square(eq, NT, E), K.before[:, :, :], sc[:, :, :], E, ["dve.msk"])
        S.step("dve", "pick", lambda e, i: e.scalar_tensor_tensor(
            rank[:, :, :], rank[:, :, :], 3.5, s_[:, :, :], ALU.is_lt, ALU.mult), ["dve.crank"])
        S.step("dve", "sum", lambda e, i: e.tensor_reduce(tot[:, :], rank[:, :, :], AX.X, ALU.add), ["dve.pick"])
        S.step("dve", "eps", lambda e, i: e.tensor_scalar(tot[:, :], tot[:, :], 1e-20, None, ALU.add), ["dve.sum"])
        S.step("dve", "inv", lambda e, i: e.reciprocal(tot[:, :], tot[:, :]), ["dve.eps"])
        S.step("dve", "x25", lambda e, i: e.tensor_scalar(tot[:, :], tot[:, :], 2.5, None, ALU.mult), ["dve.inv"])
        S.step("dve", "gate", lambda e, i: e.tensor_tensor(
            gate[:, :, 0:E], rank[:, :, :], tot[:, :].unsqueeze(2).to_broadcast([P, NT, E]), ALU.mult), ["dve.x25"])
        S.step("dve", "one", lambda e, i: e.memset(gate[:, :, E:EA], 1.0))
        S.run()

        S = Stage(K, "g_e", EA // 2)
        for s in range(2):
            def loads(e, i, s=s):
                sem = S.dma[f"w{s}"][0]
                e.dma_start(raw[:, s, 0:D].rearrange("p (c f) -> p c f", c=DC), I["L1_ffn_upT"][bass.ds(2 * i + s, 1), :, :].rearrange(
                    "e (c p) f -> p (e c) f", p=P)).then_inc(sem, 16)
                e.dma_start(raw[:, s, D:2 * D].unsqueeze(1), I["L1_ffn_downT"][bass.ds(2 * i + s, 1), :, :].rearrange(
                    "e p d -> p e d")).then_inc(sem, 16)
            S.step("sp", f"w{s}", loads, [f"pool.lo{s}<1"], dmas=2)
            S.step("pool", f"hi{s}", lambda e, i, s=s: e.tensor_copy(w1[0][:, s, :], raw[:, s, :]), [f"sp.w{s}", f"pe.y{4 * s + 3}_1<1"])
            S.step("pool", f"lo{s}", lambda e, i, s=s: e.tensor_tensor(
                w1[1][:, s, :], raw[:, s, :], w1[0][:, s, :].bitcast(F32), ALU.subtract), [f"pool.hi{s}"])
        jobs = [(s, g) for s in range(2) for g in range(NG)]

        def earlier(name, n, back):
            return name.format(n - back) if n >= back else name.format(n - back + len(jobs)) + "<1"

        def hidden(n):
            s, g = jobs[n]

            def product(e, i):
                for c in range(DC):
                    done = product3(e, K.ps[:, n % 4, :], [w[:, s, c * P:(c + 1) * P] for w in w1],
                                    [x[:, c, g * 512:(g + 1) * 512] for x in (xnH, xnL)], c == 0, c == DC - 1)
                return done
            S.step("pe", f"h{n}", product, [earlier("act.r{}", n, 4), f"pool.lo{s}"])
            S.step("act", f"r{n}", lambda e, i: e.activation(r[:, n % 2, :], K.ps[:, n % 4, :], ACT.Relu),
                   [f"pe.h{n}"])
            S.step("act", f"h{n}", lambda e, i: e.activation(hr[:, n % 2, :], r[:, n % 2, :], ACT.Square),
                   [f"act.r{n}", earlier("dve.l{}", n, 2)])
            S.step("act", f"g{n}", lambda e, i: e.activation(h[0][:, n % 4, :], hr[:, n % 2, :], ACT.Copy),
                   [f"act.h{n}", earlier("pe.y{}_1", n, 4)])
            S.step("dve", f"l{n}", lambda e, i: e.tensor_tensor(
                h[1][:, n % 4, :], hr[:, n % 2, :], h[0][:, n % 4, :].bitcast(F32), ALU.subtract), [f"act.g{n}"])

        def outputs(n, lag):
            s, g = jobs[n]
            for half in range(2):
                bank = 4 + 2 * (n % 2) + half

                def product(e, i, half=half, bank=bank):
                    for t in range(2):
                        at = (2 * half + t) * P
                        done = product3(e, K.ps[:, bank, t * D:(t + 1) * D], [x[:, n % 4, at:at + P] for x in h],
                                        [w[:, s, D:2 * D] for w in w1], True, True)
                    return done
                S.step("pe", f"y{n}_{half}", product, [f"dve.l{n}", earlier("dve.y{}_%d" % half, n, 2)], lag=lag)

                def add(e, i, half=half, bank=bank):
                    for t in range(2):
                        row = 4 * g + 2 * half + t
                        done = e.scalar_tensor_tensor(K.x[:, row, :], K.ps[:, bank, t * D:(t + 1) * D],
                                                      gate[:, row, bass.ds(2 * i + s, 1)], K.x[:, row, :], ALU.mult, ALU.add)
                    return done
                S.step("dve", f"y{n}_{half}", add, [f"pe.y{n}_{half}"], lag=lag)
        for n in range(len(jobs)):
            hidden(n)
            outputs((n - 2) % len(jobs), lag=int(n < 2))
        S.run()


LAYERS = [cross_attention_0, delta_attention, experts_0, cross_attention_1, self_attention, experts_1]


def program(nc, ins, out):
    with ExitStack() as ctx:
        K = Kern(nc, ctx, ins, out)
        K.pending = []
        K.count = {e: K.sem("count_" + e) for e in ENGINES}
        K.gate = {e: K.sem("gate_" + e) for e in ENGINES}
        K.base = {e: 0 for e in ENGINES}
        K.x = K.sb("x", [P, NT, D])
        K.xnb = K.sb("xnb", [P, 2, D])
        K.xs = K.sb("xs", [P, 2, DC, P])
        K.bn = K.sb("bn", [P, NT, 6])
        K.mv = K.sb("mv", [P, NT, 2])
        K.std = K.sb("std", [P, NT])
        K.rstd = K.sb("rstd", [P, NT])
        K.ident = K.sb("ident", [P, P])
        K.masks = K.sb("masks", [P, MASK_COLS])
        K.before = K.sb("before", [P, 16, 16])
        at = MASK_AT
        K.low, K.eye, K.half, K.blocks, K.upto, K.headsel = (
            K.masks[:, at[n][0]:at[n][1]] for n in ("low", "eye", "half", "blocks", "upto", "headsel"))
        K.head16, K.diag16 = (K.masks[:, at[n][0]:at[n][1]] for n in ("head16", "diag16"))
        K.between = [K.masks[:, at[n][0]:at[n][1]] for n in ("between2", "between4", "between8", "between16")]
        K.ps = ctx.enter_context(nc.psum_tensor("ps", [P, 8, 512], F32))
        constants(K)
        for layer in LAYERS:
            layer(K)
        store(K)


def shape_masks():
    r, c = np.arange(P) % L, np.arange(L)
    b, bb, cc = np.arange(P)[:, None] // L, np.arange(P)[None, :] // L, np.arange(P)[None, :] % L
    i = r[:, None]
    parts = {
        "low": c[None, :] < i,
        "eye": c[None, :] == i,
        "half": (i % 2 == 1) & (c[None, :] == i - 1),
        "blocks": b == bb,
        "upto": (b == bb) & (i <= cc),
        "headsel": np.arange(P)[:, None] // 64 == np.arange(2)[None, :],
    }
    parts["head16"] = np.arange(P)[:, None] // 16 == np.arange(8)[None, :]
    parts["diag16"] = b == np.arange(64)[None, :] // 16
    for m in (2, 4, 8, 16):
        parts[f"between{m}"] = (b == bb) & (i // (2 * m) == cc // (2 * m)) & (i % (2 * m) < m) & (cc % (2 * m) >= m)
    at, n = {}, 0
    for k, v in parts.items():
        at[k] = (n, n + v.shape[1])
        n += v.shape[1]
    return np.concatenate([v.astype(np.float32) for v in parts.values()], axis=1), at, n


MASKS, MASK_AT, MASK_COLS = shape_masks()


def rope_rows():
    inv = np.float32(1.0) / np.float32(10000.0) ** (np.arange(0, 64, 2, dtype=np.float32) / np.float32(64))
    angle = (np.arange(L - 1, dtype=np.float32)[:, None] * inv[None, :].astype(np.float32)).astype(np.float32)
    table = np.zeros((L, 2, 64), np.float32)
    table[0, 0] = 1.0
    table[1:, 0] = np.cos(np.concatenate([angle, angle], axis=1))
    table[1:, 1] = np.concatenate([-np.sin(angle), np.sin(angle)], axis=1)
    return np.tile(table, (BT, 1, 1))


def columns(v):
    return v.reshape(-1, P).T


def kernel(**inputs):
    import concourse.bacc as bacc
    from concourse.bass_utils import run_bass_kernel_spmd

    a = {k: np.asarray(v) for k, v in inputs.items()}
    laid = {
        "x": a["x"].reshape(ROWS, D),
        "ctx": a["ctx_1024"],
        "ctxT": a["ctx_1024"].transpose(0, 2, 1),
        "mask": a["mask_Bx1xS2_ik1"],
        "L0_xattn_WkT": a["L0_xattn_Wk"].T,
    }
    for n in ("Wq", "Wv", "Wo", "bo", "g0", "beta0"):
        laid["L0_xattn_" + n] = a["L0_xattn_" + n]
    laid["masks"] = MASKS
    laid["before"] = (np.arange(16)[None, :] < np.arange(16)[:, None]).astype(np.float32)
    for n in ("W_q", "W_k", "W_v", "W_b", "W_fuse1", "W_fuse2", "b_fuse2", "others_log_tau", "W_o"):
        laid["L0_attn_" + n] = a["L0_attn_" + n]
    laid["L0_attn_b_fuse1"] = columns(a["L0_attn_b_fuse1"])
    laid["L0_attn_conv"] = np.stack([a["L0_attn_conv_w_" + n].reshape(DC, P, TAPS).transpose(1, 0, 2) for n in "qkv"], axis=1)
    laid["L0_attn_fir"] = np.concatenate([a["L0_attn_fir_short_w"].reshape(DC, P, SHORT),
                                          a["L0_attn_fir_long_w"].reshape(DC, P, LONG)], axis=2).transpose(1, 0, 2)
    laid["L0_attn_norm_w"] = np.tile(a["L0_attn_norm_w"], 2).reshape(P, 1)
    for n in ("Wq", "Wk", "Wv", "Wo"):
        laid[f"L1_xattn_{n}T"] = a["L1_xattn_" + n].T
    for n in ("bq", "bk", "bv"):
        laid["L1_xattn_" + n] = columns(a["L1_xattn_" + n])
    laid["L1_xattn_bo"] = a["L1_xattn_bo"]
    order = [4 * (2 * g + r) + h for g in range(2) for h in range(4) for r in range(2)]
    wq = a["L1_attn_Wq"].reshape(16, 64, D)[order].reshape(1024, D)
    laid["L1_attn_WqkvT"] = np.concatenate([wq, a["L1_attn_Wk"], a["L1_attn_Wv"]], axis=0).T
    laid["L1_attn_WoT"] = a["L1_attn_Wo"].reshape(D, 16, 64)[:, order].reshape(D, 1024).T
    laid["rope"] = rope_rows()
    for n in ("q_norm_w", "k_norm_w"):
        laid["L1_attn_" + n] = a["L1_attn_" + n]
    laid["L1_ffn_gate_wT"] = a["L1_ffn_gate_w"].T
    laid["L1_ffn_bias_e"] = a["L1_ffn_bias_e"]
    up = np.concatenate([a["L1_ffn_up_w"], a["L1_ffn_shared_up"].reshape(4, P, D)], axis=0)
    down = np.concatenate([a["L1_ffn_down_w"], a["L1_ffn_shared_down"].reshape(D, 4, P).transpose(1, 0, 2)], axis=0)
    laid["L1_ffn_upT"], laid["L1_ffn_downT"] = up.transpose(0, 2, 1), down.transpose(0, 2, 1)
    laid["L0_ffn_WrT"] = a["L0_ffn_Wr"].T
    laid["L0_ffn_W1T"] = a["L0_ffn_W1"].transpose(0, 2, 1)
    laid["L0_ffn_W2T"] = a["L0_ffn_W2"].transpose(0, 2, 1)
    for n in ("bq", "bk", "bv"):
        laid["L0_xattn_" + n] = columns(a["L0_xattn_" + n])
    nc = bacc.Bacc("TRN2", target_bir_lowering=False, num_devices=1)
    arrays, ins = {}, {}
    for name, v in laid.items():
        v = np.ascontiguousarray(v)
        arrays["in_" + name] = v
        ins[name] = nc.dram_tensor("in_" + name, v.shape, mybir.dt.from_np(v.dtype), kind="ExternalInput").ap()
    out = nc.dram_tensor("out_0", (ROWS, D), F32, kind="ExternalOutput").ap()
    program(nc, ins, out)
    r = run_bass_kernel_spmd(nc, [arrays], core_ids=[0])
    return r.results[0]["out_0"].reshape(B, L, D)
```
